# Optimizing a Trainium2 kernel written in Bass

```python
import numpy as np
import jax
import jax.numpy as jnp

def _softmax(x, axis=-1):
    return jax.nn.softmax(x, axis=axis)

def _gelu(x):
    return jax.nn.gelu(x, approximate=True)

def _silu(x):
    return jax.nn.silu(x)

def _sigmoid(x):
    return jax.nn.sigmoid(x)

def _layernorm(x, axis=-1, eps=1e-05):
    m = jnp.mean(x, axis=axis, keepdims=True)
    v = jnp.var(x, axis=axis, keepdims=True)
    return (x - m) / jnp.sqrt(v + eps)

def _scatter_add(tgt, idx, src, axis=0):
    return tgt.at[idx].add(src)

def _segment_sum(src, seg, n):
    return jax.ops.segment_sum(src, seg, n)
kernel_name = 'mk_audio_tower_d1_tok_audfeat1024_r4_100dc5'

def setup_inputs(seed: int=0):
    np.random.seed(seed)
    _w = jnp.asarray

    def _rec_inputs():
        import jax
        import jax.numpy as jnp
        _rk = jax.random.key(seed)
        x = 0.00021031 + 1.00007 * jax.random.normal(jax.random.fold_in(_rk, 1), (32, 750, 256), jnp.float32)
        return x
    x = _rec_inputs()

    def _L0_tok_setup():
        import jax, jax.numpy as jnp
        import numpy as np
        DIM = 256
        SEGMENT_SIZE = 256
        DILATION_RATE = 2
        key = jax.random.key(seed)
        x = jax.random.normal(key, (4, 2048, DIM), dtype=jnp.float32)
        return {'x': x}
    _L0_tok_all = _L0_tok_setup()
    _L0_tok_in = {k: v for k, v in _L0_tok_all.items() if k in ()}
    del _L0_tok_all

    def _L0_attn_setup():
        import jax, jax.numpy as jnp
        import numpy as np
        from jax import lax
        D_MODEL = 256
        D_STATE = 16
        D_CONV = 4
        D_INNER = 2 * D_MODEL

        def _selective_scan(u, dt, A, Bm, Cm):
            dA = jnp.exp(jnp.einsum('bld,dn->bldn', dt, A))
            dB = jnp.einsum('bld,bln->bldn', dt, Bm)
            batch, L, D = u.shape
            N = A.shape[1]
            h0 = jnp.zeros((batch, D, N), dtype=u.dtype)

            def step(h, inp):
                dA_i, dB_i, u_i, C_i = inp
                h = dA_i * h + dB_i * u_i[:, :, None]
                y = jnp.einsum('bdn,bn->bd', h, C_i)
                return (h, y)
            xs = (jnp.moveaxis(dA, 1, 0), jnp.moveaxis(dB, 1, 0), jnp.moveaxis(u, 1, 0), jnp.moveaxis(Cm, 1, 0))
            _, ys = lax.scan(step, h0, xs)
            return jnp.moveaxis(ys, 0, 1)
        key = jax.random.key(seed)
        ks = jax.random.split(key, 8)
        s = 0.02
        x = jax.random.normal(ks[0], (2, 256, D_MODEL), dtype=jnp.float32)
        W_in = jax.random.normal(ks[1], (2 * D_INNER, D_MODEL), dtype=jnp.float32) * s
        W_conv = jax.random.normal(ks[2], (D_INNER, 1, D_CONV), dtype=jnp.float32) * s
        b_conv = jnp.zeros((D_INNER,), dtype=jnp.float32)
        W_dt = jax.random.normal(ks[3], (D_INNER, D_INNER), dtype=jnp.float32) * s
        b_dt = jnp.zeros((D_INNER,), dtype=jnp.float32)
        W_B = jax.random.normal(ks[4], (D_STATE, D_INNER), dtype=jnp.float32) * s
        W_C = jax.random.normal(ks[5], (D_STATE, D_INNER), dtype=jnp.float32) * s
        A_log = jnp.log(jnp.tile(jnp.arange(1, D_STATE + 1, dtype=jnp.float32), (D_INNER, 1)))
        W_out = jax.random.normal(ks[6], (D_MODEL, D_INNER), dtype=jnp.float32) * s
        return {'x': x, 'W_in': W_in, 'W_conv': W_conv, 'b_conv': b_conv, 'W_dt': W_dt, 'b_dt': b_dt, 'W_B': W_B, 'W_C': W_C, 'A_log': A_log, 'W_out': W_out}
    _L0_attn_all = _L0_attn_setup()
    _L0_attn_in = {k: v for k, v in _L0_attn_all.items() if k in ('W_in', 'W_conv', 'b_conv', 'W_dt', 'b_dt', 'W_B', 'W_C', 'A_log', 'W_out')}
    del _L0_attn_all

    def _L0_ffn_setup():
        import jax, jax.numpy as jnp
        import numpy as np
        B, S, H, I = (2, 512, 256, 128)
        E, K, G, TG = (64, 8, 8, 4)
        SCALE = 2.5
        CAP = 256
        key = jax.random.key(seed)
        ks = jax.random.split(key, 6)
        hidden_states = jax.random.normal(ks[0], (B, S, H), jnp.float32)
        gate_w = jax.random.normal(ks[1], (E, H), jnp.float32) * 0.02
        gate_bias = jax.random.normal(ks[2], (E,), jnp.float32) * 0.02
        w_gate = jax.random.normal(ks[3], (E, H, I), jnp.float32) * (1.0 / np.sqrt(H))
        w_up = jax.random.normal(ks[4], (E, H, I), jnp.float32) * (1.0 / np.sqrt(H))
        w_down = jax.random.normal(ks[5], (E, I, H), jnp.float32) * (1.0 / np.sqrt(I))
        return {'hidden_states': hidden_states, 'gate_w': gate_w, 'gate_bias': gate_bias, 'w_gate': w_gate, 'w_up': w_up, 'w_down': w_down}
    _L0_ffn_all = _L0_ffn_setup()
    _L0_ffn_in = {k: v for k, v in _L0_ffn_all.items() if k in ('gate_w', 'gate_bias', 'w_gate', 'w_up', 'w_down')}
    del _L0_ffn_all
    return {'x': x, 'L0_attn_W_in': _L0_attn_in['W_in'], 'L0_attn_W_conv': _L0_attn_in['W_conv'], 'L0_attn_b_conv': _L0_attn_in['b_conv'], 'L0_attn_W_dt': _L0_attn_in['W_dt'], 'L0_attn_b_dt': _L0_attn_in['b_dt'], 'L0_attn_W_B': _L0_attn_in['W_B'], 'L0_attn_W_C': _L0_attn_in['W_C'], 'L0_attn_A_log': _L0_attn_in['A_log'], 'L0_attn_W_out': _L0_attn_in['W_out'], 'L0_ffn_gate_w': _L0_ffn_in['gate_w'], 'L0_ffn_gate_bias': _L0_ffn_in['gate_bias'], 'L0_ffn_w_gate': _L0_ffn_in['w_gate'], 'L0_ffn_w_up': _L0_ffn_in['w_up'], 'L0_ffn_w_down': _L0_ffn_in['w_down']}

def reference(x, L0_attn_W_in, L0_attn_W_conv, L0_attn_b_conv, L0_attn_W_dt, L0_attn_b_dt, L0_attn_W_B, L0_attn_W_C, L0_attn_A_log, L0_attn_W_out, L0_ffn_gate_w, L0_ffn_gate_bias, L0_ffn_w_gate, L0_ffn_w_up, L0_ffn_w_down):
    import jax
    import jax.numpy as jnp

    def _L0_tok_ref(x):
        import jax, jax.numpy as jnp
        import numpy as np
        DIM = 256
        SEGMENT_SIZE = 256
        DILATION_RATE = 2
        B, S, D = x.shape
        pad = -S % SEGMENT_SIZE
        x = jnp.pad(x, ((0, 0), (0, pad), (0, 0)))
        x = x.reshape(B, -1, SEGMENT_SIZE, D)
        x = x[:, :, ::DILATION_RATE, :]
        q = k = v = x
        scale = 1.0 / jnp.sqrt(jnp.asarray(D, dtype=x.dtype))
        scores = jnp.einsum('bsqd,bskd->bsqk', q, k) * scale
        probs = jax.nn.softmax(scores, axis=-1)
        attn = jnp.einsum('bsqk,bskd->bsqd', probs, v)
        return attn.reshape(B, -1, D)

    def _L0_attn_ref(x, W_in, W_conv, b_conv, W_dt, b_dt, W_B, W_C, A_log, W_out):
        import jax, jax.numpy as jnp
        import numpy as np
        from jax import lax
        D_MODEL = 256
        D_STATE = 16
        D_CONV = 4
        D_INNER = 2 * D_MODEL

        def _selective_scan(u, dt, A, Bm, Cm):
            dA = jnp.exp(jnp.einsum('bld,dn->bldn', dt, A))
            dB = jnp.einsum('bld,bln->bldn', dt, Bm)
            batch, L, D = u.shape
            N = A.shape[1]
            h0 = jnp.zeros((batch, D, N), dtype=u.dtype)

            def step(h, inp):
                dA_i, dB_i, u_i, C_i = inp
                h = dA_i * h + dB_i * u_i[:, :, None]
                y = jnp.einsum('bdn,bn->bd', h, C_i)
                return (h, y)
            xs = (jnp.moveaxis(dA, 1, 0), jnp.moveaxis(dB, 1, 0), jnp.moveaxis(u, 1, 0), jnp.moveaxis(Cm, 1, 0))
            _, ys = lax.scan(step, h0, xs)
            return jnp.moveaxis(ys, 0, 1)
        batch, L, _ = x.shape
        xz = x @ W_in.T
        x_in, z = jnp.split(xz, 2, axis=-1)
        xc = jnp.moveaxis(x_in, 1, 2)
        xc = lax.conv_general_dilated(xc, W_conv, (1,), [(D_CONV - 1, 0)], dimension_numbers=('NCH', 'OIH', 'NCH'), feature_group_count=D_INNER)
        xc = xc + b_conv[None, :, None]
        xc = jax.nn.silu(xc)
        x_conv = jnp.moveaxis(xc, 1, 2)
        dt = jax.nn.softplus(x_conv @ W_dt.T + b_dt)
        Bm = x_conv @ W_B.T
        Cm = x_conv @ W_C.T
        A = -jnp.exp(A_log)
        y = _selective_scan(x_conv, dt, A, Bm, Cm)
        out = y * jax.nn.silu(z)
        return out @ W_out.T

    def _L0_ffn_ref(hidden_states, gate_w, gate_bias, w_gate, w_up, w_down):
        import jax, jax.numpy as jnp
        import numpy as np
        B, S, H, I = (2, 512, 256, 128)
        E, K, G, TG = (64, 8, 8, 4)
        SCALE = 2.5
        CAP = 256
        b, s, h = hidden_states.shape
        x = hidden_states.reshape(-1, h)
        n = x.shape[0]
        logits = x.astype(jnp.float32) @ gate_w.astype(jnp.float32).T
        scores = jax.nn.sigmoid(logits)
        sfc = scores + gate_bias[None, :]
        group_scores = jax.lax.top_k(sfc.reshape(n, G, E // G), 2)[0].sum(-1)
        gidx = jax.lax.top_k(group_scores, TG)[1]
        gmask = jnp.zeros((n, G), bool).at[jnp.arange(n)[:, None], gidx].set(True)
        smask = jnp.repeat(gmask, E // G, axis=1)
        tmp = jnp.where(smask, sfc, -jnp.inf)
        topk_idx = jax.lax.top_k(tmp, K)[1]
        topk_w = jnp.take_along_axis(scores, topk_idx, axis=1)
        topk_w = topk_w / (topk_w.sum(-1, keepdims=True) + 1e-20)
        topk_w = topk_w * SCALE
        e = topk_idx.reshape(-1)
        token = jnp.repeat(jnp.arange(n), K)
        oh = jax.nn.one_hot(e, E, dtype=jnp.int32)
        pos = jnp.take_along_axis(jnp.cumsum(oh, 0) - 1, e[:, None], 1)[:, 0]
        valid = pos < CAP
        pos_c = jnp.where(valid, pos, CAP)
        buf = jnp.zeros((E, CAP + 1, h), x.dtype).at[e, pos_c].set(x[token])[:, :CAP]
        g = jnp.einsum('ech,ehi->eci', buf, w_gate)
        u = jnp.einsum('ech,ehi->eci', buf, w_up)
        y = jnp.einsum('eci,eih->ech', jax.nn.silu(g) * u, w_down)
        y_slots = y[e, jnp.minimum(pos, CAP - 1)]
        w_slot = topk_w.reshape(-1) * valid.astype(topk_w.dtype)
        out = jnp.zeros((n, h), jnp.float32).at[token].add(y_slots * w_slot[:, None])
        return out.reshape(b, s, h)
    h = _L0_tok_ref(x)
    h = h + _L0_attn_ref(_layernorm(h, axis=-1), L0_attn_W_in, L0_attn_W_conv, L0_attn_b_conv, L0_attn_W_dt, L0_attn_b_dt, L0_attn_W_B, L0_attn_W_C, L0_attn_A_log, L0_attn_W_out)
    h = h + _L0_ffn_ref(_layernorm(h, axis=-1), L0_ffn_gate_w, L0_ffn_gate_bias, L0_ffn_w_gate, L0_ffn_w_up, L0_ffn_w_down)
    return h

_drawn_inputs = setup_inputs


def setup_inputs(seed=0):
    import zlib

    import numpy as np

    out = dict(_drawn_inputs(seed))
    spreads = {'L0_attn_b_conv': (0.0, 0.8), 'L0_attn_b_dt': (0.0, 0.8)}
    factors = {'L0_attn_W_in': 8.0,
     'L0_attn_W_conv': 8.0,
     'L0_attn_W_dt': 8.0,
     'L0_attn_W_B': 8.0,
     'L0_attn_W_C': 8.0,
     'L0_attn_A_log': 8.0,
     'L0_attn_W_out': 8.0,
     'L0_ffn_gate_w': 8.0,
     'L0_ffn_gate_bias': 8.0,
     'L0_ffn_w_gate': 8.0,
     'L0_ffn_w_up': 8.0,
     'L0_ffn_w_down': 8.0}
    for name, (base, spread) in spreads.items():
        noise = np.random.default_rng([zlib.crc32(name.encode()), seed]).standard_normal(out[name].shape)
        drawn = base * np.exp(spread * noise) if base else spread * noise
        out[name] = jnp.asarray(drawn.astype(out[name].dtype))
    for name, factor in factors.items():
        out[name] = (out[name] * factor).astype(out[name].dtype)
    return out
```

```python
from contextlib import ExitStack

import concourse.bass as bass
from concourse import mybir

F32 = mybir.dt.float32
BF16 = mybir.dt.bfloat16
U32 = mybir.dt.uint32
I32 = mybir.dt.int32
ALU = mybir.AluOpType
ACT = mybir.ActivationFunctionType
AX = mybir.AxisListType

P = 128
D = 256
SEG = 256
DIL = 2
NSEG = 3
L = NSEG * P
DI = 512
CH = DI // P
KD = D // P
NS = 16
GN = 4
NG = NS // GN
TAPS = 4
NE = 64
EPS = 1e-5
POOL_C = (3,)


def after(eng, sem, count):
    if isinstance(count, int) and count <= 0:
        return
    eng.wait_ge(sem, count)


def sequence_phase(nc, x, w, bc_dram, h_out, x_tab, lg_tab):
    NB, S, _ = x.shape
    TAIL = (S - (NSEG - 1) * SEG + DIL - 1) // DIL

    with ExitStack() as ctx:
        def sb(name, shape, dt=F32):
            return ctx.enter_context(nc.sbuf_tensor(name, shape, dt))

        def ps(name, shape):
            return ctx.enter_context(nc.psum_tensor(name, shape, F32))

        def sem(name):
            return ctx.enter_context(nc.semaphore(name))

        w_in = sb("w_in", [P, KD, 2 * DI])
        w_dt = sb("w_dt", [P, CH, DI])
        w_bc = sb("w_bc", [P, CH, 2 * NS])
        w_out = sb("w_out", [P, CH, D])
        w_gt = sb("w_gt", [P, KD, NE])
        w_cv = sb("w_cv", [P, CH, TAPS])
        b_cv = sb("b_cv", [P, CH])
        b_dt = sb("b_dt", [P, CH])
        a_neg = sb("a_neg", [P, CH, NS])
        ident = sb("ident", [P, P])
        xs = [sb(f"xs{q}", [P, NSEG, D]) for q in range(2)]
        hres = [sb(f"hres{q}", [P, NSEG, D]) for q in range(2)]
        dt = [sb(f"dt{q}", [P, CH, L]) for q in range(2)]
        zs = [sb(f"zs{q}", [P, CH, L]) for q in range(2)]
        turned = sb("turned", [P, KD, L])
        prob = sb("prob", [P, NSEG, P])
        prob_t = sb("prob_t", [P, NSEG, P])
        normed = sb("normed", [P, NSEG, D])
        xin = sb("xin", [P, CH, TAPS - 1 + L])
        u = sb("u", [P, CH, L])
        soft = sb("soft", [P, CH, L])
        dtu = sb("dtu", [P, CH, L])
        bc_rows = sb("bc_rows", [2 * NS, L])
        b_all = sb("b_all", [P, NS, L])
        c_all = sb("c_all", [P, NS, L])
        yz = sb("yz", [P, CH, L])
        logit = sb("logit", [P, NSEG, NE])
        decay = [sb(f"decay{g}", [P, GN, L]) for g in range(NG)]
        hid = [sb(f"hid{g}", [P, GN, L]) for g in range(NG)]
        rmax = sb("rmax", [P, NSEG])
        nmax = sb("nmax", [P, NSEG])
        rsum = sb("rsum", [P, NSEG])
        rinv = sb("rinv", [P, NSEG])
        stat = [sb(f"stat{j}", [P, NSEG, 6]) for j in range(2)]
        mv = [sb(f"mv{j}", [P, NSEG, 2]) for j in range(2)]
        lnv = [sb(f"lnv{j}", [P, NSEG]) for j in range(2)]
        rs0 = [sb(f"rs0{j}", [P, NSEG]) for j in range(2)]
        nw = [sb(f"nw{j}", [P, 3, NSEG]) for j in range(2)]
        rstd = [sb(f"rstd{j}", [P, NSEG]) for j in range(2)]
        epsc = sb("epsc", [P, 1])

        psY = [ps(f"psY{j}", [P, 512]) for j in range(2)]
        psT = ps("psT", [P, 2, 512])
        psW = ps("psW", [P, 2, 512])
        psX = ps("psX", [P, 2, 512])
        psXf = psX[:, :, :].rearrange("p a b -> p (a b)")

        s_turn = sem("wait_carrier")
        s_w = sem("weights_loaded")
        s_a0 = sem("a_log_exped")
        s_const = sem("constants_set")
        s_id0 = sem("ident_cleared")
        s_idn = sem("ident_set")
        s_x = sem("x_loaded")
        s_bcw = sem("bc_rows_stored")
        s_B = [sem(f"b_loaded{g}") for g in range(NG)]
        s_C = [sem(f"c_loaded{g}") for g in range(NG)]
        s_hst = sem("h_stored")
        s_xst = sem("x2_stored")
        s_lst = sem("logits_stored")
        s_dec = [sem(f"decay_ready{g}") for g in range(NG)]
        s_dbu = [sem(f"dbu_ready{g}") for g in range(NG)]
        s_h = [sem(f"scan_done{g}") for g in range(NG)]
        s_hc = [sem(f"hc_ready{g}") for g in range(NG)]
        s_ys = [sem(f"y_summed{g}") for g in range(NG)]
        s_yz = sem("y_gated")
        s_qT, s_qTc = sem("q_turned"), sem("q_turned_copied")
        s_S, s_rm, s_nm, s_E = sem("scores_ready"), sem("row_max"), sem("neg_max"), sem("prob_ready")
        s_ET, s_ETc = sem("prob_turned"), sem("prob_turned_copied")
        s_at, s_ri, s_h1 = sem("attended"), sem("sums_inverted"), sem("h1_ready")
        s_st = [sem(f"stats{j}") for j in range(2)]
        s_mv = [sem(f"mean_var{j}") for j in range(2)]
        s_lv = [sem(f"log_var{j}") for j in range(2)]
        s_r0 = [sem(f"rstd_first{j}") for j in range(2)]
        s_nw = [sem(f"newton{j}") for j in range(2)]
        s_rs = [sem(f"rstd_ready{j}") for j in range(2)]
        s_xn = [sem(f"normed{j}") for j in range(2)]
        s_xT, s_xTc = sem("xn_turned"), sem("xn_turned_copied")
        s_x2T, s_x2Tc = sem("x2_turned"), sem("x2_turned_copied")
        s_xp = [sem(f"xin_product{j}") for j in range(2)]
        s_xc = [sem(f"xin_copied{j}") for j in range(2)]
        s_cv = sem("conv_tap")
        s_zp = [sem(f"z_product{j}") for j in range(2)]
        s_zs = [sem(f"z_silu{j}") for j in range(2)]
        s_u = sem("u_ready")
        s_dp = [sem(f"dt_product{j}") for j in range(2)]
        s_dx = [sem(f"dt_biased{j}") for j in range(2)]
        s_da = [sem(f"dt_abs{j}") for j in range(2)]
        s_de = [sem(f"dt_exp{j}") for j in range(2)]
        s_dl = [sem(f"dt_log{j}") for j in range(2)]
        s_dt = [sem(f"dt_ready{j}") for j in range(2)]
        s_dtu = [sem(f"dtu_ready{j}") for j in range(2)]
        s_bcp, s_bcc = sem("bc_product"), sem("bc_rows_ready")
        s_op, s_h2 = sem("out_product"), sem("h2_ready")
        s_lg, s_lgc = sem("logit_product"), sem("logit_copied")

        def min_seq(count):
            return min(count, NB) if isinstance(count, int) else count

        def bodies(seq):
            def run(eng, body):
                body(0, 0, True, False)
                if NB > 2:
                    with eng.Fori(0, (NB - 2) // 2) as i:
                        body(2 * i + 1, 1, False, False)
                        body(2 * i + 2, 0, False, False)
                body(NB - 1, (NB - 1) % 2, False, True)
            return run

        each = bodies(NB)
        block = ctx.enter_context(nc.Block())

        @block.sync
        def _(sp):
            def wait(sem, count):
                after(sp, sem, count)
                if not isinstance(count, int):
                    sp.sem_inc(s_turn, 1)

            sp.dma_start(w_in[:, :, :], w["in_t"].rearrange("(k p) n -> p k n", p=P)).then_inc(s_w, 16)
            sp.dma_start(w_dt[:, :, :], w["dt_t"].rearrange("(c p) n -> p c n", p=P)).then_inc(s_w, 16)
            sp.dma_start(w_bc[:, :, 0:NS], w["b_t"].rearrange("(c p) n -> p c n", p=P)).then_inc(s_w, 16)
            sp.dma_start(w_bc[:, :, NS:2 * NS], w["c_t"].rearrange("(c p) n -> p c n", p=P)).then_inc(s_w, 16)
            sp.dma_start(w_out[:, :, :], w["out_t"].rearrange("(c p) n -> p c n", p=P)).then_inc(s_w, 16)
            sp.dma_start(w_gt[:, :, :], w["gate_t"].rearrange("(k p) n -> p k n", p=P)).then_inc(s_w, 16)
            sp.dma_start(w_cv[:, :, :], w["conv"].rearrange("(c p) n -> p c n", p=P)).then_inc(s_w, 16)
            sp.dma_start(b_cv[:, :], w["b_conv"]).then_inc(s_w, 16)
            sp.dma_start(b_dt[:, :], w["b_dt"]).then_inc(s_w, 16)
            sp.dma_start(a_neg[:, :, :], w["a_log"].rearrange("(c p) n -> p c n", p=P)).then_inc(s_w, 16)

            def load_x(n, q):
                sp.dma_start(xs[q][:, 0:NSEG - 1, :],
                             x[n, 0:(NSEG - 1) * SEG, :].rearrange("(s p j) d -> j p s d", s=NSEG - 1, j=DIL)[0]
                             ).then_inc(s_x, 16)
                sp.dma_start(xs[q][0:TAIL, NSEG - 1, :],
                             x[n, (NSEG - 1) * SEG:S, :].rearrange("(p j) d -> j p d", j=DIL)[0]
                             ).then_inc(s_x, 16)

            def share_bc(n, q, own):
                wait(s_bcc, n + 1)
                sp.dma_start(bc_dram[q], bc_rows[:, :]).then_inc(s_bcw, 16)
                wait(s_bcw, 16 * (n + 1))
                for kind, g in (("b", 0), ("b", 1), ("c", 0), ("b", 2), ("c", 1), ("b", 3), ("c", 2), ("c", 3)):
                    to, done, used, at = ((b_all, s_B, s_dbu, 0) if kind == "b" else (c_all, s_C, s_hc, NS))
                    wait(used[g], own)
                    src = bc_dram[q, at + g * GN:at + (g + 1) * GN, :].rearrange("n l -> (n l)")
                    sp.dma_start(to[:, g * GN:(g + 1) * GN, :].rearrange("p n l -> p (n l)"),
                                 src.partition_broadcast(P)).then_inc(done[g], 16)

            def store_out(m, q):
                wait(s_h2, m + 1)
                sp.dma_start(h_out[bass.ds(m * L, L), :].rearrange("(s p) d -> p s d", p=P),
                             hres[q][:, :, :]).then_inc(s_hst, 16)
                wait(s_xn[1], m + 1)
                sp.dma_start(x_tab[bass.ds(m * L, L), 0:D].rearrange("(s p) d -> p s d", p=P),
                             normed[:, :, :]).then_inc(s_xst, 16)
                wait(s_lgc, m + 1)
                sp.dma_start(lg_tab[m], logit[:, :, :]).then_inc(s_lst, 16)

            sp.sem_inc(s_lst, 16)
            wait(s_const, 1)
            load_x(0, 0)
            wait(s_x, 32)
            load_x(1, 1)
            share_bc(0, 0, 0)

            def body(b, q, first, last):
                if not last:
                    wait(s_x, 32 * (b + 2))
                    wait(s_at, b + 1)
                    if not (isinstance(b, int) and b + 2 >= NB):
                        load_x(b + 2, q)
                if not first:
                    store_out(b - 1, 1 - q)
                if not last:
                    share_bc(b + 1, 1 - q, 4 * b + 4)

            def run():
                body(0, 0, True, False)
                if NB > 4:
                    with sp.Fori(0, (NB - 4) // 2) as i:
                        body(2 * i + 1, 1, False, False)
                        body(2 * i + 2, 0, False, False)
                for b in range(max(1, NB - 3), NB):
                    body(b, b % 2, False, b == NB - 1)

            run()
            store_out(NB - 1, (NB - 1) % 2)
            wait(s_hst, 16 * NB)
            wait(s_xst, 16 * NB)
            wait(s_lst, 16 * (NB + 1))

        @block.gpsimd
        def _(pool):
            nc.gpsimd.memset(ident[:, :], 0.0).then_inc(s_id0, 1)
            pool.wait_ge(s_id0, 1)
            nc.gpsimd.affine_select(out=ident[:, :], in_=ident[:, :], compare_op=ALU.not_equal, fill=1.0,
                                    base=0, pattern=[[-1, P]], channel_multiplier=1).then_inc(s_idn, 1)

            def times_b(b, c, g):
                cc = 4 * b + c
                if g == 0 and c == 0:
                    pool.wait_ge(s_dtu[0], b + 1)
                if g == 0 and c == 2:
                    pool.wait_ge(s_dtu[1], b + 1)
                if c == 0:
                    pool.wait_ge(s_B[g], 16 * (b + 1))
                after(pool, s_ys[g], cc)
                nc.gpsimd.tensor_tensor(hid[g][:, :, :], dtu[:, c, :].unsqueeze(1).to_broadcast([P, GN, L]),
                                        b_all[:, g * GN:(g + 1) * GN, :], ALU.mult).then_inc(s_dbu[g], 1)

            def times_c(b, c, g):
                if g not in POOL_C:
                    return
                if c == 0:
                    pool.wait_ge(s_C[g], 16 * (b + 1))
                pool.wait_ge(s_h[g], 4 * b + c + 1)
                nc.gpsimd.tensor_tensor(hid[g][:, :, :], hid[g][:, :, :],
                                        c_all[:, g * GN:(g + 1) * GN, :], ALU.mult).then_inc(s_hc[g], 1)

            def drive(n, q, half):
                pool.wait_ge(s_dt[half], n + 1)
                a, z = 2 * half, 2 * half + 2
                if half == 0:
                    pool.wait_ge(s_u, n + 1)
                nc.gpsimd.tensor_tensor(dtu[:, a:z, :], dt[q][:, a:z, :], u[:, a:z, :],
                                        ALU.mult).then_inc(s_dtu[half], 1)

            def body(b, q, first, last):
                for k in range(16):
                    times_b(b, k // 4, k % 4)
                    if k >= 2:
                        times_c(b, (k - 2) // 4, (k - 2) % 4)
                    elif not first:
                        times_c(b - 1, 3, k + 2)
                if last:
                    times_c(b, 3, 2)
                    times_c(b, 3, 3)
                else:
                    if not first:
                        pass
                    pool.wait_ge(s_dbu[3], 4 * b + 4)
                    drive(b + 1, 1 - q, 0)
                    drive(b + 1, 1 - q, 1)

            drive(0, 0, 0)
            drive(0, 0, 1)
            each(pool, body)

        @block.scalar
        def _(act):
            def decays(b, q, c, g):
                if g == 0 and c % 2 == 0:
                    act.wait_ge(s_dt[c // 2], b + 1)
                after(act, s_h[g], 4 * b + c)
                for j in range(GN):
                    last = nc.scalar.activation(decay[g][:, j, 1:L], dt[q][:, c, 1:L], ACT.Exp,
                                                scale=a_neg[:, c, g * GN + j:g * GN + j + 1])
                last.then_inc(s_dec[g], 1)

            def copy_turned(n, ready, done):
                act.wait_ge(ready, n + 1)
                nc.scalar.activation(turned[:, :, :], psT[:, :, 0:L], ACT.Copy).then_inc(done, 1)

            def probs(n):
                act.wait_ge(s_nm, n + 1)
                for s in range(NSEG):
                    last = nc.scalar.activation(prob[:, s, :], psW[:, 0, s * P:(s + 1) * P], ACT.Exp,
                                                bias=nmax[:, s:s + 1], scale=D ** -0.5,
                                                accum_out=rsum[:, s:s + 1])
                last.then_inc(s_E, 1)

            def copy_prob_t(n):
                act.wait_ge(s_ET, n + 1)
                nc.scalar.activation(prob_t[:, :, :].rearrange("p s k -> p (s k)"), psT[:, 0, 0:L],
                                     ACT.Copy).then_inc(s_ETc, 1)

            def first_rstd(n, j):
                act.wait_ge(s_mv[j], n + 1)
                nc.scalar.activation(lnv[j][:, :], mv[j][:, :, 1], ACT.Ln, bias=epsc[:, 0:1]).then_inc(s_lv[j], 1)
                act.wait_ge(s_lv[j], n + 1)
                nc.scalar.activation(rs0[j][:, :], lnv[j][:, :], ACT.Exp, scale=-0.5).then_inc(s_r0[j], 1)

            def copy_xin(n, half):
                act.wait_ge(s_xp[half], n + 1)
                src = (psW, psX)[half]
                nc.scalar.activation(xin[:, 2 * half:2 * half + 2, TAPS - 1:], src[:, :, 0:L],
                                     ACT.Copy).then_inc(s_xc[half], 1)

            def silus(n, q):
                act.wait_ge(s_cv, TAPS * (n + 1))
                nc.scalar.activation(u[:, :, :], u[:, :, :], ACT.Silu).then_inc(s_u, 1)
                for half, src in ((0, psT), (1, psW)):
                    act.wait_ge(s_zp[half], n + 1)
                    nc.scalar.activation(zs[q][:, 2 * half:2 * half + 2, :], src[:, :, 0:L],
                                         ACT.Silu).then_inc(s_zs[half], 1)

            def softplus(n, half):
                act.wait_ge(s_dp[half], n + 1)
                src = (psT, psW)[half]
                a, z = 2 * half, 2 * half + 2
                for c in range(a, z):
                    last = nc.scalar.activation(xin[:, c, TAPS - 1:], src[:, c - a, 0:L], ACT.Identity,
                                                bias=b_dt[:, c:c + 1])
                last.then_inc(s_dx[half], 1)
                act.wait_ge(s_dx[half], n + 1)
                nc.scalar.activation(soft[:, a:z, :], xin[:, a:z, TAPS - 1:], ACT.Abs).then_inc(s_da[half], 1)
                act.wait_ge(s_da[half], n + 1)
                nc.scalar.activation(soft[:, a:z, :], soft[:, a:z, :], ACT.Exp, scale=-1.0).then_inc(s_de[half], 1)
                act.wait_ge(s_de[half], n + 1)
                nc.scalar.activation(soft[:, a:z, :], soft[:, a:z, :], ACT.Ln, bias=1.0).then_inc(s_dl[half], 1)

            def copy_logits(m):
                act.wait_ge(s_lg, m + 1)
                act.wait_ge(s_lst, 16 * (m + 1))
                nc.scalar.activation(logit[:, :, :], psW[:, 0, 0:NSEG * NE].rearrange("p (s e) -> p s e", s=NSEG),
                                     ACT.Copy).then_inc(s_lgc, 1)

            act.wait_ge(s_w, 160)
            act.wait_ge(s_const, 1)
            nc.scalar.activation(a_neg[:, :, :], a_neg[:, :, :], ACT.Exp).then_inc(s_a0, 1)
            act.wait_ge(s_a0, 1)
            nc.scalar.activation(a_neg[:, :, :], a_neg[:, :, :], ACT.Copy, scale=-1.0).then_inc(s_a0, 1)
            copy_turned(0, s_qT, s_qTc)
            probs(0)
            copy_prob_t(0)
            first_rstd(0, 0)
            copy_turned(0, s_xT, s_xTc)
            copy_xin(0, 0)
            copy_xin(0, 1)
            silus(0, 0)
            softplus(0, 0)
            softplus(0, 1)
            act.wait_ge(s_a0, 2)

            def body(b, q, first, last):
                n, m, r = b + 1, b - 1, 1 - q
                for k in range(16):
                    decays(b, q, k // 4, k % 4)
                    if not last:
                        if k == 0:
                            copy_turned(n, s_qT, s_qTc)
                        if k == 2:
                            probs(n)
                        if k == 4:
                            copy_prob_t(n)
                        if k == 6:
                            first_rstd(n, 0)
                        if k == 8:
                            copy_turned(n, s_xT, s_xTc)
                        if k == 9:
                            copy_xin(n, 0)
                            copy_xin(n, 1)
                        if k == 12:
                            silus(n, r)
                        if k == 14:
                            softplus(n, 0)
                        if k == 15:
                            softplus(n, 1)
                    if not first:
                        if k == 3:
                            first_rstd(m, 1)
                        if k == 5:
                            copy_turned(m, s_x2T, s_x2Tc)
                        if k == 6:
                            copy_logits(m)

            each(act, body)
            first_rstd(NB - 1, 1)
            copy_turned(NB - 1, s_x2T, s_x2Tc)
            copy_logits(NB - 1)

        @block.vector
        def _(dve):
            for g in range(NG):
                nc.vector.memset(decay[g][:, :, 0:1], 0.0)
            nc.vector.memset(xin[:, :, 0:TAPS - 1], 0.0)
            nc.vector.memset(epsc[:, :], EPS)
            nc.vector.memset(xs[0][:, NSEG - 1, :], 0.0)
            nc.vector.memset(xs[1][:, NSEG - 1, :], 0.0).then_inc(s_const, 1)

            def scan(b, c, g):
                dve.wait_ge(s_dec[g], 4 * b + c + 1)
                dve.wait_ge(s_dbu[g], 4 * b + c + 1)
                flat = hid[g][:, :, :].rearrange("p n l -> p (n l)")
                nc.vector.tensor_tensor_scan(flat, decay[g][:, :, :].rearrange("p n l -> p (n l)"), flat,
                                             0.0, ALU.mult, ALU.add).then_inc(s_h[g], 1)

            def times_c(b, c, g):
                if g in POOL_C:
                    return
                if c == 0:
                    dve.wait_ge(s_C[g], 16 * (b + 1))
                dve.wait_ge(s_h[g], 4 * b + c + 1)
                nc.vector.tensor_tensor(hid[g][:, :, :], hid[g][:, :, :],
                                        c_all[:, g * GN:(g + 1) * GN, :], ALU.mult).then_inc(s_hc[g], 1)

            def gate(b, q, c):
                dve.wait_ge(s_ys[3], 4 * b + c + 1)
                if c == 0:
                    dve.wait_ge(s_zs[1], b + 1)
                    after(dve, s_op, b)
                nc.vector.tensor_tensor(yz[:, c, :], psY[c % 2][:, 0:L], zs[q][:, c, :],
                                        ALU.mult).then_inc(s_yz, 1)

            def row_max(n):
                dve.wait_ge(s_S, n + 1)
                nc.vector.tensor_reduce(rmax[:, :], psW[:, 0, 0:L].rearrange("p (s k) -> p s k", s=NSEG),
                                        AX.X, ALU.max).then_inc(s_rm, 1)
                dve.wait_ge(s_rm, n + 1)
                nc.vector.tensor_scalar(nmax[:, :], rmax[:, :], -(D ** -0.5), None, ALU.mult).then_inc(s_nm, 1)

            def stats(n, j, src):
                for s in range(NSEG):
                    last = nc.vector.bn_stats(stat[j][:, s, :], src[:, s, :])
                last.then_inc(s_st[j], 1)
                dve.wait_ge(s_st[j], n + 1)
                dve.sem_inc(s_turn, 1)
                for s in range(NSEG):
                    last = nc.vector.bn_aggr(mv[j][:, s, :], stat[j][:, s, :])
                last.then_inc(s_mv[j], 1)

            def norm(n, j, src):
                v, y, t = mv[j][:, :, 1], rs0[j][:, :], nw[j]
                dve.wait_ge(s_r0[j], n + 1)
                nc.vector.scalar_tensor_tensor(out=t[:, 0, :], in0=v, scalar=EPS, in1=y,
                                               op0=ALU.add, op1=ALU.mult).then_inc(s_nw[j], 1)
                dve.wait_ge(s_nw[j], 3 * n + 1)
                nc.vector.tensor_tensor(t[:, 1, :], t[:, 0, :], y, ALU.mult).then_inc(s_nw[j], 1)
                dve.wait_ge(s_nw[j], 3 * n + 2)
                nc.vector.tensor_scalar(t[:, 2, :], t[:, 1, :], -0.5, 1.5, ALU.mult, ALU.add).then_inc(s_nw[j], 1)
                dve.wait_ge(s_nw[j], 3 * n + 3)
                nc.vector.tensor_tensor(rstd[j][:, :], t[:, 2, :], y, ALU.mult).then_inc(s_rs[j], 1)
                dve.wait_ge(s_rs[j], n + 1)
                if j == 0:
                    after(dve, s_xst, 16 * (n - 1))
                    after(dve, s_x2T, n - 1)
                else:
                    dve.wait_ge(s_xT, min_seq(n + 2))
                    if isinstance(n, int):
                        after(dve, s_xst, 16 * n)
                for s in range(NSEG):
                    last = nc.vector.tensor_scalar(normed[:, s, :], src[:, s, :], mv[j][:, s, 0:1],
                                                   rstd[j][:, s:s + 1], ALU.subtract, ALU.mult)
                last.then_inc(s_xn[j], 1)

            def attended(n, q):
                dve.wait_ge(s_E, n + 1)
                nc.vector.reciprocal(rinv[:, :], rsum[:, :]).then_inc(s_ri, 1)
                dve.wait_ge(s_at, n + 1)
                dve.wait_ge(s_ri, n + 1)
                after(dve, s_hst, 16 * (n - 1))
                for s in range(NSEG):
                    last = nc.vector.tensor_scalar(hres[q][:, s, :], psXf[:, s * D:(s + 1) * D],
                                                   rinv[:, s:s + 1], None, ALU.mult)
                last.then_inc(s_h1, 1)
                dve.wait_ge(s_h1, n + 1)
                stats(n, 0, hres[q])

            def add_block(m, q):
                dve.wait_ge(s_op, m + 1)
                h = hres[q][:, :, :].rearrange("p s d -> p (s d)")
                nc.vector.tensor_tensor(h, psXf[:, 0:NSEG * D], h, ALU.add).then_inc(s_h2, 1)
                dve.wait_ge(s_h2, m + 1)
                stats(m, 1, hres[q])

            def conv(n, part):
                for k in range(TAPS):
                    for c in range(CH):
                        src = xin[:, c, k:k + L]
                        if k == 0:
                            last = nc.vector.tensor_scalar(u[:, c, :], src, w_cv[:, c, 0:1], b_cv[:, c:c + 1],
                                                           ALU.mult, ALU.add)
                        else:
                            last = nc.vector.scalar_tensor_tensor(out=u[:, c, :], in0=src,
                                                                  scalar=w_cv[:, c, k:k + 1], in1=u[:, c, :],
                                                                  op0=ALU.mult, op1=ALU.add)
                    last.then_inc(s_cv, 1)
                    if k < TAPS - 1:
                        dve.wait_ge(s_cv, TAPS * n + k + 1)

            def run_conv(n):
                dve.wait_ge(s_xc[0], n + 1)
                dve.wait_ge(s_xc[1], n + 1)
                after(dve, s_dtu[1], n)
                after(dve, s_bcp, n)
                conv(n, 0)

            def copy_bc(n):
                dve.wait_ge(s_bcp, n + 1)
                after(dve, s_bcw, 16 * n)
                nc.vector.tensor_copy(bc_rows[:, :], psX[0:2 * NS, 0, 0:L]).then_inc(s_bcc, 1)

            def finish_dt(n, q, half):
                a, z = 2 * half, 2 * half + 2
                dve.wait_ge(s_dl[half], n + 1)
                nc.vector.scalar_tensor_tensor(out=dt[q][:, a:z, :], in0=xin[:, a:z, TAPS - 1:], scalar=0.0,
                                               in1=soft[:, a:z, :], op0=ALU.max, op1=ALU.add).then_inc(s_dt[half], 1)

            dve.wait_ge(s_w, 160)
            row_max(0)
            attended(0, 0)
            norm(0, 0, hres[0])
            run_conv(0)
            copy_bc(0)
            finish_dt(0, 0, 0)
            finish_dt(0, 0, 1)

            def body(b, q, first, last):
                n, m, r = b + 1, b - 1, 1 - q
                for k in range(16):
                    scan(b, k // 4, k % 4)
                    times_c(b, k // 4, k % 4)
                    if k % 4 == 1 and k > 4:
                        gate(b, q, k // 4 - 1)
                    if k == 5:
                        pass
                    if not first:
                        if k == 1:
                            gate(m, r, 3)
                        if k == 2:
                            add_block(m, r)
                        if k == 4:
                            norm(m, 1, hres[r])
                    if not last:
                        if k == 1:
                            row_max(n)
                        if k == 5:
                            attended(n, r)
                        if k == 7:
                            norm(n, 0, hres[r])
                        if k == 10:
                            run_conv(n)
                        if k == 13:
                            copy_bc(n)
                        if k == 15:
                            finish_dt(n, r, 0)
                            finish_dt(n, r, 1)

            each(dve, body)
            gate(NB - 1, (NB - 1) % 2, 3)
            add_block(NB - 1, (NB - 1) % 2)
            norm(NB - 1, 1, hres[(NB - 1) % 2])

        @block.tensor
        def _(pe):
            def turn_q(n, q):
                pe.wait_ge(s_x, 32 * (n + 1))
                after(pe, s_dx[0], n)
                for kd in range(KD):
                    for s in range(NSEG):
                        last = nc.tensor.transpose(psT[:, kd, s * P:(s + 1) * P],
                                                   xs[q][:, s, kd * P:(kd + 1) * P], ident[:, :])
                last.then_inc(s_qT, 1)

            def scores(n):
                pe.wait_ge(s_qTc, n + 1)
                after(pe, s_dx[1], n)
                for s in range(NSEG):
                    for kd in range(KD):
                        t = turned[:, kd, s * P:(s + 1) * P]
                        last = nc.tensor.matmul(psW[:, 0, s * P:(s + 1) * P], t, t, start=(kd == 0),
                                                stop=(kd == KD - 1))
                last.then_inc(s_S, 1)

            def turn_prob(n):
                pe.wait_ge(s_E, n + 1)
                for s in range(NSEG):
                    last = nc.tensor.transpose(psT[:, 0, s * P:(s + 1) * P], prob[:, s, :], ident[:, :])
                last.then_inc(s_ET, 1)

            def attend(n, q):
                pe.wait_ge(s_ETc, n + 1)
                after(pe, s_h2, n - 1)
                after(pe, s_bcc, n)
                for s in range(NSEG):
                    last = nc.tensor.matmul(psXf[:, s * D:(s + 1) * D], prob_t[:, s, :], xs[q][:, s, :],
                                            start=True, stop=True)
                last.then_inc(s_at, 1)

            def turn_normed(n, j, done, free):
                pe.wait_ge(s_xn[j], n + 1)
                for kd in range(KD):
                    for s in range(NSEG):
                        last = nc.tensor.transpose(psT[:, kd, s * P:(s + 1) * P],
                                                   normed[:, s, kd * P:(kd + 1) * P], ident[:, :])
                last.then_inc(done, 1)

            def project(n, dst, lhs, cols, rhs, kk, done):
                for j, c in enumerate(cols):
                    for k in range(kk):
                        last = nc.tensor.matmul(dst[:, j, 0:L], lhs[:, k, c * P:(c + 1) * P], rhs[:, k, :],
                                                start=(k == 0), stop=(k == kk - 1))
                last.then_inc(done, 1)

            def project_xin(n):
                pe.wait_ge(s_xTc, n + 1)
                after(pe, s_lgc, n - 1)
                project(n, psW, w_in, (0, 1), turned, KD, s_xp[0])
                pe.wait_ge(s_h1, n + 1)
                project(n, psX, w_in, (2, 3), turned, KD, s_xp[1])

            def project_z(n, half):
                if half == 0:
                    project(n, psT, w_in, (4, 5), turned, KD, s_zp[0])
                else:
                    pe.wait_ge(s_xc[0], n + 1)
                    project(n, psW, w_in, (6, 7), turned, KD, s_zp[1])

            def project_bc(n):
                pe.wait_ge(s_u, n + 1)
                pe.wait_ge(s_xc[1], n + 1)
                for k in range(CH):
                    last = nc.tensor.matmul(psX[0:2 * NS, 0, 0:L], w_bc[:, k, :], u[:, k, :],
                                            start=(k == 0), stop=(k == CH - 1))
                last.then_inc(s_bcp, 1)

            def project_dt(n, half):
                pe.wait_ge(s_zs[half], n + 1)
                project(n, (psT, psW)[half], w_dt, (2 * half, 2 * half + 1), u, CH, s_dp[half])

            def project_out(m):
                pe.wait_ge(s_yz, CH * (m + 1))
                after(pe, s_bcc, min_seq(m + 2))
                for s in range(NSEG):
                    for c in range(CH):
                        last = nc.tensor.matmul(psXf[:, s * D:(s + 1) * D], yz[:, c, s * P:(s + 1) * P],
                                                w_out[:, c, :], start=(c == 0), stop=(c == CH - 1))
                last.then_inc(s_op, 1)

            def route(m, with_next):
                pe.wait_ge(s_x2Tc, m + 1)
                for s in range(NSEG):
                    for kd in range(KD):
                        last = nc.tensor.matmul(psW[:, 0, s * NE:(s + 1) * NE], turned[:, kd, s * P:(s + 1) * P],
                                                w_gt[:, kd, :], start=(kd == 0), stop=(kd == KD - 1))
                last.then_inc(s_lg, 1)

            def sum_y(b, c, g):
                pe.wait_ge(s_hc[g], 4 * b + c + 1)
                if g == 0:
                    after(pe, s_yz, 4 * b + c - 1)
                for j in range(GN):
                    last = nc.tensor.matmul(psY[c % 2][:, 0:L], ident[:, :], hid[g][:, j, :],
                                            start=(g == 0 and j == 0), stop=(g == NG - 1 and j == GN - 1))
                last.then_inc(s_ys[g], 1)

            pe.wait_ge(s_w, 160)
            pe.wait_ge(s_idn, 1)
            turn_q(0, 0)
            scores(0)
            turn_prob(0)
            attend(0, 0)
            turn_normed(0, 0, s_xT, None)
            project_xin(0)
            pe.wait_ge(s_xTc, 1)
            project_z(0, 0)
            project_z(0, 1)
            project_bc(0)
            project_dt(0, 0)
            project_dt(0, 1)

            def body(b, q, first, last):
                n, m, r = b + 1, b - 1, 1 - q
                for k in range(16):
                    sum_y(b, k // 4, k % 4)
                    if not last:
                        if k == 0:
                            turn_q(n, r)
                        if k == 1:
                            scores(n)
                        if k == 3:
                            turn_prob(n)
                        if k == 4:
                            attend(n, r)
                    if not first:
                        if k == 1:
                            project_out(m)
                        if k == 5:
                            pe.wait_ge(s_ETc, m + 2) if not last else None
                            turn_normed(m, 1, s_x2T, None)
                        if k == 6:
                            pe.wait_ge(s_E, m + 2) if not last else None
                            route(m, not last)
                    if not last:
                        if k == 8:
                            turn_normed(n, 0, s_xT, None)
                        if k == 9:
                            project_xin(n)
                        if k == 10:
                            project_z(n, 0)
                        if k == 11:
                            project_z(n, 1)
                        if k == 13:
                            project_bc(n)
                            project_dt(n, 0)
                        if k == 14:
                            project_dt(n, 1)

            each(pe, body)
            project_out(NB - 1)
            turn_normed(NB - 1, 1, s_x2T, None)
            route(NB - 1, False)


def router_phase(nc, w, lg_tab, x_tab, r_tab, inc_dram, NT):
    G = 8
    GE = NE // G
    TOPG = 4
    SCALE = 2.5
    FAR = -3.0e38
    TAKEN = -3.2e38
    NTG = NT * G
    RW = P + 1
    PT = 4
    with ExitStack() as ctx:
        def sb(name, shape, dt=F32):
            return ctx.enter_context(nc.sbuf_tensor(name, shape, dt))

        def sem(name):
            return ctx.enter_context(nc.semaphore(name))

        logits = sb("r_logits", [P, NT, NE])
        score = sb("r_score", [P, NT, NE])
        biased = sb("r_biased", [P, NT, NE])
        work = sb("r_work", [P, NT, NE])
        masked = logits
        small = sb("r_small", [P, 4, NTG, 2])
        gsum = sb("r_gsum", [P, NT, G])
        rank = sb("r_rank", [P, NT, G])
        top8 = sb("r_top8", [P, NT, 8])
        chosen = sb("r_chosen", [P, NT, NE], BF16)
        wsum = sb("r_wsum", [P, NT])
        winv = sb("r_winv", [P, NT])
        bias = sb("r_bias", [P, NE])
        tri = sb("r_tri", [P, P], BF16)
        ones = sb("r_ones", [NE, NT])
        incl = sb("r_incl", [NE, NT])
        counts = sb("r_counts", [NE, NT, RW])
        psR = [ctx.enter_context(nc.psum_tensor(f"r_psR{j}", [P, 512], F32)) for j in range(2)]

        s_ld, s_e, s_sc = sem("r_loaded"), sem("r_exped"), sem("r_scored")
        s_v = sem("r_vector_step")
        s_tri0, s_tri = sem("r_tri_ones"), sem("r_tri_set")
        s_ch, s_w, s_run, s_cc = sem("r_chosen_ready"), sem("r_weights_ready"), sem("r_running"), sem("r_copied")
        s_rt, s_out = sem("r_counts_ready"), sem("r_stored")
        block = ctx.enter_context(nc.Block())

        @block.sync
        def _(sp):
            sp.dma_start(logits[:, :, :].rearrange("p (b s) e -> p b (s e)", s=NSEG),
                         lg_tab.rearrange("b p s e -> p b (s e)")).then_inc(s_ld, 16)
            sp.dma_start(bias[:, :], w["gate_bias"].partition_broadcast(P)).then_inc(s_ld, 16)
            sp.wait_ge(s_w, 1)
            sp.dma_start(x_tab.rearrange("(t p) c -> p t c", p=P)[:, :, D:D + NE], work[:, :, :]).then_inc(s_out, 16)
            sp.wait_ge(s_rt, 1)
            sp.dma_start(r_tab.rearrange("(e t) c -> e t c", e=NE), counts[:, :, :]).then_inc(s_out, 16)
            sp.dma_start(inc_dram, incl[:, :]).then_inc(s_out, 16)
            sp.wait_ge(s_out, 48)

        @block.gpsimd
        def _(pool):
            nc.gpsimd.memset(tri[:, :], 1.0).then_inc(s_tri0, 1)
            pool.wait_ge(s_tri0, 1)
            nc.gpsimd.affine_select(out=tri[:, :], in_=tri[:, :], compare_op=ALU.is_ge, fill=0.0,
                                    base=0, pattern=[[1, P]], channel_multiplier=-1).then_inc(s_tri, 1)

        @block.scalar
        def _(act):
            act.wait_ge(s_ld, 32)
            nc.scalar.activation(logits[:, :, :], logits[:, :, :], ACT.Exp, scale=-1.0).then_inc(s_e, 1)
            for j in range(NT // PT):
                act.wait_ge(s_run, j + 1)
                nc.scalar.activation(counts[:, j * PT:(j + 1) * PT, 0:P],
                                     psR[j % 2][0:NE, :].rearrange("e (t k) -> e t k", t=PT),
                                     ACT.Copy).then_inc(s_cc, 1)

        @block.tensor
        def _(pe):
            pe.wait_ge(s_tri, 1)
            pe.wait_ge(s_ch, 1)
            for j in range(NT // PT):
                after(pe, s_cc, j - 1)
                for t in range(PT):
                    last = nc.tensor.matmul(psR[j % 2][0:NE, t * P:(t + 1) * P], chosen[:, j * PT + t, :],
                                            tri[:, :], start=True, stop=True)
                last.then_inc(s_run, 1)

        @block.vector
        def _(dve):
            steps = [0]

            def step(ins):
                steps[0] += 1
                ins.then_inc(s_v, 1)
                dve.wait_ge(s_v, steps[0])

            step(nc.vector.memset(ones[:, :], 1.0))
            dve.wait_ge(s_e, 1)
            step(nc.vector.tensor_scalar(logits[:, :, :], logits[:, :, :], 1.0, None, ALU.add))
            step(nc.vector.reciprocal(score[:, :, :], logits[:, :, :]))
            step(nc.vector.tensor_tensor(biased[:, :, :], score[:, :, :],
                                         bias[:, :].unsqueeze(1).to_broadcast([P, NT, NE]), ALU.add))
            grp = biased[:, :, :].rearrange("p t (g h k) -> p (t g) h k", g=G, h=2)
            w2 = work[:, :, :].rearrange("p t e -> p (t e)")
            hi = w2[:, 0:NTG * 4].rearrange("p (n k) -> p n k", k=4)
            lo = w2[:, NTG * 4:NTG * 8].rearrange("p (n k) -> p n k", k=4)
            nc.vector.tensor_tensor(hi, grp[:, :, 0, :], grp[:, :, 1, :], ALU.max)
            step(nc.vector.tensor_tensor(lo, grp[:, :, 0, :], grp[:, :, 1, :], ALU.min))
            hi2, mn, mx, lo2 = (small[:, j, :, :] for j in range(4))
            nc.vector.tensor_tensor(hi2, hi[:, :, 0:2], hi[:, :, 2:4], ALU.max)
            nc.vector.tensor_tensor(mn, hi[:, :, 0:2], hi[:, :, 2:4], ALU.min)
            step(nc.vector.tensor_tensor(mx, lo[:, :, 0:2], lo[:, :, 2:4], ALU.max))
            step(nc.vector.tensor_tensor(lo2, mn, mx, ALU.max))
            v = [w2[:, j * NTG:(j + 1) * NTG] for j in range(4)]
            nc.vector.tensor_tensor(v[0], hi2[:, :, 0], hi2[:, :, 1], ALU.max)
            nc.vector.tensor_tensor(v[1], hi2[:, :, 0], hi2[:, :, 1], ALU.min)
            step(nc.vector.tensor_tensor(v[2], lo2[:, :, 0], lo2[:, :, 1], ALU.max))
            step(nc.vector.tensor_tensor(v[3], v[1], v[2], ALU.max))
            gs = gsum[:, :, :]
            step(nc.vector.tensor_tensor(gs.rearrange("p t g -> p (t g)"), v[0], v[3], ALU.add))
            cmp = work[:, :, :].rearrange("p t (g j) -> p t g j", g=G)
            for g in range(G):
                own = gs[:, :, g:g + 1]
                if g:
                    nc.vector.tensor_tensor(cmp[:, :, g, 0:g], gs[:, :, 0:g], own.to_broadcast([P, NT, g]), ALU.is_ge)
                last = nc.vector.tensor_tensor(cmp[:, :, g, g:G], gs[:, :, g:G], own.to_broadcast([P, NT, G - g]),
                                               ALU.is_gt)
            step(last)
            rk = rank[:, :, :].rearrange("p t g -> p (t g)")
            step(nc.vector.tensor_reduce(rk, work[:, :, :].rearrange("p t (g j) -> p (t g) j", g=G), AX.X, ALU.add))
            step(nc.vector.tensor_scalar(rk, rk, float(TOPG), FAR, ALU.is_ge, ALU.mult))
            step(nc.vector.tensor_tensor(masked[:, :, :].rearrange("p t (g k) -> p (t g) k", g=G),
                                         biased[:, :, :].rearrange("p t (g k) -> p (t g) k", g=G),
                                         rk.unsqueeze(2).to_broadcast([P, NTG, GE]), ALU.add))
            for t in range(NT):
                last = nc.vector.max(top8[:, t, :], masked[:, t, :])
            step(last)
            for t in range(NT):
                last = nc.vector.match_replace(work[:, t, :], top8[:, t, :], masked[:, t, :], TAKEN)
            step(last)
            nc.vector.tensor_tensor(chosen[:, :, :], work[:, :, :], masked[:, :, :], ALU.not_equal).then_inc(s_ch, 1)
            dve.wait_ge(s_ch, 1)
            step(nc.vector.tensor_tensor(biased[:, :, :], score[:, :, :], chosen[:, :, :], ALU.mult))
            step(nc.vector.tensor_reduce(wsum[:, :], biased[:, :, :], AX.X, ALU.add))
            step(nc.vector.tensor_scalar(wsum[:, :], wsum[:, :], 1e-20, None, ALU.add))
            step(nc.vector.reciprocal(winv[:, :], wsum[:, :]))
            step(nc.vector.tensor_scalar(winv[:, :], winv[:, :], SCALE, None, ALU.mult))
            nc.vector.tensor_tensor(work[:, :, :], biased[:, :, :],
                                    winv[:, :].unsqueeze(2).to_broadcast([P, NT, NE]), ALU.mult).then_inc(s_w, 1)
            dve.wait_ge(s_cc, NT // PT)
            step(nc.vector.tensor_tensor_scan(incl[:, :], ones[:, :], counts[:, :, P - 1], 0.0, ALU.mult, ALU.add))
            nc.vector.tensor_tensor(counts[:, :, P], incl[:, :], counts[:, :, P - 1], ALU.subtract).then_inc(s_rt, 1)


def expert_phase(nc, w, x_tab, r_tab, inc_dram, h_out, NT):
    NTOK = NT * P
    CAP = 256
    NH = CAP // P
    NSL = NE * NH
    RW = P + 1
    XW = D + NE
    LB = 8
    EB = 4
    I = w["gate"].shape[2]
    assert I == P
    with ExitStack() as ctx:
        def sb(name, shape, dt=F32):
            return ctx.enter_context(nc.sbuf_tensor(name, shape, dt))

        def sem(name):
            return ctx.enter_context(nc.semaphore(name))

        ident = sb("e_ident", [P, P])
        zero = sb("e_zero", [P, NH, D])
        incl = sb("e_incl", [P, NE, NT])
        below = sb("e_below", [P, NE, NT])
        tile_of = sb("e_tile_of", [P, NE, NH])
        over = sb("e_over", [P, NE, NH])
        tile_in = sb("e_tile_in", [P, NE, NH])
        base_i = sb("e_base_i", [P, NE, NH], I32)
        base = sb("e_base", [P, NE, NH])
        slot_i = sb("e_slot_i", [P, NE, NH], I32)
        slot = sb("e_slot", [P, NE, NH])
        row = sb("e_row", [P, NSL], U32)
        row_st = [sb(f"e_row_st{q}", [P, LB], U32) for q in range(2)]
        rrow = [sb(f"e_rrow{q}", [P, LB, RW]) for q in range(2)]
        lslot = [sb(f"e_lslot{q}", [P, LB]) for q in range(2)]
        le = [sb(f"e_le{q}", [P, LB, P]) for q in range(2)]
        place = sb("e_place", [P, NSL])
        tok = sb("e_tok", [P, NSL])
        far = sb("e_far", [P, NSL])
        src = sb("e_src", [P, NSL], U32)
        dst = sb("e_dst", [P, NSL], U32)
        src_st = [sb(f"e_src_st{q}", [P, NH], U32) for q in range(EB)]
        dst_st = [sb(f"e_dst_st{q}", [P, NH], U32) for q in range(EB)]
        xg = [sb(f"e_xg{q}", [P, NH, XW]) for q in range(EB)]
        xt = [sb(f"e_xt{q}", [P, KD, CAP]) for q in range(2)]
        wg = [sb(f"e_wg{q}", [P, KD, I]) for q in range(EB)]
        wu = [sb(f"e_wu{q}", [P, KD, I]) for q in range(EB)]
        wd = [sb(f"e_wd{q}", [P, D]) for q in range(EB)]
        sg = [sb(f"e_sg{q}", [P, CAP]) for q in range(2)]
        at = [sb(f"e_at{q}", [P, CAP]) for q in range(2)]
        wcol = [sb(f"e_wcol{q}", [P, NH]) for q in range(2)]
        ys = [sb(f"e_ys{q}", [P, NH, D]) for q in range(2)]
        psG = [ctx.enter_context(nc.psum_tensor(f"e_psG{j}", [P, KD, CAP], F32)) for j in range(2)]
        psU = [ctx.enter_context(nc.psum_tensor(f"e_psU{j}", [P, 2, CAP], F32)) for j in range(2)]
        psO = [ctx.enter_context(nc.psum_tensor(f"e_psO{j}", [P, NH, D], F32)) for j in range(2)]

        s_c0, s_c = sem("e_ident_cleared"), sem("e_constants_set")
        s_z, s_zst, s_inc = sem("e_zeros_set"), sem("e_spare_rows_zeroed"), sem("e_incl_loaded")
        s_v = sem("e_vector_step")
        s_rowst = [sem(f"e_row_staged{q}") for q in range(2)]
        s_rr = [sem(f"e_rrow_gathered{q}") for q in range(2)]
        s_ls = [sem(f"e_lslot_ready{q}") for q in range(2)]
        s_le = [sem(f"e_le_ready{q}") for q in range(2)]
        s_pl = [sem(f"e_place_ready{q}") for q in range(2)]
        s_wt = [sem(f"e_weights_loaded{q}") for q in range(EB)]
        s_st = sem("e_indices_staged")
        s_xg = [sem(f"e_x_gathered{q}") for q in range(EB)]
        s_xT, s_xTc = sem("e_x_turned"), sem("e_x_turned_copied")
        s_gu, s_sg, s_at = sem("e_gate_up"), sem("e_silu"), sem("e_act_ready")
        s_yo, s_wc, s_ys = sem("e_down"), sem("e_wcol_ready"), sem("e_scaled")
        s_sc = sem("e_scattered")
        s_turn = sem("e_pool_turn")
        block = ctx.enter_context(nc.Block())

        @block.sync
        def _(sp):
            sp.wait_ge(s_z, 1)
            sp.dma_start(h_out[NTOK:NTOK + CAP, :].rearrange("(h p) d -> p h d", p=P), zero[:, :, :]).then_inc(s_zst, 16)
            sp.dma_start(incl[:, :, :].rearrange("p e t -> p (e t)"),
                         inc_dram.rearrange("e t -> (e t)").partition_broadcast(P)).then_inc(s_inc, 16)

            def load(e, q):
                sp.dma_start(wg[q][:, :, :], w["gate"][e].rearrange("(k p) i -> p k i", p=P)).then_inc(s_wt[q], 16)
                sp.dma_start(wu[q][:, :, :], w["up"][e].rearrange("(k p) i -> p k i", p=P)).then_inc(s_wt[q], 16)
                sp.dma_start(wd[q][:, :], w["down"][e]).then_inc(s_wt[q], 16)

            for q in range(EB):
                load(q, q)
            with sp.Fori(1, NE // EB) as i:
                for q in range(EB):
                    sp.wait_ge(s_yo, EB * i + q - EB + 1)
                    sp.sem_inc(s_turn, 1)
                    load(EB * i + q, q)
            sp.wait_ge(s_zst, 16)

        @block.gpsimd
        def _(pool):
            nc.gpsimd.memset(ident[:, :], 0.0).then_inc(s_c0, 1)
            pool.wait_ge(s_c0, 1)
            nc.gpsimd.affine_select(out=ident[:, :], in_=ident[:, :], compare_op=ALU.not_equal, fill=1.0,
                                    base=0, pattern=[[-1, P]], channel_multiplier=1).then_inc(s_c, 1)
            nc.gpsimd.iota(base_i[:, :, :], pattern=[[NT, NE], [0, NH]], base=0, channel_multiplier=0).then_inc(s_c, 1)
            nc.gpsimd.iota(slot_i[:, :, :], pattern=[[0, NE], [P, NH]], base=0, channel_multiplier=1).then_inc(s_c, 1)
            with pool.Fori(0, NSL // LB // 2) as i:
                for q in range(2):
                    pool.wait_ge(s_rowst[q], i + 1)
                    pool.sem_inc(s_turn, 1)
                    for j in range(LB):
                        nc.gpsimd.indirect_dma_start(
                            out=rrow[q][:, j, :], out_offset=None, in_=r_tab,
                            in_offset=bass.IndirectOffsetOnAxis(ap=row_st[q][:, j:j + 1], axis=0)).then_inc(s_rr[q], 16)

            def gather(e, q):
                pool.wait_ge(s_st, e + 1)
                pool.sem_inc(s_turn, 1)
                for h in range(NH):
                    nc.gpsimd.indirect_dma_start(
                        out=xg[q][:, h, :], out_offset=None, in_=x_tab,
                        in_offset=bass.IndirectOffsetOnAxis(ap=src_st[q][:, h:h + 1], axis=0)).then_inc(s_xg[q], 16)

            def scatter(e, q):
                pool.wait_ge(s_ys, e + 1)
                after(pool, s_sc, 16 * NH * e)
                pool.sem_inc(s_turn, 1)
                for h in range(NH):
                    nc.gpsimd.indirect_dma_start(
                        out=h_out, out_offset=bass.IndirectOffsetOnAxis(ap=dst_st[q][:, h:h + 1], axis=0),
                        in_=ys[q % 2][:, h, :], in_offset=None, compute_op=ALU.add).then_inc(s_sc, 16)

            pool.wait_ge(s_zst, 16)
            gather(0, 0)
            gather(1, 1)
            for e in range(EB):
                gather(e + 2, (e + 2) % EB)
                scatter(e, e)
            with pool.Fori(1, NE // EB - 1) as i:
                for q in range(EB):
                    gather(EB * i + q + 2, (q + 2) % EB)
                    scatter(EB * i + q, q)
            for q in range(EB):
                e = NE - EB + q
                if q + 2 < EB:
                    gather(e + 2, q + 2)
                scatter(e, q)
            pool.wait_ge(s_sc, 16 * NH * NE)

        @block.scalar
        def _(act):
            def expert(e, q):
                r = q % 2
                act.wait_ge(s_xT, e + 1)
                nc.scalar.activation(xt[r][:, :, :], psG[r][:, :, :], ACT.Copy).then_inc(s_xTc, 1)
                act.wait_ge(s_gu, e + 1)
                nc.scalar.activation(sg[r][:, :], psU[r][:, 0, :], ACT.Silu).then_inc(s_sg, 1)

            with act.Fori(0, NE // EB) as i:
                for q in range(EB):
                    expert(EB * i + q, q)

        @block.tensor
        def _(pe):
            pe.wait_ge(s_c, 3)

            def expert(i, e, q):
                r = q % 2
                pe.wait_ge(s_xg[q], 16 * NH * (i + 1))
                after(pe, s_xTc, e - 1)
                for h in range(NH):
                    for k in range(KD):
                        last = nc.tensor.transpose(psG[r][:, k, h * P:(h + 1) * P], xg[q][:, h, k * P:(k + 1) * P],
                                                   ident[:, :])
                last.then_inc(s_xT, 1)
                pe.wait_ge(s_wt[q], 48 * (i + 1))
                pe.wait_ge(s_xTc, e + 1)
                after(pe, s_at, e - 1)
                for j, m in enumerate((wg, wu)):
                    for k in range(KD):
                        last = nc.tensor.matmul(psU[r][:, j, :], m[q][:, k, :], xt[r][:, k, :],
                                                start=(k == 0), stop=(k == KD - 1))
                last.then_inc(s_gu, 1)
                pe.wait_ge(s_at, e + 1)
                after(pe, s_ys, e - 1)
                for h in range(NH):
                    last = nc.tensor.matmul(psO[r][:, h, :], at[r][:, h * P:(h + 1) * P], wd[q][:, :],
                                            start=True, stop=True)
                last.then_inc(s_yo, 1)

            for q in range(EB):
                expert(0, q, q)
            with pe.Fori(1, NE // EB) as i:
                for q in range(EB):
                    expert(i, EB * i + q, q)

        @block.vector
        def _(dve):
            steps = [0]

            def step(ins):
                steps[0] += 1
                ins.then_inc(s_v, 1)
                dve.wait_ge(s_v, steps[0])

            nc.vector.memset(zero[:, :, :], 0.0).then_inc(s_z, 1)
            dve.wait_ge(s_c, 3)
            nc.vector.tensor_copy(base[:, :, :], base_i[:, :, :])
            step(nc.vector.tensor_copy(slot[:, :, :], slot_i[:, :, :]))
            dve.wait_ge(s_inc, 16)
            for h in range(NH):
                step(nc.vector.tensor_scalar(below[:, :, :], incl[:, :, :], slot[:, 0, h:h + 1], None, ALU.is_le))
                step(nc.vector.tensor_reduce(tile_of[:, :, h], below[:, :, :], AX.X, ALU.add))
            nc.vector.tensor_scalar(over[:, :, :], tile_of[:, :, :], float(NT), None, ALU.is_ge)
            step(nc.vector.tensor_scalar(tile_in[:, :, :], tile_of[:, :, :], float(NT - 1), None, ALU.min))
            flat = lambda t: t[:, :, :].rearrange("p e h -> p (e h)")
            step(nc.vector.tensor_tensor(row[:, :], flat(tile_in), flat(base), ALU.add))

            def stage_rows(j, q):
                nc.vector.tensor_copy(row_st[q][:, :], row[:, bass.ds(j * LB, LB)]).then_inc(s_rowst[q], 1)

            def locate(i, j, q):
                dve.wait_ge(s_rr[q], 16 * LB * (i + 1))
                nc.vector.tensor_tensor(lslot[q][:, :], flat(slot)[:, bass.ds(j * LB, LB)], rrow[q][:, :, P],
                                        ALU.subtract).then_inc(s_ls[q], 1)
                dve.wait_ge(s_ls[q], i + 1)
                nc.vector.tensor_tensor(le[q][:, :, :], rrow[q][:, :, 0:P],
                                        lslot[q][:, :].unsqueeze(2).to_broadcast([P, LB, P]),
                                        ALU.is_le).then_inc(s_le[q], 1)
                dve.wait_ge(s_le[q], i + 1)
                nc.vector.tensor_reduce(place[:, bass.ds(j * LB, LB)], le[q][:, :, :], AX.X,
                                        ALU.add).then_inc(s_pl[q], 1)

            NL = NSL // LB // 2
            stage_rows(0, 0)
            stage_rows(1, 1)
            with dve.Fori(0, NL - 1) as i:
                for q in range(2):
                    locate(i, 2 * i + q, q)
                    stage_rows(2 * i + q + 2, q)
            for q in range(2):
                locate(NL - 1, 2 * (NL - 1) + q, q)
            dve.wait_ge(s_pl[0], NL)
            dve.wait_ge(s_pl[1], NL)
            step(nc.vector.scalar_tensor_tensor(out=tok[:, :], in0=flat(tile_in), scalar=float(P), in1=place[:, :],
                                                op0=ALU.mult, op1=ALU.add))
            nc.vector.tensor_scalar(src[:, :], tok[:, :], float(NTOK - 1), None, ALU.min)
            step(nc.vector.scalar_tensor_tensor(out=far[:, :], in0=flat(slot), scalar=float(NTOK), in1=tok[:, :],
                                                op0=ALU.add, op1=ALU.subtract))
            step(nc.vector.tensor_tensor(far[:, :], far[:, :], flat(over), ALU.mult))
            step(nc.vector.tensor_tensor(dst[:, :], far[:, :], tok[:, :], ALU.add))

            def stage(e, q):
                nc.vector.tensor_copy(src_st[q][:, :], src[:, bass.ds(e * NH, NH)])
                nc.vector.tensor_copy(dst_st[q][:, :], dst[:, bass.ds(e * NH, NH)]).then_inc(s_st, 1)

            def expert(i, e, q):
                r = q % 2
                dve.wait_ge(s_sg, e + 1)
                nc.vector.tensor_tensor(at[r][:, :], sg[r][:, :], psU[r][:, 1, :], ALU.mult).then_inc(s_at, 1)
                nc.vector.tensor_copy(wcol[r][:, :], xg[q][:, :, bass.ds(D + e, 1)].rearrange("p h o -> p (h o)")
                                      ).then_inc(s_wc, 1)
                dve.wait_ge(s_yo, e + 1)
                dve.wait_ge(s_wc, e + 1)
                after(dve, s_sc, 16 * NH * (e - 1))
                for h in range(NH):
                    last = nc.vector.tensor_scalar(ys[r][:, h, :], psO[r][:, h, :], wcol[r][:, h:h + 1], None,
                                                   ALU.mult)
                last.then_inc(s_ys, 1)

            for q in range(EB):
                stage(q, q)
            for q in range(EB):
                expert(0, q, q)
                dve.wait_ge(s_sc, 16 * NH * (q + 1))
                stage(q + EB, q)
            with dve.Fori(1, NE // EB - 1) as i:
                for q in range(EB):
                    expert(i, EB * i + q, q)
                    dve.wait_ge(s_sc, 16 * NH * (EB * i + q + 1))
                    stage(EB * i + q + EB, q)
            for q in range(EB):
                expert(NE // EB - 1, NE - EB + q, q)


def audio_tower_kernel(nc, x, w, out):
    NT = x.shape[0] * NSEG
    bc_dram = nc.dram_tensor("bc_rows_dram", (2, 2 * NS, L), F32, kind="Internal").ap()
    lg_tab = nc.dram_tensor("logits_dram", (x.shape[0], P, NSEG, NE), F32, kind="Internal").ap()
    x_tab = nc.dram_tensor("x2_weights_dram", (NT * P, D + NE), F32, kind="Internal").ap()
    r_tab = nc.dram_tensor("running_dram", (NE * NT, P + 1), F32, kind="Internal").ap()
    inc_dram = nc.dram_tensor("incl_dram", (NE, NT), F32, kind="Internal").ap()
    sequence_phase(nc, x, w, bc_dram, out, x_tab, lg_tab)
    router_phase(nc, w, lg_tab, x_tab, r_tab, inc_dram, NT)
    expert_phase(nc, w, x_tab, r_tab, inc_dram, out, NT)


def kernel(**inputs):
    import numpy as np
    import concourse.bacc as bacc
    from concourse.bass_utils import run_bass_kernel_spmd

    def as_is(name):
        return np.ascontiguousarray(inputs[name])

    def turned(name):
        return np.ascontiguousarray(np.asarray(inputs[name]).T)

    def by_chunk(name):
        return np.ascontiguousarray(np.asarray(inputs[name]).reshape(CH, P).T)

    host = {
        "x": as_is("x"),
        "in_t": turned("L0_attn_W_in"),
        "conv": as_is("L0_attn_W_conv").reshape(DI, TAPS),
        "b_conv": by_chunk("L0_attn_b_conv"),
        "dt_t": turned("L0_attn_W_dt"),
        "b_dt": by_chunk("L0_attn_b_dt"),
        "b_t": turned("L0_attn_W_B"),
        "c_t": turned("L0_attn_W_C"),
        "a_log": as_is("L0_attn_A_log"),
        "out_t": turned("L0_attn_W_out"),
        "gate_t": turned("L0_ffn_gate_w"),
        "gate_bias": as_is("L0_ffn_gate_bias"),
        "gate": as_is("L0_ffn_w_gate"),
        "up": as_is("L0_ffn_w_up"),
        "down": as_is("L0_ffn_w_down"),
    }
    nc = bacc.Bacc("TRN2", target_bir_lowering=False, num_devices=1)
    w = {k: nc.dram_tensor(f"in_{k}_dram", v.shape, F32, kind="ExternalInput").ap() for k, v in host.items()}
    NB = host["x"].shape[0]
    SPARE = 256
    out = nc.dram_tensor("out_dram", (NB * L + SPARE, D), F32, kind="ExternalOutput").ap()
    audio_tower_kernel(nc, w["x"], w, out)
    r = run_bass_kernel_spmd(nc, [{f"in_{k}_dram": v for k, v in host.items()}], core_ids=[0])
    return r.results[0]["out_dram"][:NB * L].reshape(NB, L, D)
```

```python
from contextlib import ExitStack

import concourse.bass as bass
from concourse import mybir

F32 = mybir.dt.float32
BF16 = mybir.dt.bfloat16
U32 = mybir.dt.uint32
I32 = mybir.dt.int32
ALU = mybir.AluOpType
ACT = mybir.ActivationFunctionType
AX = mybir.AxisListType

P = 128
D = 256
SEG = 256
DIL = 2
NSEG = 3
L = NSEG * P
DI = 512
CH = DI // P
KD = D // P
NS = 16
GN = 4
NG = NS // GN
TAPS = 4
NE = 64
EPS = 1e-5
UNITS = CH * NG
POOL_C = (3,)
POOL_LAG = 3


def after(eng, sem, count):
    if isinstance(count, int) and count <= 0:
        return
    eng.wait_ge(sem, count)


def sequence_phase(nc, x, w, bc_dram, h_out, x_tab, lg_tab):
    NB, S, _ = x.shape
    TAIL = (S - (NSEG - 1) * SEG + DIL - 1) // DIL

    with ExitStack() as ctx:
        def sb(name, shape, dt=F32):
            return ctx.enter_context(nc.sbuf_tensor(name, shape, dt))

        def ps(name, shape):
            return ctx.enter_context(nc.psum_tensor(name, shape, F32))

        def sem(name):
            return ctx.enter_context(nc.semaphore(name))

        w_in = sb("w_in", [P, KD, 2 * DI])
        w_dt = sb("w_dt", [P, CH, DI])
        w_bc = sb("w_bc", [P, CH, 2 * NS])
        w_out = sb("w_out", [P, CH, D])
        w_gt = sb("w_gt", [P, KD, NE])
        w_cv = sb("w_cv", [P, CH, TAPS])
        b_cv = sb("b_cv", [P, CH])
        b_dt = sb("b_dt", [P, CH])
        a_neg = sb("a_neg", [P, CH, NS])
        ident = sb("ident", [P, P])
        xs = sb("xs", [P, NSEG, D])
        h1 = sb("h1", [P, NSEG, D])
        h2 = sb("h2", [P, NSEG, D])
        dt = [sb(f"dt{q}", [P, CH, L]) for q in range(2)]
        zs = [sb(f"zs{q}", [P, CH, L]) for q in range(2)]
        turned = sb("turned", [P, KD, L])
        normed = sb("normed", [P, NSEG, D])
        xin = sb("xin", [P, CH, TAPS - 1 + L])
        u = sb("u", [P, CH, L])
        soft = sb("soft", [P, CH, L])
        prob = soft[:, 0, :].rearrange("p (s k) -> p s k", s=NSEG)
        prob_t = soft[:, 1, :].rearrange("p (s k) -> p s k", s=NSEG)
        dtu = sb("dtu", [P, CH, L])
        bc_rows = sb("bc_rows", [2 * NS, L])
        b_all = sb("b_all", [P, NS, L])
        c_all = sb("c_all", [P, NS, L])
        yz = sb("yz", [P, CH, L])
        logit = sb("logit", [P, NSEG, NE])
        decay = [sb(f"decay{j}", [P, GN, L]) for j in range(2)]
        hid = [[sb(f"hid{j}{g}", [P, GN, L]) for g in range(NG)] for j in range(2)]
        rmax = sb("rmax", [P, NSEG])
        nmax = sb("nmax", [P, NSEG])
        rsum = sb("rsum", [P, NSEG])
        rinv = sb("rinv", [P, NSEG])
        stat = [sb(f"stat{j}", [P, NSEG, 6]) for j in range(2)]
        mv = [sb(f"mv{j}", [P, NSEG, 2]) for j in range(2)]
        lnv = [sb(f"lnv{j}", [P, NSEG]) for j in range(2)]
        rs0 = [sb(f"rs0{j}", [P, NSEG]) for j in range(2)]
        nw = [sb(f"nw{j}", [P, 3, NSEG]) for j in range(2)]
        rstd = [sb(f"rstd{j}", [P, NSEG]) for j in range(2)]
        epsc = sb("epsc", [P, 1])

        psY = [ps(f"psY{j}", [P, 512]) for j in range(2)]
        psT = ps("psT", [P, 2, 512])
        psW = ps("psW", [P, 2, 512])
        psX = ps("psX", [P, 2, 512])
        psXf = psX[:, :, :].rearrange("p a b -> p (a b)")

        s_turn = sem("wait_carrier")
        s_w = sem("weights_loaded")
        s_a0 = sem("a_log_exped")
        s_const = sem("constants_set")
        s_id0 = sem("ident_cleared")
        s_idn = sem("ident_set")
        s_x = sem("x_loaded")
        s_h1st, s_hb = sem("h1_stored"), sem("h1_back")
        s_bcw = sem("bc_rows_stored")
        s_B = [sem(f"b_loaded{g}") for g in range(NG)]
        s_C = [sem(f"c_loaded{g}") for g in range(NG)]
        s_hst = sem("h_stored")
        s_xst = sem("x2_stored")
        s_lst = sem("logits_stored")
        s_dec = [sem(f"decay_ready{g}") for g in range(NG)]
        s_dbu = [sem(f"dbu_ready{g}") for g in range(NG)]
        s_h = [sem(f"scan_done{g}") for g in range(NG)]
        s_hc = [sem(f"hc_ready{g}") for g in range(NG)]
        s_ys = [sem(f"y_summed{g}") for g in range(NG)]
        s_yz = sem("y_gated")
        s_qT, s_qTc = sem("q_turned"), sem("q_turned_copied")
        s_S, s_rm, s_nm, s_E = sem("scores_ready"), sem("row_max"), sem("neg_max"), sem("prob_ready")
        s_ET, s_ETc = sem("prob_turned"), sem("prob_turned_copied")
        s_at, s_ri, s_h1 = sem("attended"), sem("sums_inverted"), sem("h1_ready")
        s_st = [sem(f"stats{j}") for j in range(2)]
        s_mv = [sem(f"mean_var{j}") for j in range(2)]
        s_lv = [sem(f"log_var{j}") for j in range(2)]
        s_r0 = [sem(f"rstd_first{j}") for j in range(2)]
        s_nw = [sem(f"newton{j}") for j in range(2)]
        s_rs = [sem(f"rstd_ready{j}") for j in range(2)]
        s_xn = [sem(f"normed{j}") for j in range(2)]
        s_xT, s_xTc = sem("xn_turned"), sem("xn_turned_copied")
        s_x2T, s_x2Tc = sem("x2_turned"), sem("x2_turned_copied")
        s_xp = [sem(f"xin_product{j}") for j in range(2)]
        s_xc = [sem(f"xin_copied{j}") for j in range(2)]
        s_cv = sem("conv_tap")
        s_zp = [sem(f"z_product{j}") for j in range(2)]
        s_zs = [sem(f"z_silu{j}") for j in range(2)]
        s_u = sem("u_ready")
        s_dp = [sem(f"dt_product{j}") for j in range(2)]
        s_dx = [sem(f"dt_biased{j}") for j in range(2)]
        s_da = [sem(f"dt_abs{j}") for j in range(2)]
        s_de = [sem(f"dt_exp{j}") for j in range(2)]
        s_dl = [sem(f"dt_log{j}") for j in range(2)]
        s_dt = [sem(f"dt_ready{j}") for j in range(2)]
        s_dtu = [sem(f"dtu_ready{j}") for j in range(2)]
        s_bcp, s_bcc = sem("bc_product"), sem("bc_rows_ready")
        s_op, s_h2 = sem("out_product"), sem("h2_ready")
        s_lg, s_lgc = sem("logit_product"), sem("logit_copied")

        def last_seq(count):
            return min(count, NB) if isinstance(count, int) else count

        def each(eng, body):
            body(0, 0, before=False, next=True, after_next=True)
            if NB > 4:
                with eng.Fori(0, (NB - 4) // 2) as i:
                    body(2 * i + 1, 1, before=True, next=True, after_next=True)
                    body(2 * i + 2, 0, before=True, next=True, after_next=True)
            body(NB - 3, (NB - 3) % 2, before=True, next=True, after_next=True)
            body(NB - 2, (NB - 2) % 2, before=True, next=True, after_next=False)
            body(NB - 1, (NB - 1) % 2, before=True, next=False, after_next=False)

        block = ctx.enter_context(nc.Block())

        @block.sync
        def _(sp):
            def wait(sem, count):
                after(sp, sem, count)
                if not isinstance(count, int):
                    sp.sem_inc(s_turn, 1)

            def load_x(n):
                sp.dma_start(xs[:, 0:NSEG - 1, :],
                             x[n, 0:(NSEG - 1) * SEG, :].rearrange("(s p j) d -> j p s d", s=NSEG - 1, j=DIL)[0]
                             ).then_inc(s_x, 16)
                sp.dma_start(xs[0:TAIL, NSEG - 1, :],
                             x[n, (NSEG - 1) * SEG:S, :].rearrange("(p j) d -> j p d", j=DIL)[0]
                             ).then_inc(s_x, 16)

            def rows(tab, n):
                return tab[bass.ds(n * L, L), 0:D].rearrange("(s p) d -> p s d", p=P)

            def store_h1(n):
                wait(s_h1, n + 1)
                sp.dma_start(rows(h_out, n), h1[:, :, :]).then_inc(s_h1st, 16)

            def load_h1(m):
                wait(s_h1st, 16 * (m + 1))
                wait(s_hst, 16 * (m + 1))
                sp.dma_start(h2[:, :, :], rows(h_out, m)).then_inc(s_hb, 16)

            def store_out(m):
                wait(s_h2, m + 1)
                sp.dma_start(rows(h_out, m), h2[:, :, :]).then_inc(s_hst, 16)
                wait(s_xn[1], m + 1)
                sp.dma_start(rows(x_tab, m), normed[:, :, :]).then_inc(s_xst, 16)

            def store_logits(m):
                wait(s_lgc, m + 1)
                sp.dma_start(lg_tab[m], logit[:, :, :]).then_inc(s_lst, 16)

            def store_bc(n, q):
                wait(s_bcc, n + 1)
                sp.dma_start(bc_dram[q], bc_rows[:, :]).then_inc(s_bcw, 16)
                wait(s_bcw, 16 * (n + 1))

            def share(kind, g, q, own):
                to, done, used, at = ((b_all, s_B, s_dbu, 0) if kind == "b" else (c_all, s_C, s_hc, NS))
                wait(used[g], own)
                src = bc_dram[q, at + g * GN:at + (g + 1) * GN, :].rearrange("n l -> (n l)")
                sp.dma_start(to[:, g * GN:(g + 1) * GN, :].rearrange("p n l -> p (n l)"),
                             src.partition_broadcast(P)).then_inc(done[g], 16)

            SHARES = (("b", 0), ("b", 1), ("b", 2), ("c", 0), ("b", 3), ("c", 1), ("c", 2), ("c", 3))

            wait(s_const, 1)
            load_x(0)
            sp.dma_start(w_in[:, :, :], w["in_t"].rearrange("(k p) n -> p k n", p=P)).then_inc(s_w, 16)
            sp.dma_start(w_dt[:, :, :], w["dt_t"].rearrange("(c p) n -> p c n", p=P)).then_inc(s_w, 16)
            sp.dma_start(w_bc[:, :, 0:NS], w["b_t"].rearrange("(c p) n -> p c n", p=P)).then_inc(s_w, 16)
            sp.dma_start(w_bc[:, :, NS:2 * NS], w["c_t"].rearrange("(c p) n -> p c n", p=P)).then_inc(s_w, 16)
            sp.dma_start(w_out[:, :, :], w["out_t"].rearrange("(c p) n -> p c n", p=P)).then_inc(s_w, 16)
            sp.dma_start(w_gt[:, :, :], w["gate_t"].rearrange("(k p) n -> p k n", p=P)).then_inc(s_w, 16)
            sp.dma_start(w_cv[:, :, :], w["conv"].rearrange("(c p) n -> p c n", p=P)).then_inc(s_w, 16)
            sp.dma_start(b_cv[:, :], w["b_conv"]).then_inc(s_w, 16)
            sp.dma_start(b_dt[:, :], w["b_dt"]).then_inc(s_w, 16)
            sp.dma_start(a_neg[:, :, :], w["a_log"].rearrange("(c p) n -> p c n", p=P)).then_inc(s_w, 16)
            for done in (s_hst, s_xst, s_lst):
                sp.sem_inc(done, 16)
            wait(s_at, 1)
            load_x(1)
            store_h1(0)
            store_bc(0, 0)
            for kind, g in SHARES:
                share(kind, g, 0, 0)

            def body(b, q, before, next, after_next):
                n, m = b + 1, b - 1
                if after_next:
                    wait(s_at, n + 1)
                    load_x(b + 2)
                if next:
                    store_h1(n)
                if before:
                    load_h1(m)
                    store_out(m)
                if next:
                    store_bc(n, 1 - q)
                    for kind, g in SHARES[:2]:
                        share(kind, g, 1 - q, 4 * b + 4)
                if before:
                    store_logits(m)
                if next:
                    for kind, g in SHARES[2:]:
                        share(kind, g, 1 - q, 4 * b + 4)

            each(sp, body)
            load_h1(NB - 1)
            store_out(NB - 1)
            store_logits(NB - 1)
            wait(s_hst, 16 * (NB + 1))
            wait(s_xst, 16 * (NB + 1))
            wait(s_lst, 16 * (NB + 1))

        @block.gpsimd
        def _(pool):
            nc.gpsimd.memset(ident[:, :], 0.0).then_inc(s_id0, 1)
            pool.wait_ge(s_id0, 1)
            nc.gpsimd.affine_select(out=ident[:, :], in_=ident[:, :], compare_op=ALU.not_equal, fill=1.0,
                                    base=0, pattern=[[-1, P]], channel_multiplier=1).then_inc(s_idn, 1)

            def times_b(b, c, g):
                cc = 4 * b + c
                if g == 0 and c % 2 == 0:
                    pool.wait_ge(s_dtu[c // 2], b + 1)
                if c == 0:
                    pool.wait_ge(s_B[g], 16 * (b + 1))
                after(pool, s_ys[g], cc - 1)
                nc.gpsimd.tensor_tensor(hid[c % 2][g][:, :, :], dtu[:, c, :].unsqueeze(1).to_broadcast([P, GN, L]),
                                        b_all[:, g * GN:(g + 1) * GN, :], ALU.mult).then_inc(s_dbu[g], 1)

            def times_c(b, k):
                c, g = k // NG, k % NG
                if g not in POOL_C:
                    return
                if c == 0:
                    pool.wait_ge(s_C[g], 16 * (b + 1))
                pool.wait_ge(s_h[g], 4 * b + c + 1)
                nc.gpsimd.tensor_tensor(hid[c % 2][g][:, :, :], hid[c % 2][g][:, :, :],
                                        c_all[:, g * GN:(g + 1) * GN, :], ALU.mult).then_inc(s_hc[g], 1)

            def drive(n, q, half):
                pool.wait_ge(s_dt[half], n + 1)
                a, z = 2 * half, 2 * half + 2
                if half == 0:
                    pool.wait_ge(s_u, n + 1)
                nc.gpsimd.tensor_tensor(dtu[:, a:z, :], dt[q][:, a:z, :], u[:, a:z, :],
                                        ALU.mult).then_inc(s_dtu[half], 1)

            def body(b, q, before, next, after_next):
                for k in range(UNITS):
                    times_b(b, k // NG, k % NG)
                    if k >= POOL_LAG:
                        times_c(b, k - POOL_LAG)
                    elif before:
                        times_c(b - 1, UNITS + k - POOL_LAG)
                if next:
                    pool.wait_ge(s_dbu[3], 4 * b + 4)
                    drive(b + 1, 1 - q, 0)
                    drive(b + 1, 1 - q, 1)
                else:
                    for k in range(UNITS - POOL_LAG, UNITS):
                        times_c(b, k)

            drive(0, 0, 0)
            drive(0, 0, 1)
            each(pool, body)

        @block.scalar
        def _(act):
            def decays(b, q, c, g):
                cc = 4 * b + c
                if g == 0 and c % 2 == 0:
                    act.wait_ge(s_dt[c // 2], b + 1)
                after(act, s_h[(g + 2) % NG], cc + 1 if g >= 2 else cc)
                for j in range(GN):
                    last = nc.scalar.activation(decay[g % 2][:, j, 1:L], dt[q][:, c, 1:L], ACT.Exp,
                                                scale=a_neg[:, c, g * GN + j:g * GN + j + 1])
                last.then_inc(s_dec[g], 1)

            def copy_turned(n, ready, done):
                act.wait_ge(ready, n + 1)
                nc.scalar.activation(turned[:, :, :], psT[:, :, 0:L], ACT.Copy).then_inc(done, 1)

            def probs(n):
                act.wait_ge(s_nm, n + 1)
                after(act, s_dt[1], n)
                for s in range(NSEG):
                    last = nc.scalar.activation(prob[:, s, :], psW[:, 0, s * P:(s + 1) * P], ACT.Exp,
                                                bias=nmax[:, s:s + 1], scale=D ** -0.5,
                                                accum_out=rsum[:, s:s + 1])
                last.then_inc(s_E, 1)

            def copy_prob_t(n):
                act.wait_ge(s_ET, n + 1)
                nc.scalar.activation(soft[:, 1, :], psT[:, 0, 0:L], ACT.Copy).then_inc(s_ETc, 1)

            def first_rstd(n, j):
                act.wait_ge(s_mv[j], n + 1)
                nc.scalar.activation(lnv[j][:, :], mv[j][:, :, 1], ACT.Ln, bias=epsc[:, 0:1]).then_inc(s_lv[j], 1)
                act.wait_ge(s_lv[j], n + 1)
                nc.scalar.activation(rs0[j][:, :], lnv[j][:, :], ACT.Exp, scale=-0.5).then_inc(s_r0[j], 1)

            def copy_xin(n, half):
                act.wait_ge(s_xp[half], n + 1)
                src = (psW, psX)[half]
                nc.scalar.activation(xin[:, 2 * half:2 * half + 2, TAPS - 1:], src[:, :, 0:L],
                                     ACT.Copy).then_inc(s_xc[half], 1)

            def silus(n, q):
                act.wait_ge(s_cv, TAPS * (n + 1))
                nc.scalar.activation(u[:, :, :], u[:, :, :], ACT.Silu).then_inc(s_u, 1)
                for half, src in ((0, psT), (1, psW)):
                    act.wait_ge(s_zp[half], n + 1)
                    nc.scalar.activation(zs[q][:, 2 * half:2 * half + 2, :], src[:, :, 0:L],
                                         ACT.Silu).then_inc(s_zs[half], 1)

            def softplus(n, half):
                act.wait_ge(s_dp[half], n + 1)
                act.wait_ge(s_at, n + 1)
                src = (psT, psW)[half]
                a, z = 2 * half, 2 * half + 2
                for c in range(a, z):
                    last = nc.scalar.activation(xin[:, c, TAPS - 1:], src[:, c - a, 0:L], ACT.Identity,
                                                bias=b_dt[:, c:c + 1])
                last.then_inc(s_dx[half], 1)
                act.wait_ge(s_dx[half], n + 1)
                nc.scalar.activation(soft[:, a:z, :], xin[:, a:z, TAPS - 1:], ACT.Abs).then_inc(s_da[half], 1)
                act.wait_ge(s_da[half], n + 1)
                nc.scalar.activation(soft[:, a:z, :], soft[:, a:z, :], ACT.Exp, scale=-1.0).then_inc(s_de[half], 1)
                act.wait_ge(s_de[half], n + 1)
                nc.scalar.activation(soft[:, a:z, :], soft[:, a:z, :], ACT.Ln, bias=1.0).then_inc(s_dl[half], 1)

            def copy_logits(m):
                act.wait_ge(s_lg, m + 1)
                act.wait_ge(s_lst, 16 * (m + 1))
                nc.scalar.activation(logit[:, :, :], psW[:, 0, 0:NSEG * NE].rearrange("p (s e) -> p s e", s=NSEG),
                                     ACT.Copy).then_inc(s_lgc, 1)

            act.preload_act_table_set("natural_log_exp_and_others")
            act.wait_ge(s_w, 160)
            act.wait_ge(s_const, 1)
            nc.scalar.activation(a_neg[:, :, :], a_neg[:, :, :], ACT.Exp).then_inc(s_a0, 1)
            act.wait_ge(s_a0, 1)
            nc.scalar.activation(a_neg[:, :, :], a_neg[:, :, :], ACT.Copy, scale=-1.0).then_inc(s_a0, 1)
            copy_turned(0, s_qT, s_qTc)
            probs(0)
            copy_prob_t(0)
            first_rstd(0, 0)
            copy_turned(0, s_xT, s_xTc)
            copy_xin(0, 0)
            copy_xin(0, 1)
            silus(0, 0)
            act.preload_act_table_set("natural_log_exp_and_others")
            softplus(0, 0)
            softplus(0, 1)
            copy_turned(1, s_qT, s_qTc)
            act.wait_ge(s_a0, 2)

            def body(b, q, before, next, after_next):
                n, m, a, r = b + 1, b - 1, b + 2, 1 - q
                for k in range(UNITS):
                    decays(b, q, k // NG, k % NG)
                    if next:
                        if k == 0:
                            probs(n)
                        if k == 1:
                            copy_prob_t(n)
                        if k == 3:
                            first_rstd(n, 0)
                        if k == 5:
                            copy_turned(n, s_xT, s_xTc)
                        if k == 6:
                            copy_xin(n, 0)
                            copy_xin(n, 1)
                    if before and k == 6:
                        first_rstd(m, 1)
                    if next:
                        if k == 10:
                            silus(n, r)
                            act.preload_act_table_set("natural_log_exp_and_others")
                        if k == 11:
                            softplus(n, 0)
                        if k == 12:
                            softplus(n, 1)
                    if before:
                        if k == 13:
                            copy_turned(m, s_x2T, s_x2Tc)
                        if k == 14:
                            copy_logits(m)
                    if after_next and k == 14:
                        copy_turned(a, s_qT, s_qTc)

            each(act, body)
            first_rstd(NB - 1, 1)
            copy_turned(NB - 1, s_x2T, s_x2Tc)
            copy_logits(NB - 1)

        @block.vector
        def _(dve):
            for j in range(2):
                nc.vector.memset(decay[j][:, :, 0:1], 0.0)
            nc.vector.memset(xin[:, :, 0:TAPS - 1], 0.0)
            nc.vector.memset(epsc[:, :], EPS)
            nc.vector.memset(xs[:, NSEG - 1, :], 0.0).then_inc(s_const, 1)

            def scan(b, c, g):
                dve.wait_ge(s_dec[g], 4 * b + c + 1)
                dve.wait_ge(s_dbu[g], 4 * b + c + 1)
                flat = hid[c % 2][g][:, :, :].rearrange("p n l -> p (n l)")
                nc.vector.tensor_tensor_scan(flat, decay[g % 2][:, :, :].rearrange("p n l -> p (n l)"), flat,
                                             0.0, ALU.mult, ALU.add).then_inc(s_h[g], 1)

            def times_c(b, c, g):
                if g in POOL_C:
                    return
                if c == 0:
                    dve.wait_ge(s_C[g], 16 * (b + 1))
                dve.wait_ge(s_h[g], 4 * b + c + 1)
                nc.vector.tensor_tensor(hid[c % 2][g][:, :, :], hid[c % 2][g][:, :, :],
                                        c_all[:, g * GN:(g + 1) * GN, :], ALU.mult).then_inc(s_hc[g], 1)

            def gate(b, q, c):
                dve.wait_ge(s_ys[3], 4 * b + c + 1)
                if c == 0:
                    dve.wait_ge(s_zs[1], b + 1)
                    after(dve, s_op, b)
                nc.vector.tensor_tensor(yz[:, c, :], psY[c % 2][:, 0:L], zs[q][:, c, :],
                                        ALU.mult).then_inc(s_yz, 1)

            def row_max(n):
                dve.wait_ge(s_S, n + 1)
                nc.vector.tensor_reduce(rmax[:, :], psW[:, 0, 0:L].rearrange("p (s k) -> p s k", s=NSEG),
                                        AX.X, ALU.max).then_inc(s_rm, 1)
                dve.wait_ge(s_rm, n + 1)
                nc.vector.tensor_scalar(nmax[:, :], rmax[:, :], -(D ** -0.5), None, ALU.mult).then_inc(s_nm, 1)

            def stats(n, j, src):
                for s in range(NSEG):
                    last = nc.vector.bn_stats(stat[j][:, s, :], src[:, s, :])
                last.then_inc(s_st[j], 1)
                dve.wait_ge(s_st[j], n + 1)
                dve.sem_inc(s_turn, 1)
                for s in range(NSEG):
                    last = nc.vector.bn_aggr(mv[j][:, s, :], stat[j][:, s, :])
                last.then_inc(s_mv[j], 1)

            def norm(n, j, src):
                v, y, t = mv[j][:, :, 1], rs0[j][:, :], nw[j]
                dve.wait_ge(s_r0[j], n + 1)
                nc.vector.scalar_tensor_tensor(out=t[:, 0, :], in0=v, scalar=EPS, in1=y,
                                               op0=ALU.add, op1=ALU.mult).then_inc(s_nw[j], 1)
                dve.wait_ge(s_nw[j], 3 * n + 1)
                nc.vector.tensor_tensor(t[:, 1, :], t[:, 0, :], y, ALU.mult).then_inc(s_nw[j], 1)
                dve.wait_ge(s_nw[j], 3 * n + 2)
                nc.vector.tensor_scalar(t[:, 2, :], t[:, 1, :], -0.5, 1.5, ALU.mult, ALU.add).then_inc(s_nw[j], 1)
                dve.wait_ge(s_nw[j], 3 * n + 3)
                nc.vector.tensor_tensor(rstd[j][:, :], t[:, 2, :], y, ALU.mult).then_inc(s_rs[j], 1)
                dve.wait_ge(s_rs[j], n + 1)
                if j == 0:
                    dve.wait_ge(s_xst, 16 * (n - 1) if not isinstance(n, int) else 16 * max(n - 1, 1))
                else:
                    dve.wait_ge(s_xT, last_seq(n + 2))
                    dve.wait_ge(s_xst, 16 * (n + 1))
                for s in range(NSEG):
                    last = nc.vector.tensor_scalar(normed[:, s, :], src[:, s, :], mv[j][:, s, 0:1],
                                                   rstd[j][:, s:s + 1], ALU.subtract, ALU.mult)
                last.then_inc(s_xn[j], 1)

            def attended(n):
                dve.wait_ge(s_E, n + 1)
                nc.vector.reciprocal(rinv[:, :], rsum[:, :]).then_inc(s_ri, 1)
                dve.wait_ge(s_at, n + 1)
                dve.wait_ge(s_ri, n + 1)
                after(dve, s_h1st, 16 * n)
                for s in range(NSEG):
                    last = nc.vector.tensor_scalar(h1[:, s, :], psXf[:, s * D:(s + 1) * D],
                                                   rinv[:, s:s + 1], None, ALU.mult)
                last.then_inc(s_h1, 1)
                dve.wait_ge(s_h1, n + 1)
                stats(n, 0, h1)

            def add_block(m):
                dve.wait_ge(s_op, m + 1)
                dve.wait_ge(s_hb, 16 * (m + 1))
                h = h2[:, :, :].rearrange("p s d -> p (s d)")
                nc.vector.tensor_tensor(h, psXf[:, 0:NSEG * D], h, ALU.add).then_inc(s_h2, 1)
                dve.wait_ge(s_h2, m + 1)
                stats(m, 1, h2)

            def conv(n):
                dve.wait_ge(s_xc[0], n + 1)
                dve.wait_ge(s_xc[1], n + 1)
                after(dve, s_dtu[1], n)
                for k in range(TAPS):
                    for c in range(CH):
                        src = xin[:, c, k:k + L]
                        if k == 0:
                            last = nc.vector.tensor_scalar(u[:, c, :], src, w_cv[:, c, 0:1], b_cv[:, c:c + 1],
                                                           ALU.mult, ALU.add)
                        else:
                            last = nc.vector.scalar_tensor_tensor(out=u[:, c, :], in0=src,
                                                                  scalar=w_cv[:, c, k:k + 1], in1=u[:, c, :],
                                                                  op0=ALU.mult, op1=ALU.add)
                    last.then_inc(s_cv, 1)
                    if k < TAPS - 1:
                        dve.wait_ge(s_cv, TAPS * n + k + 1)

            def copy_bc(n):
                dve.wait_ge(s_bcp, n + 1)
                after(dve, s_bcw, 16 * n)
                nc.vector.tensor_copy(bc_rows[:, :], psX[0:2 * NS, 0, 0:L]).then_inc(s_bcc, 1)

            def finish_dt(n, q, half):
                a, z = 2 * half, 2 * half + 2
                dve.wait_ge(s_dl[half], n + 1)
                nc.vector.scalar_tensor_tensor(out=dt[q][:, a:z, :], in0=xin[:, a:z, TAPS - 1:], scalar=0.0,
                                               in1=soft[:, a:z, :], op0=ALU.max, op1=ALU.add).then_inc(s_dt[half], 1)

            dve.wait_ge(s_w, 160)
            row_max(0)
            attended(0)
            norm(0, 0, h1)
            conv(0)
            copy_bc(0)
            finish_dt(0, 0, 0)
            finish_dt(0, 0, 1)
            row_max(1)

            def body(b, q, before, next, after_next):
                n, m, a, r = b + 1, b - 1, b + 2, 1 - q
                for k in range(UNITS):
                    scan(b, k // NG, k % NG)
                    times_c(b, k // NG, k % NG)
                    if k in (5, 9, 13):
                        gate(b, q, k // NG - 1)
                    if before and k == 1:
                        gate(m, r, 3)
                    if next:
                        if k == 1:
                            attended(n)
                        if k == 2:
                            norm(n, 0, h1)
                    if before:
                        if k == 3:
                            add_block(m)
                        if k == 6:
                            norm(m, 1, h2)
                    if next:
                        if k == 7:
                            conv(n)
                        if k == 9:
                            copy_bc(n)
                        if k == 11:
                            finish_dt(n, r, 0)
                        if k == 12:
                            finish_dt(n, r, 1)
                    if after_next and k == 13:
                        row_max(a)

            each(dve, body)
            gate(NB - 1, (NB - 1) % 2, 3)
            add_block(NB - 1)
            norm(NB - 1, 1, h2)

        @block.tensor
        def _(pe):
            def turn_q(n):
                pe.wait_ge(s_x, 32 * (n + 1))
                for kd in range(KD):
                    for s in range(NSEG):
                        last = nc.tensor.transpose(psT[:, kd, s * P:(s + 1) * P],
                                                   xs[:, s, kd * P:(kd + 1) * P], ident[:, :])
                last.then_inc(s_qT, 1)

            def scores(n):
                pe.wait_ge(s_qTc, n + 1)
                for s in range(NSEG):
                    for kd in range(KD):
                        t = turned[:, kd, s * P:(s + 1) * P]
                        last = nc.tensor.matmul(psW[:, 0, s * P:(s + 1) * P], t, t, start=(kd == 0),
                                                stop=(kd == KD - 1))
                last.then_inc(s_S, 1)

            def turn_prob(n):
                pe.wait_ge(s_E, n + 1)
                for s in range(NSEG):
                    last = nc.tensor.transpose(psT[:, 0, s * P:(s + 1) * P], prob[:, s, :], ident[:, :])
                last.then_inc(s_ET, 1)

            def attend(n):
                pe.wait_ge(s_ETc, n + 1)
                after(pe, s_bcc, n)
                for s in range(NSEG):
                    last = nc.tensor.matmul(psXf[:, s * D:(s + 1) * D], prob_t[:, s, :], xs[:, s, :],
                                            start=True, stop=True)
                last.then_inc(s_at, 1)

            def turn_normed(n, j, done):
                pe.wait_ge(s_xn[j], n + 1)
                for kd in range(KD):
                    for s in range(NSEG):
                        last = nc.tensor.transpose(psT[:, kd, s * P:(s + 1) * P],
                                                   normed[:, s, kd * P:(kd + 1) * P], ident[:, :])
                last.then_inc(done, 1)

            def project(dst, lhs, cols, rhs, kk, done):
                for j, c in enumerate(cols):
                    for k in range(kk):
                        last = nc.tensor.matmul(dst[:, j, 0:L], lhs[:, k, c * P:(c + 1) * P], rhs[:, k, :],
                                                start=(k == 0), stop=(k == kk - 1))
                last.then_inc(done, 1)

            def project_xin(n):
                pe.wait_ge(s_xTc, n + 1)
                project(psW, w_in, (0, 1), turned, KD, s_xp[0])
                pe.wait_ge(s_h1, n + 1)
                after(pe, s_h2, n - 1)
                project(psX, w_in, (2, 3), turned, KD, s_xp[1])

            def project_z(n, half):
                if half == 0:
                    project(psT, w_in, (4, 5), turned, KD, s_zp[0])
                else:
                    pe.wait_ge(s_xc[0], n + 1)
                    project(psW, w_in, (6, 7), turned, KD, s_zp[1])

            def project_bc(n):
                pe.wait_ge(s_u, n + 1)
                pe.wait_ge(s_xc[1], n + 1)
                for k in range(CH):
                    last = nc.tensor.matmul(psX[0:2 * NS, 0, 0:L], w_bc[:, k, :], u[:, k, :],
                                            start=(k == 0), stop=(k == CH - 1))
                last.then_inc(s_bcp, 1)

            def project_dt(n, half):
                pe.wait_ge(s_zs[half], n + 1)
                project((psT, psW)[half], w_dt, (2 * half, 2 * half + 1), u, CH, s_dp[half])

            def project_out(m):
                pe.wait_ge(s_yz, CH * (m + 1))
                pe.wait_ge(s_h1, last_seq(m + 3))
                for s in range(NSEG):
                    for c in range(CH):
                        last = nc.tensor.matmul(psXf[:, s * D:(s + 1) * D], yz[:, c, s * P:(s + 1) * P],
                                                w_out[:, c, :], start=(c == 0), stop=(c == CH - 1))
                last.then_inc(s_op, 1)

            def route(m):
                pe.wait_ge(s_x2Tc, m + 1)
                pe.wait_ge(s_dx[1], last_seq(m + 3))
                for s in range(NSEG):
                    for kd in range(KD):
                        last = nc.tensor.matmul(psW[:, 0, s * NE:(s + 1) * NE], turned[:, kd, s * P:(s + 1) * P],
                                                w_gt[:, kd, :], start=(kd == 0), stop=(kd == KD - 1))
                last.then_inc(s_lg, 1)

            def sum_y(b, c, g):
                pe.wait_ge(s_hc[g], 4 * b + c + 1)
                if g == 0:
                    after(pe, s_yz, 4 * b + c - 1)
                for j in range(GN):
                    last = nc.tensor.matmul(psY[c % 2][:, 0:L], ident[:, :], hid[c % 2][g][:, j, :],
                                            start=(g == 0 and j == 0), stop=(g == NG - 1 and j == GN - 1))
                last.then_inc(s_ys[g], 1)

            pe.wait_ge(s_idn, 1)
            turn_q(0)
            scores(0)
            turn_prob(0)
            attend(0)
            turn_normed(0, 0, s_xT)
            pe.wait_ge(s_w, 160)
            project_xin(0)
            project_z(0, 0)
            project_z(0, 1)
            project_bc(0)
            project_dt(0, 0)
            project_dt(0, 1)
            pe.wait_ge(s_dx[0], 1)
            turn_q(1)
            pe.wait_ge(s_dx[1], 1)
            scores(1)
            turn_prob(1)
            attend(1)

            def body(b, q, before, next, after_next):
                n, m, a = b + 1, b - 1, b + 2
                for k in range(UNITS):
                    sum_y(b, k // NG, k % NG)
                    if before and k == 1:
                        project_out(m)
                    if next:
                        if k == 2:
                            turn_normed(n, 0, s_xT)
                        if k == 3:
                            project_xin(n)
                        if k == 4:
                            project_z(n, 0)
                        if k == 5:
                            project_z(n, 1)
                        if k == 8:
                            project_bc(n)
                            project_dt(n, 0)
                        if k == 9:
                            project_dt(n, 1)
                    if before:
                        if k == 10:
                            pe.wait_ge(s_dx[0], last_seq(m + 3))
                            turn_normed(m, 1, s_x2T)
                        if k == 11:
                            route(m)
                    if after_next:
                        if k == 11:
                            if before:
                                pe.wait_ge(s_x2Tc, m + 1)
                            else:
                                pe.wait_ge(s_dx[0], n + 1)
                            turn_q(a)
                        if k == 12:
                            if before:
                                pe.wait_ge(s_lgc, m + 1)
                            else:
                                pe.wait_ge(s_dx[1], n + 1)
                            scores(a)
                        if k == 14:
                            turn_prob(a)
                        if k == 15:
                            attend(a)

            each(pe, body)
            project_out(NB - 1)
            turn_normed(NB - 1, 1, s_x2T)
            route(NB - 1)


def router_phase(nc, w, lg_tab, x_tab, r_tab, inc_dram, NT):
    G = 8
    GE = NE // G
    TOPG = 4
    SCALE = 2.5
    FAR = -3.0e38
    TAKEN = -3.2e38
    NTG = NT * G
    RW = P + 1
    PT = 4
    with ExitStack() as ctx:
        def sb(name, shape, dt=F32):
            return ctx.enter_context(nc.sbuf_tensor(name, shape, dt))

        def sem(name):
            return ctx.enter_context(nc.semaphore(name))

        logits = sb("r_logits", [P, NT, NE])
        score = sb("r_score", [P, NT, NE])
        biased = sb("r_biased", [P, NT, NE])
        work = sb("r_work", [P, NT, NE])
        masked = logits
        small = sb("r_small", [P, 4, NTG, 2])
        gsum = sb("r_gsum", [P, NT, G])
        rank = sb("r_rank", [P, NT, G])
        top8 = sb("r_top8", [P, NT, 8])
        chosen = sb("r_chosen", [P, NT, NE], BF16)
        wsum = sb("r_wsum", [P, NT])
        winv = sb("r_winv", [P, NT])
        bias = sb("r_bias", [P, NE])
        tri = sb("r_tri", [P, P], BF16)
        ones = sb("r_ones", [NE, NT])
        incl = sb("r_incl", [NE, NT])
        counts = sb("r_counts", [NE, NT, RW])
        psR = [ctx.enter_context(nc.psum_tensor(f"r_psR{j}", [P, 512], F32)) for j in range(2)]

        s_ld, s_e, s_sc = sem("r_loaded"), sem("r_exped"), sem("r_scored")
        s_v = sem("r_vector_step")
        s_tri0, s_tri = sem("r_tri_ones"), sem("r_tri_set")
        s_ch, s_w, s_run, s_cc = sem("r_chosen_ready"), sem("r_weights_ready"), sem("r_running"), sem("r_copied")
        s_rt, s_out = sem("r_counts_ready"), sem("r_stored")
        block = ctx.enter_context(nc.Block())

        @block.sync
        def _(sp):
            sp.dma_start(logits[:, :, :].rearrange("p (b s) e -> p b (s e)", s=NSEG),
                         lg_tab.rearrange("b p s e -> p b (s e)")).then_inc(s_ld, 16)
            sp.dma_start(bias[:, :], w["gate_bias"].partition_broadcast(P)).then_inc(s_ld, 16)
            sp.wait_ge(s_w, 1)
            sp.dma_start(x_tab.rearrange("(t p) c -> p t c", p=P)[:, :, D:D + NE], work[:, :, :]).then_inc(s_out, 16)
            sp.wait_ge(s_rt, 1)
            sp.dma_start(r_tab.rearrange("(e t) c -> e t c", e=NE), counts[:, :, :]).then_inc(s_out, 16)
            sp.dma_start(inc_dram, incl[:, :]).then_inc(s_out, 16)
            sp.wait_ge(s_out, 48)

        @block.gpsimd
        def _(pool):
            nc.gpsimd.memset(tri[:, :], 1.0).then_inc(s_tri0, 1)
            pool.wait_ge(s_tri0, 1)
            nc.gpsimd.affine_select(out=tri[:, :], in_=tri[:, :], compare_op=ALU.is_ge, fill=0.0,
                                    base=0, pattern=[[1, P]], channel_multiplier=-1).then_inc(s_tri, 1)

        @block.scalar
        def _(act):
            act.wait_ge(s_ld, 32)
            nc.scalar.activation(logits[:, :, :], logits[:, :, :], ACT.Exp, scale=-1.0).then_inc(s_e, 1)
            for j in range(NT // PT):
                act.wait_ge(s_run, j + 1)
                nc.scalar.activation(counts[:, j * PT:(j + 1) * PT, 0:P],
                                     psR[j % 2][0:NE, :].rearrange("e (t k) -> e t k", t=PT),
                                     ACT.Copy).then_inc(s_cc, 1)

        @block.tensor
        def _(pe):
            pe.wait_ge(s_tri, 1)
            pe.wait_ge(s_ch, 1)
            for j in range(NT // PT):
                after(pe, s_cc, j - 1)
                for t in range(PT):
                    last = nc.tensor.matmul(psR[j % 2][0:NE, t * P:(t + 1) * P], chosen[:, j * PT + t, :],
                                            tri[:, :], start=True, stop=True)
                last.then_inc(s_run, 1)

        @block.vector
        def _(dve):
            steps = [0]

            def step(ins):
                steps[0] += 1
                ins.then_inc(s_v, 1)
                dve.wait_ge(s_v, steps[0])

            step(nc.vector.memset(ones[:, :], 1.0))
            dve.wait_ge(s_e, 1)
            step(nc.vector.tensor_scalar(logits[:, :, :], logits[:, :, :], 1.0, None, ALU.add))
            step(nc.vector.reciprocal(score[:, :, :], logits[:, :, :]))
            step(nc.vector.tensor_tensor(biased[:, :, :], score[:, :, :],
                                         bias[:, :].unsqueeze(1).to_broadcast([P, NT, NE]), ALU.add))
            grp = biased[:, :, :].rearrange("p t (g h k) -> p (t g) h k", g=G, h=2)
            w2 = work[:, :, :].rearrange("p t e -> p (t e)")
            hi = w2[:, 0:NTG * 4].rearrange("p (n k) -> p n k", k=4)
            lo = w2[:, NTG * 4:NTG * 8].rearrange("p (n k) -> p n k", k=4)
            nc.vector.tensor_tensor(hi, grp[:, :, 0, :], grp[:, :, 1, :], ALU.max)
            step(nc.vector.tensor_tensor(lo, grp[:, :, 0, :], grp[:, :, 1, :], ALU.min))
            hi2, mn, mx, lo2 = (small[:, j, :, :] for j in range(4))
            nc.vector.tensor_tensor(hi2, hi[:, :, 0:2], hi[:, :, 2:4], ALU.max)
            nc.vector.tensor_tensor(mn, hi[:, :, 0:2], hi[:, :, 2:4], ALU.min)
            step(nc.vector.tensor_tensor(mx, lo[:, :, 0:2], lo[:, :, 2:4], ALU.max))
            step(nc.vector.tensor_tensor(lo2, mn, mx, ALU.max))
            v = [w2[:, j * NTG:(j + 1) * NTG] for j in range(4)]
            nc.vector.tensor_tensor(v[0], hi2[:, :, 0], hi2[:, :, 1], ALU.max)
            nc.vector.tensor_tensor(v[1], hi2[:, :, 0], hi2[:, :, 1], ALU.min)
            step(nc.vector.tensor_tensor(v[2], lo2[:, :, 0], lo2[:, :, 1], ALU.max))
            step(nc.vector.tensor_tensor(v[3], v[1], v[2], ALU.max))
            gs = gsum[:, :, :]
            step(nc.vector.tensor_tensor(gs.rearrange("p t g -> p (t g)"), v[0], v[3], ALU.add))
            cmp = work[:, :, :].rearrange("p t (g j) -> p t g j", g=G)
            for g in range(G):
                own = gs[:, :, g:g + 1]
                if g:
                    nc.vector.tensor_tensor(cmp[:, :, g, 0:g], gs[:, :, 0:g], own.to_broadcast([P, NT, g]), ALU.is_ge)
                last = nc.vector.tensor_tensor(cmp[:, :, g, g:G], gs[:, :, g:G], own.to_broadcast([P, NT, G - g]),
                                               ALU.is_gt)
            step(last)
            rk = rank[:, :, :].rearrange("p t g -> p (t g)")
            step(nc.vector.tensor_reduce(rk, work[:, :, :].rearrange("p t (g j) -> p (t g) j", g=G), AX.X, ALU.add))
            step(nc.vector.tensor_scalar(rk, rk, float(TOPG), FAR, ALU.is_ge, ALU.mult))
            step(nc.vector.tensor_tensor(masked[:, :, :].rearrange("p t (g k) -> p (t g) k", g=G),
                                         biased[:, :, :].rearrange("p t (g k) -> p (t g) k", g=G),
                                         rk.unsqueeze(2).to_broadcast([P, NTG, GE]), ALU.add))
            for t in range(NT):
                last = nc.vector.max(top8[:, t, :], masked[:, t, :])
            step(last)
            for t in range(NT):
                last = nc.vector.match_replace(work[:, t, :], top8[:, t, :], masked[:, t, :], TAKEN)
            step(last)
            nc.vector.tensor_tensor(chosen[:, :, :], work[:, :, :], masked[:, :, :], ALU.not_equal).then_inc(s_ch, 1)
            dve.wait_ge(s_ch, 1)
            step(nc.vector.tensor_tensor(biased[:, :, :], score[:, :, :], chosen[:, :, :], ALU.mult))
            step(nc.vector.tensor_reduce(wsum[:, :], biased[:, :, :], AX.X, ALU.add))
            step(nc.vector.tensor_scalar(wsum[:, :], wsum[:, :], 1e-20, None, ALU.add))
            step(nc.vector.reciprocal(winv[:, :], wsum[:, :]))
            step(nc.vector.tensor_scalar(winv[:, :], winv[:, :], SCALE, None, ALU.mult))
            nc.vector.tensor_tensor(work[:, :, :], biased[:, :, :],
                                    winv[:, :].unsqueeze(2).to_broadcast([P, NT, NE]), ALU.mult).then_inc(s_w, 1)
            dve.wait_ge(s_cc, NT // PT)
            step(nc.vector.tensor_tensor_scan(incl[:, :], ones[:, :], counts[:, :, P - 1], 0.0, ALU.mult, ALU.add))
            nc.vector.tensor_tensor(counts[:, :, P], incl[:, :], counts[:, :, P - 1], ALU.subtract).then_inc(s_rt, 1)


def expert_phase(nc, w, x_tab, r_tab, inc_dram, h_out, NT):
    NTOK = NT * P
    CAP = 256
    NH = CAP // P
    NSL = NE * NH
    RW = P + 1
    XW = D + NE
    LB = 8
    EB = 4
    I = w["gate"].shape[2]
    assert I == P
    with ExitStack() as ctx:
        def sb(name, shape, dt=F32):
            return ctx.enter_context(nc.sbuf_tensor(name, shape, dt))

        def sem(name):
            return ctx.enter_context(nc.semaphore(name))

        ident = sb("e_ident", [P, P])
        zero = sb("e_zero", [P, NH, D])
        incl = sb("e_incl", [P, NE, NT])
        below = sb("e_below", [P, NE, NT])
        tile_of = sb("e_tile_of", [P, NE, NH])
        over = sb("e_over", [P, NE, NH])
        tile_in = sb("e_tile_in", [P, NE, NH])
        base_i = sb("e_base_i", [P, NE, NH], I32)
        base = sb("e_base", [P, NE, NH])
        slot_i = sb("e_slot_i", [P, NE, NH], I32)
        slot = sb("e_slot", [P, NE, NH])
        row = sb("e_row", [P, NSL], U32)
        row_st = [sb(f"e_row_st{q}", [P, LB], U32) for q in range(2)]
        rrow = [sb(f"e_rrow{q}", [P, LB, RW]) for q in range(2)]
        lslot = [sb(f"e_lslot{q}", [P, LB]) for q in range(2)]
        le = [sb(f"e_le{q}", [P, LB, P]) for q in range(2)]
        place = sb("e_place", [P, NSL])
        tok = sb("e_tok", [P, NSL])
        far = sb("e_far", [P, NSL])
        src = sb("e_src", [P, NSL], U32)
        dst = sb("e_dst", [P, NSL], U32)
        src_st = [sb(f"e_src_st{q}", [P, NH], U32) for q in range(EB)]
        dst_st = [sb(f"e_dst_st{q}", [P, NH], U32) for q in range(EB)]
        xg = [sb(f"e_xg{q}", [P, NH, XW]) for q in range(EB)]
        xt = [sb(f"e_xt{q}", [P, KD, CAP]) for q in range(2)]
        wg = [sb(f"e_wg{q}", [P, KD, I]) for q in range(EB)]
        wu = [sb(f"e_wu{q}", [P, KD, I]) for q in range(EB)]
        wd = [sb(f"e_wd{q}", [P, D]) for q in range(EB)]
        sg = [sb(f"e_sg{q}", [P, CAP]) for q in range(2)]
        at = [sb(f"e_at{q}", [P, CAP]) for q in range(2)]
        wcol = [sb(f"e_wcol{q}", [P, NH]) for q in range(2)]
        ys = [sb(f"e_ys{q}", [P, NH, D]) for q in range(2)]
        psG = [ctx.enter_context(nc.psum_tensor(f"e_psG{j}", [P, KD, CAP], F32)) for j in range(2)]
        psU = [ctx.enter_context(nc.psum_tensor(f"e_psU{j}", [P, 2, CAP], F32)) for j in range(2)]
        psO = [ctx.enter_context(nc.psum_tensor(f"e_psO{j}", [P, NH, D], F32)) for j in range(2)]

        s_c0, s_c = sem("e_ident_cleared"), sem("e_constants_set")
        s_z, s_zst, s_inc = sem("e_zeros_set"), sem("e_spare_rows_zeroed"), sem("e_incl_loaded")
        s_v = sem("e_vector_step")
        s_rowst = [sem(f"e_row_staged{q}") for q in range(2)]
        s_rr = [sem(f"e_rrow_gathered{q}") for q in range(2)]
        s_ls = [sem(f"e_lslot_ready{q}") for q in range(2)]
        s_le = [sem(f"e_le_ready{q}") for q in range(2)]
        s_pl = [sem(f"e_place_ready{q}") for q in range(2)]
        s_wt = [sem(f"e_weights_loaded{q}") for q in range(EB)]
        s_st = sem("e_indices_staged")
        s_xg = [sem(f"e_x_gathered{q}") for q in range(EB)]
        s_xT, s_xTc = sem("e_x_turned"), sem("e_x_turned_copied")
        s_gu, s_sg, s_at = sem("e_gate_up"), sem("e_silu"), sem("e_act_ready")
        s_yo, s_wc, s_ys = sem("e_down"), sem("e_wcol_ready"), sem("e_scaled")
        s_sc = sem("e_scattered")
        s_turn = sem("e_pool_turn")
        block = ctx.enter_context(nc.Block())

        @block.sync
        def _(sp):
            sp.wait_ge(s_z, 1)
            sp.dma_start(h_out[NTOK:NTOK + CAP, :].rearrange("(h p) d -> p h d", p=P), zero[:, :, :]).then_inc(s_zst, 16)
            sp.dma_start(incl[:, :, :].rearrange("p e t -> p (e t)"),
                         inc_dram.rearrange("e t -> (e t)").partition_broadcast(P)).then_inc(s_inc, 16)

            def load(e, q):
                sp.dma_start(wg[q][:, :, :], w["gate"][e].rearrange("(k p) i -> p k i", p=P)).then_inc(s_wt[q], 16)
                sp.dma_start(wu[q][:, :, :], w["up"][e].rearrange("(k p) i -> p k i", p=P)).then_inc(s_wt[q], 16)
                sp.dma_start(wd[q][:, :], w["down"][e]).then_inc(s_wt[q], 16)

            for q in range(EB):
                load(q, q)
            with sp.Fori(1, NE // EB) as i:
                for q in range(EB):
                    sp.wait_ge(s_yo, EB * i + q - EB + 1)
                    sp.sem_inc(s_turn, 1)
                    load(EB * i + q, q)
            sp.wait_ge(s_zst, 16)

        @block.gpsimd
        def _(pool):
            nc.gpsimd.memset(ident[:, :], 0.0).then_inc(s_c0, 1)
            pool.wait_ge(s_c0, 1)
            nc.gpsimd.affine_select(out=ident[:, :], in_=ident[:, :], compare_op=ALU.not_equal, fill=1.0,
                                    base=0, pattern=[[-1, P]], channel_multiplier=1).then_inc(s_c, 1)
            nc.gpsimd.iota(base_i[:, :, :], pattern=[[NT, NE], [0, NH]], base=0, channel_multiplier=0).then_inc(s_c, 1)
            nc.gpsimd.iota(slot_i[:, :, :], pattern=[[0, NE], [P, NH]], base=0, channel_multiplier=1).then_inc(s_c, 1)
            with pool.Fori(0, NSL // LB // 2) as i:
                for q in range(2):
                    pool.wait_ge(s_rowst[q], i + 1)
                    pool.sem_inc(s_turn, 1)
                    for j in range(LB):
                        nc.gpsimd.indirect_dma_start(
                            out=rrow[q][:, j, :], out_offset=None, in_=r_tab,
                            in_offset=bass.IndirectOffsetOnAxis(ap=row_st[q][:, j:j + 1], axis=0)).then_inc(s_rr[q], 16)

            def gather(e, q):
                pool.wait_ge(s_st, e + 1)
                pool.sem_inc(s_turn, 1)
                for h in range(NH):
                    nc.gpsimd.indirect_dma_start(
                        out=xg[q][:, h, :], out_offset=None, in_=x_tab,
                        in_offset=bass.IndirectOffsetOnAxis(ap=src_st[q][:, h:h + 1], axis=0)).then_inc(s_xg[q], 16)

            def scatter(e, q):
                pool.wait_ge(s_ys, e + 1)
                after(pool, s_sc, 16 * NH * e)
                pool.sem_inc(s_turn, 1)
                for h in range(NH):
                    nc.gpsimd.indirect_dma_start(
                        out=h_out, out_offset=bass.IndirectOffsetOnAxis(ap=dst_st[q][:, h:h + 1], axis=0),
                        in_=ys[q % 2][:, h, :], in_offset=None, compute_op=ALU.add).then_inc(s_sc, 16)

            pool.wait_ge(s_zst, 16)
            gather(0, 0)
            gather(1, 1)
            for e in range(EB):
                gather(e + 2, (e + 2) % EB)
                scatter(e, e)
            with pool.Fori(1, NE // EB - 1) as i:
                for q in range(EB):
                    gather(EB * i + q + 2, (q + 2) % EB)
                    scatter(EB * i + q, q)
            for q in range(EB):
                e = NE - EB + q
                if q + 2 < EB:
                    gather(e + 2, q + 2)
                scatter(e, q)
            pool.wait_ge(s_sc, 16 * NH * NE)

        @block.scalar
        def _(act):
            def expert(e, q):
                r = q % 2
                act.wait_ge(s_xT, e + 1)
                nc.scalar.activation(xt[r][:, :, :], psG[r][:, :, :], ACT.Copy).then_inc(s_xTc, 1)
                act.wait_ge(s_gu, e + 1)
                nc.scalar.activation(sg[r][:, :], psU[r][:, 0, :], ACT.Silu).then_inc(s_sg, 1)

            with act.Fori(0, NE // EB) as i:
                for q in range(EB):
                    expert(EB * i + q, q)

        @block.tensor
        def _(pe):
            pe.wait_ge(s_c, 3)

            def expert(i, e, q):
                r = q % 2
                pe.wait_ge(s_xg[q], 16 * NH * (i + 1))
                after(pe, s_xTc, e - 1)
                for h in range(NH):
                    for k in range(KD):
                        last = nc.tensor.transpose(psG[r][:, k, h * P:(h + 1) * P], xg[q][:, h, k * P:(k + 1) * P],
                                                   ident[:, :])
                last.then_inc(s_xT, 1)
                pe.wait_ge(s_wt[q], 48 * (i + 1))
                pe.wait_ge(s_xTc, e + 1)
                after(pe, s_at, e - 1)
                for j, m in enumerate((wg, wu)):
                    for k in range(KD):
                        last = nc.tensor.matmul(psU[r][:, j, :], m[q][:, k, :], xt[r][:, k, :],
                                                start=(k == 0), stop=(k == KD - 1))
                last.then_inc(s_gu, 1)
                pe.wait_ge(s_at, e + 1)
                after(pe, s_ys, e - 1)
                for h in range(NH):
                    last = nc.tensor.matmul(psO[r][:, h, :], at[r][:, h * P:(h + 1) * P], wd[q][:, :],
                                            start=True, stop=True)
                last.then_inc(s_yo, 1)

            for q in range(EB):
                expert(0, q, q)
            with pe.Fori(1, NE // EB) as i:
                for q in range(EB):
                    expert(i, EB * i + q, q)

        @block.vector
        def _(dve):
            steps = [0]

            def step(ins):
                steps[0] += 1
                ins.then_inc(s_v, 1)
                dve.wait_ge(s_v, steps[0])

            nc.vector.memset(zero[:, :, :], 0.0).then_inc(s_z, 1)
            dve.wait_ge(s_c, 3)
            nc.vector.tensor_copy(base[:, :, :], base_i[:, :, :])
            step(nc.vector.tensor_copy(slot[:, :, :], slot_i[:, :, :]))
            dve.wait_ge(s_inc, 16)
            for h in range(NH):
                step(nc.vector.tensor_scalar(below[:, :, :], incl[:, :, :], slot[:, 0, h:h + 1], None, ALU.is_le))
                step(nc.vector.tensor_reduce(tile_of[:, :, h], below[:, :, :], AX.X, ALU.add))
            nc.vector.tensor_scalar(over[:, :, :], tile_of[:, :, :], float(NT), None, ALU.is_ge)
            step(nc.vector.tensor_scalar(tile_in[:, :, :], tile_of[:, :, :], float(NT - 1), None, ALU.min))
            flat = lambda t: t[:, :, :].rearrange("p e h -> p (e h)")
            step(nc.vector.tensor_tensor(row[:, :], flat(tile_in), flat(base), ALU.add))

            def stage_rows(j, q):
                nc.vector.tensor_copy(row_st[q][:, :], row[:, bass.ds(j * LB, LB)]).then_inc(s_rowst[q], 1)

            def locate(i, j, q):
                dve.wait_ge(s_rr[q], 16 * LB * (i + 1))
                nc.vector.tensor_tensor(lslot[q][:, :], flat(slot)[:, bass.ds(j * LB, LB)], rrow[q][:, :, P],
                                        ALU.subtract).then_inc(s_ls[q], 1)
                dve.wait_ge(s_ls[q], i + 1)
                nc.vector.tensor_tensor(le[q][:, :, :], rrow[q][:, :, 0:P],
                                        lslot[q][:, :].unsqueeze(2).to_broadcast([P, LB, P]),
                                        ALU.is_le).then_inc(s_le[q], 1)
                dve.wait_ge(s_le[q], i + 1)
                nc.vector.tensor_reduce(place[:, bass.ds(j * LB, LB)], le[q][:, :, :], AX.X,
                                        ALU.add).then_inc(s_pl[q], 1)

            NL = NSL // LB // 2
            stage_rows(0, 0)
            stage_rows(1, 1)
            with dve.Fori(0, NL - 1) as i:
                for q in range(2):
                    locate(i, 2 * i + q, q)
                    stage_rows(2 * i + q + 2, q)
            for q in range(2):
                locate(NL - 1, 2 * (NL - 1) + q, q)
            dve.wait_ge(s_pl[0], NL)
            dve.wait_ge(s_pl[1], NL)
            step(nc.vector.scalar_tensor_tensor(out=tok[:, :], in0=flat(tile_in), scalar=float(P), in1=place[:, :],
                                                op0=ALU.mult, op1=ALU.add))
            nc.vector.tensor_scalar(src[:, :], tok[:, :], float(NTOK - 1), None, ALU.min)
            step(nc.vector.scalar_tensor_tensor(out=far[:, :], in0=flat(slot), scalar=float(NTOK), in1=tok[:, :],
                                                op0=ALU.add, op1=ALU.subtract))
            step(nc.vector.tensor_tensor(far[:, :], far[:, :], flat(over), ALU.mult))
            step(nc.vector.tensor_tensor(dst[:, :], far[:, :], tok[:, :], ALU.add))

            def stage(e, q):
                nc.vector.tensor_copy(src_st[q][:, :], src[:, bass.ds(e * NH, NH)])
                nc.vector.tensor_copy(dst_st[q][:, :], dst[:, bass.ds(e * NH, NH)]).then_inc(s_st, 1)

            def expert(i, e, q):
                r = q % 2
                dve.wait_ge(s_sg, e + 1)
                nc.vector.tensor_tensor(at[r][:, :], sg[r][:, :], psU[r][:, 1, :], ALU.mult).then_inc(s_at, 1)
                nc.vector.tensor_copy(wcol[r][:, :], xg[q][:, :, bass.ds(D + e, 1)].rearrange("p h o -> p (h o)")
                                      ).then_inc(s_wc, 1)
                dve.wait_ge(s_yo, e + 1)
                dve.wait_ge(s_wc, e + 1)
                after(dve, s_sc, 16 * NH * (e - 1))
                for h in range(NH):
                    last = nc.vector.tensor_scalar(ys[r][:, h, :], psO[r][:, h, :], wcol[r][:, h:h + 1], None,
                                                   ALU.mult)
                last.then_inc(s_ys, 1)

            for q in range(EB):
                stage(q, q)
            for q in range(EB):
                expert(0, q, q)
                dve.wait_ge(s_sc, 16 * NH * (q + 1))
                stage(q + EB, q)
            with dve.Fori(1, NE // EB - 1) as i:
                for q in range(EB):
                    expert(i, EB * i + q, q)
                    dve.wait_ge(s_sc, 16 * NH * (EB * i + q + 1))
                    stage(EB * i + q + EB, q)
            for q in range(EB):
                expert(NE // EB - 1, NE - EB + q, q)


def audio_tower_kernel(nc, x, w, out):
    NT = x.shape[0] * NSEG
    bc_dram = nc.dram_tensor("bc_rows_dram", (2, 2 * NS, L), F32, kind="Internal").ap()
    lg_tab = nc.dram_tensor("logits_dram", (x.shape[0], P, NSEG, NE), F32, kind="Internal").ap()
    x_tab = nc.dram_tensor("x2_weights_dram", (NT * P, D + NE), F32, kind="Internal").ap()
    r_tab = nc.dram_tensor("running_dram", (NE * NT, P + 1), F32, kind="Internal").ap()
    inc_dram = nc.dram_tensor("incl_dram", (NE, NT), F32, kind="Internal").ap()
    sequence_phase(nc, x, w, bc_dram, out, x_tab, lg_tab)
    router_phase(nc, w, lg_tab, x_tab, r_tab, inc_dram, NT)
    expert_phase(nc, w, x_tab, r_tab, inc_dram, out, NT)


def kernel(**inputs):
    import numpy as np
    import concourse.bacc as bacc
    from concourse.bass_utils import run_bass_kernel_spmd

    def as_is(name):
        return np.ascontiguousarray(inputs[name])

    def turned(name):
        return np.ascontiguousarray(np.asarray(inputs[name]).T)

    def by_chunk(name):
        return np.ascontiguousarray(np.asarray(inputs[name]).reshape(CH, P).T)

    host = {
        "x": as_is("x"),
        "in_t": turned("L0_attn_W_in"),
        "conv": as_is("L0_attn_W_conv").reshape(DI, TAPS),
        "b_conv": by_chunk("L0_attn_b_conv"),
        "dt_t": turned("L0_attn_W_dt"),
        "b_dt": by_chunk("L0_attn_b_dt"),
        "b_t": turned("L0_attn_W_B"),
        "c_t": turned("L0_attn_W_C"),
        "a_log": as_is("L0_attn_A_log"),
        "out_t": turned("L0_attn_W_out"),
        "gate_t": turned("L0_ffn_gate_w"),
        "gate_bias": as_is("L0_ffn_gate_bias"),
        "gate": as_is("L0_ffn_w_gate"),
        "up": as_is("L0_ffn_w_up"),
        "down": as_is("L0_ffn_w_down"),
    }
    nc = bacc.Bacc("TRN2", target_bir_lowering=False, num_devices=1)
    w = {k: nc.dram_tensor(f"in_{k}_dram", v.shape, F32, kind="ExternalInput").ap() for k, v in host.items()}
    NB = host["x"].shape[0]
    SPARE = 256
    out = nc.dram_tensor("out_dram", (NB * L + SPARE, D), F32, kind="ExternalOutput").ap()
    audio_tower_kernel(nc, w["x"], w, out)
    r = run_bass_kernel_spmd(nc, [{f"in_{k}_dram": v for k, v in host.items()}], core_ids=[0])
    return r.results[0]["out_dram"][:NB * L].reshape(NB, L, D)
```

```python
from contextlib import ExitStack

import concourse.bass as bass
from concourse import mybir

F32 = mybir.dt.float32
BF16 = mybir.dt.bfloat16
U32 = mybir.dt.uint32
I32 = mybir.dt.int32
ALU = mybir.AluOpType
ACT = mybir.ActivationFunctionType
AX = mybir.AxisListType

P = 128
D = 256
SEG = 256
DIL = 2
NSEG = 3
L = NSEG * P
DI = 512
CH = DI // P
KD = D // P
NS = 16
GN = 4
NG = NS // GN
TAPS = 4
NE = 64
EPS = 1e-5
G = 8
GE = NE // G
SLOTS = 256
TOPG = 4
TOPK = 8
SCALE = 2.5
FAR = -3.0e38
TAKEN = -3.2e38
ABSENT = 3.2e38
ROUTE_STEPS = 15
UNITS = CH * NG
POOL_C = (3,)
K_CONV = (6, 7, 8)
K_DT = (11, 12)
K_ROUTE = (9, 11, 12)
K_MAX = 14
POOL_LAG = 2


def after(eng, sem, count):
    if isinstance(count, int) and count <= 0:
        return
    eng.wait_ge(sem, count)


def sequence_phase(nc, x, w, bc_dram, h_out, x_tab, ch_tab):
    NB, S, _ = x.shape
    TAIL = (S - (NSEG - 1) * SEG + DIL - 1) // DIL

    with ExitStack() as ctx:
        def sb(name, shape, dt=F32):
            return ctx.enter_context(nc.sbuf_tensor(name, shape, dt))

        def ps(name, shape):
            return ctx.enter_context(nc.psum_tensor(name, shape, F32))

        def sem(name):
            return ctx.enter_context(nc.semaphore(name))

        w_in = sb("w_in", [P, KD, 2 * DI])
        w_dt = sb("w_dt", [P, CH, DI])
        w_bc = sb("w_bc", [P, CH, 2 * NS])
        w_out = sb("w_out", [P, CH, D])
        w_gt = sb("w_gt", [P, KD, NE])
        w_cv = sb("w_cv", [P, CH, TAPS])
        b_cv = sb("b_cv", [P, CH])
        b_dt = sb("b_dt", [P, CH])
        a_neg = sb("a_neg", [P, CH, NS])
        ident = sb("ident", [P, P])
        xs = sb("xs", [P, NSEG, D])
        h1 = sb("h1", [P, NSEG, D])
        h2 = sb("h2", [P, NSEG, D])
        dt = [sb(f"dt{q}", [P, CH, L]) for q in range(2)]
        zs = [sb(f"zs{q}", [P, CH, L]) for q in range(2)]
        turned = sb("turned", [P, KD, L])
        normed = sb("normed", [P, NSEG, D])
        xin = sb("xin", [P, CH, TAPS - 1 + L])
        u = sb("u", [P, CH, L])
        soft = sb("soft", [P, CH, L])
        prob = soft[:, 0, :].rearrange("p (s k) -> p s k", s=NSEG)
        prob_t = soft[:, 1, :].rearrange("p (s k) -> p s k", s=NSEG)
        dtu = sb("dtu", [P, CH, L])
        bc_rows = sb("bc_rows", [2 * NS, L])
        b_all = sb("b_all", [P, NS, L])
        c_all = sb("c_all", [P, NS, L])
        yz = sb("yz", [P, CH, L])
        bias = sb("bias", [P, NE])
        denom = sb("denom", [P, NSEG, NE])
        score = sb("score", [P, NSEG, NE])
        biased = sb("biased", [P, NSEG, NE])
        masked = sb("masked", [P, NSEG, NE])
        left = denom
        halves = denom[:, :, :].rearrange("p s e -> p (s e)").rearrange("p (j n k) -> p j n k", j=2, k=GE // 2)
        quarters = masked[:, :, :].rearrange("p s e -> p (s e)").rearrange("p (j n k) -> p j n k", j=4, k=GE // 4)
        best = sb("best", [P, 4, NSEG * G])
        gsum = sb("gsum", [P, NSEG, G])
        gtop = sb("gtop", [P, NSEG, G])
        gleft = sb("gleft", [P, NSEG, G])
        top8 = sb("top8", [P, NSEG, TOPK])
        wsum = sb("wsum", [P, NSEG])
        winv = sb("winv", [P, NSEG])
        weight = sb("weight", [P, NSEG, NE])
        chosen = sb("chosen", [P, NSEG, NE], BF16)
        decay = [sb(f"decay{j}", [P, GN, L]) for j in range(2)]
        hid = [[sb(f"hid{j}{g}", [P, GN, L]) for g in range(NG)] for j in range(2)]
        rmax = sb("rmax", [P, NSEG])
        nmax = sb("nmax", [P, NSEG])
        rsum = sb("rsum", [P, NSEG])
        rinv = sb("rinv", [P, NSEG])
        stat = [sb(f"stat{j}", [P, NSEG, 6]) for j in range(2)]
        mv = [sb(f"mv{j}", [P, NSEG, 2]) for j in range(2)]
        lnv = [sb(f"lnv{j}", [P, NSEG]) for j in range(2)]
        rs0 = [sb(f"rs0{j}", [P, NSEG]) for j in range(2)]
        nw = [sb(f"nw{j}", [P, 3, NSEG]) for j in range(2)]
        rstd = [sb(f"rstd{j}", [P, NSEG]) for j in range(2)]
        epsc = sb("epsc", [P, 1])

        psY = [ps(f"psY{j}", [P, 512]) for j in range(2)]
        psT = ps("psT", [P, 2, 512])
        psW = ps("psW", [P, 2, 512])
        psX = ps("psX", [P, 2, 512])
        psXf = psX[:, :, :].rearrange("p a b -> p (a b)")

        s_turn = sem("wait_carrier")
        s_w = sem("weights_loaded")
        s_a0 = sem("a_log_exped")
        s_const = sem("constants_set")
        s_id0 = sem("ident_cleared")
        s_idn = sem("ident_set")
        s_x = sem("x_loaded")
        s_h1st, s_hb = sem("h1_stored"), sem("h1_back")
        s_bcw = sem("bc_rows_stored")
        s_B = [sem(f"b_loaded{g}") for g in range(NG)]
        s_C = [sem(f"c_loaded{g}") for g in range(NG)]
        s_hst = sem("h_stored")
        s_xst = sem("x2_stored")
        s_wst = sem("weights_stored")
        s_cst = sem("chosen_stored")
        s_dec = [sem(f"decay_ready{g}") for g in range(NG)]
        s_dbu = [sem(f"dbu_ready{g}") for g in range(NG)]
        s_h = [sem(f"scan_done{g}") for g in range(NG)]
        s_hc = [sem(f"hc_ready{g}") for g in range(NG)]
        s_ys = [sem(f"y_summed{g}") for g in range(NG)]
        s_yz = sem("y_gated")
        s_qT, s_qTc = sem("q_turned"), sem("q_turned_copied")
        s_S, s_rm, s_nm, s_E = sem("scores_ready"), sem("row_max"), sem("neg_max"), sem("prob_ready")
        s_ET, s_ETc = sem("prob_turned"), sem("prob_turned_copied")
        s_at, s_ri, s_h1 = sem("attended"), sem("sums_inverted"), sem("h1_ready")
        s_st = [sem(f"stats{j}") for j in range(2)]
        s_mv = [sem(f"mean_var{j}") for j in range(2)]
        s_lv = [sem(f"log_var{j}") for j in range(2)]
        s_r0 = [sem(f"rstd_first{j}") for j in range(2)]
        s_nw = [sem(f"newton{j}") for j in range(2)]
        s_rs = [sem(f"rstd_ready{j}") for j in range(2)]
        s_xn = [sem(f"normed{j}") for j in range(2)]
        s_xT, s_xTc = sem("xn_turned"), sem("xn_turned_copied")
        s_x2T, s_x2Tc = sem("x2_turned"), sem("x2_turned_copied")
        s_xp = [sem(f"xin_product{j}") for j in range(2)]
        s_xc = [sem(f"xin_copied{j}") for j in range(2)]
        s_cv = sem("conv_tap")
        s_zp = [sem(f"z_product{j}") for j in range(2)]
        s_zs = [sem(f"z_silu{j}") for j in range(2)]
        s_u = sem("u_ready")
        s_dp = [sem(f"dt_product{j}") for j in range(2)]
        s_dx = [sem(f"dt_biased{j}") for j in range(2)]
        s_da = [sem(f"dt_abs{j}") for j in range(2)]
        s_de = [sem(f"dt_exp{j}") for j in range(2)]
        s_dl = [sem(f"dt_log{j}") for j in range(2)]
        s_dt = [sem(f"dt_ready{j}") for j in range(2)]
        s_dtu = [sem(f"dtu_ready{j}") for j in range(2)]
        s_bcp, s_bcc = sem("bc_product"), sem("bc_rows_ready")
        s_op, s_h2 = sem("out_product"), sem("h2_ready")
        s_lg, s_lge = sem("logit_product"), sem("logit_exped")
        s_rt = sem("routing_step")
        s_wg = sem("weighing_step")
        s_wgt, s_ch = sem("expert_weights_ready"), sem("chosen_ready")

        def last_seq(count):
            return min(count, NB) if isinstance(count, int) else count

        def pool_groups(b):
            return POOL_C if not isinstance(b, int) or b < NB - 1 else ()

        def each(eng, body):
            def one(b, q):
                fixed = isinstance(b, int)
                body(b, q, before=not fixed or b >= 1, routed=not fixed or b >= 2,
                     next=not fixed or b < NB - 1, after_next=not fixed or b < NB - 2)

            one(0, 0)
            one(1, 1)
            if NB > 6:
                with eng.Fori(0, (NB - 6) // 2) as i:
                    one(2 * i + 2, 0)
                    one(2 * i + 3, 1)
            for b in range(max(NB - 4, 2), NB):
                one(b, b % 2)

        block = ctx.enter_context(nc.Block())

        @block.sync
        def _(sp):
            def wait(sem, count):
                after(sp, sem, count)
                if not isinstance(count, int):
                    sp.sem_inc(s_turn, 1)

            def load_x(n):
                sp.dma_start(xs[:, 0:NSEG - 1, :],
                             x[n, 0:(NSEG - 1) * SEG, :].rearrange("(s p j) d -> j p s d", s=NSEG - 1, j=DIL)[0]
                             ).then_inc(s_x, 16)
                sp.dma_start(xs[0:TAIL, NSEG - 1, :],
                             x[n, (NSEG - 1) * SEG:S, :].rearrange("(p j) d -> j p d", j=DIL)[0]
                             ).then_inc(s_x, 16)

            def rows(tab, n):
                return tab[bass.ds(n * L, L), 0:D].rearrange("(s p) d -> p s d", p=P)

            def store_h1(n):
                wait(s_h1, n + 1)
                sp.dma_start(rows(h_out, n), h1[:, :, :]).then_inc(s_h1st, 16)

            def load_h1(m):
                wait(s_h1st, 16 * (m + 1))
                wait(s_hst, 16 * (m + 1))
                sp.dma_start(h2[:, :, :], rows(h_out, m)).then_inc(s_hb, 16)

            def store_out(m):
                wait(s_h2, m + 1)
                sp.dma_start(rows(h_out, m), h2[:, :, :]).then_inc(s_hst, 16)
                wait(s_xn[1], m + 1)
                sp.dma_start(rows(x_tab, m), normed[:, :, :]).then_inc(s_xst, 16)

            def store_routes(m):
                wait(s_ch, m + 1)
                sp.dma_start(ch_tab[m], chosen[:, :, :]).then_inc(s_cst, 16)
                wait(s_wgt, m + 1)
                sp.dma_start(x_tab[bass.ds(m * L, L), D:D + NE].rearrange("(s p) e -> p s e", p=P),
                             weight[:, :, :]).then_inc(s_wst, 16)

            def store_bc(n, q):
                wait(s_bcc, n + 1)
                sp.dma_start(bc_dram[q], bc_rows[:, :]).then_inc(s_bcw, 16)
                wait(s_bcw, 16 * (n + 1))

            def share(kind, g, q, own):
                to, done, used, at = ((b_all, s_B, s_dbu, 0) if kind == "b" else (c_all, s_C, s_hc, NS))
                wait(used[g], own)
                src = bc_dram[q, at + g * GN:at + (g + 1) * GN, :].rearrange("n l -> (n l)")
                sp.dma_start(to[:, g * GN:(g + 1) * GN, :].rearrange("p n l -> p (n l)"),
                             src.partition_broadcast(P)).then_inc(done[g], 16)

            SHARES = (("b", 0), ("b", 1), ("b", 2), ("c", 0), ("b", 3), ("c", 1), ("c", 2), ("c", 3))

            wait(s_const, 1)
            load_x(0)
            sp.dma_start(w_in[:, :, :], w["in_t"].rearrange("(k p) n -> p k n", p=P)).then_inc(s_w, 16)
            sp.dma_start(w_dt[:, :, :], w["dt_t"].rearrange("(c p) n -> p c n", p=P)).then_inc(s_w, 16)
            sp.dma_start(w_bc[:, :, 0:NS], w["b_t"].rearrange("(c p) n -> p c n", p=P)).then_inc(s_w, 16)
            sp.dma_start(w_bc[:, :, NS:2 * NS], w["c_t"].rearrange("(c p) n -> p c n", p=P)).then_inc(s_w, 16)
            sp.dma_start(w_out[:, :, :], w["out_t"].rearrange("(c p) n -> p c n", p=P)).then_inc(s_w, 16)
            sp.dma_start(w_gt[:, :, :], w["gate_t"].rearrange("(k p) n -> p k n", p=P)).then_inc(s_w, 16)
            sp.dma_start(w_cv[:, :, :], w["conv"].rearrange("(c p) n -> p c n", p=P)).then_inc(s_w, 16)
            sp.dma_start(b_cv[:, :], w["b_conv"]).then_inc(s_w, 16)
            sp.dma_start(b_dt[:, :], w["b_dt"]).then_inc(s_w, 16)
            sp.dma_start(a_neg[:, :, :], w["a_log"].rearrange("(c p) n -> p c n", p=P)).then_inc(s_w, 16)
            sp.dma_start(bias[:, :], w["gate_bias"].partition_broadcast(P)).then_inc(s_w, 16)
            for done in (s_hst, s_xst, s_wst, s_cst):
                sp.sem_inc(done, 16)
            wait(s_at, 1)
            load_x(1)
            store_h1(0)
            store_bc(0, 0)
            for kind, g in SHARES:
                share(kind, g, 0, 0)

            def body(b, q, before, routed, next, after_next):
                n, m = b + 1, b - 1
                if after_next:
                    wait(s_at, n + 1)
                    load_x(b + 2)
                if next:
                    store_h1(n)
                if before:
                    load_h1(m)
                    store_out(m)
                if next:
                    store_bc(n, 1 - q)
                    for kind, g in SHARES[:2]:
                        share(kind, g, 1 - q, 4 * b + 4)
                if next:
                    for kind, g in SHARES[2:]:
                        share(kind, g, 1 - q, 4 * b + 4)
                if routed:
                    store_routes(b - 2)

            each(sp, body)
            load_h1(NB - 1)
            store_out(NB - 1)
            store_routes(NB - 2)
            store_routes(NB - 1)
            wait(s_hst, 16 * (NB + 1))
            wait(s_xst, 16 * (NB + 1))
            wait(s_wst, 16 * (NB + 1))
            wait(s_cst, 16 * (NB + 1))

        @block.gpsimd
        def _(pool):
            nc.gpsimd.memset(ident[:, :], 0.0).then_inc(s_id0, 1)
            pool.wait_ge(s_id0, 1)
            nc.gpsimd.affine_select(out=ident[:, :], in_=ident[:, :], compare_op=ALU.not_equal, fill=1.0,
                                    base=0, pattern=[[-1, P]], channel_multiplier=1).then_inc(s_idn, 1)

            def times_b(b, c, g):
                cc = 4 * b + c
                if g == 0 and c % 2 == 0:
                    pool.wait_ge(s_dtu[c // 2], b + 1)
                if c == 0:
                    pool.wait_ge(s_B[g], 16 * (b + 1))
                after(pool, s_ys[g], cc - 1)
                nc.gpsimd.tensor_tensor(hid[c % 2][g][:, :, :], dtu[:, c, :].unsqueeze(1).to_broadcast([P, GN, L]),
                                        b_all[:, g * GN:(g + 1) * GN, :], ALU.mult).then_inc(s_dbu[g], 1)

            def times_c(b, k):
                c, g = k // NG, k % NG
                if g not in pool_groups(b):
                    return
                if c == 0:
                    pool.wait_ge(s_C[g], 16 * (b + 1))
                pool.wait_ge(s_h[g], 4 * b + c + 1)
                nc.gpsimd.tensor_tensor(hid[c % 2][g][:, :, :], hid[c % 2][g][:, :, :],
                                        c_all[:, g * GN:(g + 1) * GN, :], ALU.mult).then_inc(s_hc[g], 1)

            def drive(n, q, half):
                pool.wait_ge(s_dt[half], n + 1)
                a, z = 2 * half, 2 * half + 2
                if half == 0:
                    pool.wait_ge(s_u, n + 1)
                nc.gpsimd.tensor_tensor(dtu[:, a:z, :], dt[q][:, a:z, :], u[:, a:z, :],
                                        ALU.mult).then_inc(s_dtu[half], 1)

            def body(b, q, before, routed, next, after_next):
                for k in range(UNITS):
                    times_b(b, k // NG, k % NG)
                    if k >= POOL_LAG:
                        times_c(b, k - POOL_LAG)
                    elif before:
                        times_c(b - 1, UNITS + k - POOL_LAG)
                if next:
                    pool.wait_ge(s_dbu[3], 4 * b + 4)
                    drive(b + 1, 1 - q, 0)
                    drive(b + 1, 1 - q, 1)
                else:
                    for k in range(UNITS - POOL_LAG, UNITS):
                        times_c(b, k)

            drive(0, 0, 0)
            drive(0, 0, 1)
            each(pool, body)

        @block.scalar
        def _(act):
            def decays(b, q, c, g):
                cc = 4 * b + c
                if g == 0 and c % 2 == 0:
                    act.wait_ge(s_dt[c // 2], b + 1)
                after(act, s_h[(g + 2) % NG], cc + 1 if g >= 2 else cc)
                for j in range(GN):
                    last = nc.scalar.activation(decay[g % 2][:, j, 1:L], dt[q][:, c, 1:L], ACT.Exp,
                                                scale=a_neg[:, c, g * GN + j:g * GN + j + 1])
                last.then_inc(s_dec[g], 1)

            def copy_turned(n, ready, done):
                act.wait_ge(ready, n + 1)
                nc.scalar.activation(turned[:, :, :], psT[:, :, 0:L], ACT.Copy).then_inc(done, 1)

            def probs(n):
                act.wait_ge(s_nm, n + 1)
                after(act, s_dt[1], n)
                for s in range(NSEG):
                    last = nc.scalar.activation(prob[:, s, :], psW[:, 0, s * P:(s + 1) * P], ACT.Exp,
                                                bias=nmax[:, s:s + 1], scale=D ** -0.5,
                                                accum_out=rsum[:, s:s + 1])
                last.then_inc(s_E, 1)

            def copy_prob_t(n):
                act.wait_ge(s_ET, n + 1)
                nc.scalar.activation(soft[:, 1, :], psT[:, 0, 0:L], ACT.Copy).then_inc(s_ETc, 1)

            def first_rstd(n, j):
                act.wait_ge(s_mv[j], n + 1)
                nc.scalar.activation(lnv[j][:, :], mv[j][:, :, 1], ACT.Ln, bias=epsc[:, 0:1]).then_inc(s_lv[j], 1)
                act.wait_ge(s_lv[j], n + 1)
                nc.scalar.activation(rs0[j][:, :], lnv[j][:, :], ACT.Exp, scale=-0.5).then_inc(s_r0[j], 1)

            def copy_xin(n, half):
                act.wait_ge(s_xp[half], n + 1)
                src = (psW, psX)[half]
                if half == 0:
                    after(act, s_dtu[1], n)
                for c in range(2 * half, 2 * half + 2):
                    nc.scalar.activation(u[:, c, :], src[:, c - 2 * half, 0:L], ACT.Identity,
                                         scale=w_cv[:, c, TAPS - 1:TAPS], bias=b_cv[:, c:c + 1])
                nc.scalar.activation(xin[:, 2 * half:2 * half + 2, TAPS - 1:], src[:, :, 0:L],
                                     ACT.Copy).then_inc(s_xc[half], 1)

            def copy_bc(n):
                act.wait_ge(s_bcp, n + 1)
                after(act, s_bcw, 16 * n)
                nc.scalar.activation(bc_rows[:, :], psX[0:2 * NS, 0, 0:L], ACT.Copy).then_inc(s_bcc, 1)

            def silus(n, q):
                act.wait_ge(s_cv, (TAPS - 1) * (n + 1))
                nc.scalar.activation(u[:, :, :], u[:, :, :], ACT.Silu).then_inc(s_u, 1)
                for half, src in ((0, psT), (1, psW)):
                    act.wait_ge(s_zp[half], n + 1)
                    nc.scalar.activation(zs[q][:, 2 * half:2 * half + 2, :], src[:, :, 0:L],
                                         ACT.Silu).then_inc(s_zs[half], 1)

            def softplus(n, half):
                act.wait_ge(s_dp[half], n + 1)
                act.wait_ge(s_at, n + 1)
                src = (psT, psW)[half]
                a, z = 2 * half, 2 * half + 2
                for c in range(a, z):
                    last = nc.scalar.activation(xin[:, c, TAPS - 1:], src[:, c - a, 0:L], ACT.Identity,
                                                bias=b_dt[:, c:c + 1])
                last.then_inc(s_dx[half], 1)
                act.wait_ge(s_dx[half], n + 1)
                nc.scalar.activation(soft[:, a:z, :], xin[:, a:z, TAPS - 1:], ACT.Abs).then_inc(s_da[half], 1)
                act.wait_ge(s_da[half], n + 1)
                nc.scalar.activation(soft[:, a:z, :], soft[:, a:z, :], ACT.Exp, scale=-1.0).then_inc(s_de[half], 1)
                act.wait_ge(s_de[half], n + 1)
                nc.scalar.activation(soft[:, a:z, :], soft[:, a:z, :], ACT.Ln, bias=1.0).then_inc(s_dl[half], 1)

            def exp_logits(m):
                act.wait_ge(s_lg, m + 1)
                after(act, s_ch, m)
                nc.scalar.activation(denom[:, :, :], psW[:, 0, 0:NSEG * NE].rearrange("p (s e) -> p s e", s=NSEG),
                                     ACT.Exp, scale=-1.0).then_inc(s_lge, 1)

            act.preload_act_table_set("natural_log_exp_and_others")
            act.wait_ge(s_const, 1)
            copy_turned(0, s_qT, s_qTc)
            probs(0)
            copy_prob_t(0)
            act.wait_ge(s_w, 176)
            nc.scalar.activation(a_neg[:, :, :], a_neg[:, :, :], ACT.Exp).then_inc(s_a0, 1)
            act.wait_ge(s_a0, 1)
            nc.scalar.activation(a_neg[:, :, :], a_neg[:, :, :], ACT.Copy, scale=-1.0).then_inc(s_a0, 1)
            first_rstd(0, 0)
            copy_turned(0, s_xT, s_xTc)
            copy_xin(0, 0)
            copy_xin(0, 1)
            silus(0, 0)
            act.preload_act_table_set("natural_log_exp_and_others")
            copy_bc(0)
            softplus(0, 0)
            softplus(0, 1)
            copy_turned(1, s_qT, s_qTc)
            act.wait_ge(s_a0, 2)

            def body(b, q, before, routed, next, after_next):
                n, m, a, r = b + 1, b - 1, b + 2, 1 - q
                for k in range(UNITS):
                    decays(b, q, k // NG, k % NG)
                    if next:
                        if k == 0:
                            probs(n)
                        if k == 1:
                            copy_prob_t(n)
                        if k == 3:
                            first_rstd(n, 0)
                        if k == 5:
                            copy_turned(n, s_xT, s_xTc)
                        if k == 6:
                            copy_xin(n, 0)
                            copy_xin(n, 1)
                    if before and k == 6:
                        first_rstd(m, 1)
                    if next:
                        if k == 10:
                            silus(n, r)
                            act.preload_act_table_set("natural_log_exp_and_others")
                        if k == 11:
                            copy_bc(n)
                            softplus(n, 0)
                        if k == 12:
                            softplus(n, 1)
                    if before:
                        if k == 13:
                            copy_turned(m, s_x2T, s_x2Tc)
                        if k == 14:
                            exp_logits(m)
                    if after_next and k == 14:
                        copy_turned(a, s_qT, s_qTc)

            each(act, body)
            first_rstd(NB - 1, 1)
            copy_turned(NB - 1, s_x2T, s_x2Tc)
            exp_logits(NB - 1)

        @block.vector
        def _(dve):
            for j in range(2):
                nc.vector.memset(decay[j][:, :, 0:1], 0.0)
            nc.vector.memset(xin[:, :, 0:TAPS - 1], 0.0)
            nc.vector.memset(epsc[:, :], EPS)
            nc.vector.memset(xs[:, NSEG - 1, :], 0.0).then_inc(s_const, 1)

            def scan(b, c, g):
                dve.wait_ge(s_dec[g], 4 * b + c + 1)
                dve.wait_ge(s_dbu[g], 4 * b + c + 1)
                flat = hid[c % 2][g][:, :, :].rearrange("p n l -> p (n l)")
                nc.vector.tensor_tensor_scan(flat, decay[g % 2][:, :, :].rearrange("p n l -> p (n l)"), flat,
                                             0.0, ALU.mult, ALU.add).then_inc(s_h[g], 1)

            def times_c(b, c, g):
                if g in pool_groups(b):
                    return
                if c == 0:
                    dve.wait_ge(s_C[g], 16 * (b + 1))
                dve.wait_ge(s_h[g], 4 * b + c + 1)
                nc.vector.tensor_tensor(hid[c % 2][g][:, :, :], hid[c % 2][g][:, :, :],
                                        c_all[:, g * GN:(g + 1) * GN, :], ALU.mult).then_inc(s_hc[g], 1)

            def gate(b, q, c):
                dve.wait_ge(s_ys[3], 4 * b + c + 1)
                if c == 0:
                    dve.wait_ge(s_zs[1], b + 1)
                    after(dve, s_op, b)
                nc.vector.tensor_tensor(yz[:, c, :], psY[c % 2][:, 0:L], zs[q][:, c, :],
                                        ALU.mult).then_inc(s_yz, 1)

            def row_max(n):
                dve.wait_ge(s_S, n + 1)
                nc.vector.tensor_reduce(rmax[:, :], psW[:, 0, 0:L].rearrange("p (s k) -> p s k", s=NSEG),
                                        AX.X, ALU.max).then_inc(s_rm, 1)
                dve.wait_ge(s_rm, n + 1)
                nc.vector.tensor_scalar(nmax[:, :], rmax[:, :], -(D ** -0.5), None, ALU.mult).then_inc(s_nm, 1)

            def stats(n, j, src):
                for s in range(NSEG):
                    last = nc.vector.bn_stats(stat[j][:, s, :], src[:, s, :])
                last.then_inc(s_st[j], 1)
                dve.wait_ge(s_st[j], n + 1)
                dve.sem_inc(s_turn, 1)
                for s in range(NSEG):
                    last = nc.vector.bn_aggr(mv[j][:, s, :], stat[j][:, s, :])
                last.then_inc(s_mv[j], 1)

            def norm(n, j, src):
                v, y, t = mv[j][:, :, 1], rs0[j][:, :], nw[j]
                dve.wait_ge(s_r0[j], n + 1)
                nc.vector.scalar_tensor_tensor(out=t[:, 0, :], in0=v, scalar=EPS, in1=y,
                                               op0=ALU.add, op1=ALU.mult).then_inc(s_nw[j], 1)
                dve.wait_ge(s_nw[j], 3 * n + 1)
                nc.vector.tensor_tensor(t[:, 1, :], t[:, 0, :], y, ALU.mult).then_inc(s_nw[j], 1)
                dve.wait_ge(s_nw[j], 3 * n + 2)
                nc.vector.tensor_scalar(t[:, 2, :], t[:, 1, :], -0.5, 1.5, ALU.mult, ALU.add).then_inc(s_nw[j], 1)
                dve.wait_ge(s_nw[j], 3 * n + 3)
                nc.vector.tensor_tensor(rstd[j][:, :], t[:, 2, :], y, ALU.mult).then_inc(s_rs[j], 1)
                dve.wait_ge(s_rs[j], n + 1)
                if j == 0:
                    dve.wait_ge(s_xst, 16 * (n - 1) if not isinstance(n, int) else 16 * max(n - 1, 1))
                else:
                    dve.wait_ge(s_xT, last_seq(n + 2))
                    dve.wait_ge(s_xst, 16 * (n + 1))
                for s in range(NSEG):
                    last = nc.vector.tensor_scalar(normed[:, s, :], src[:, s, :], mv[j][:, s, 0:1],
                                                   rstd[j][:, s:s + 1], ALU.subtract, ALU.mult)
                last.then_inc(s_xn[j], 1)

            def attended(n):
                dve.wait_ge(s_E, n + 1)
                nc.vector.reciprocal(rinv[:, :], rsum[:, :]).then_inc(s_ri, 1)
                dve.wait_ge(s_at, n + 1)
                dve.wait_ge(s_ri, n + 1)
                after(dve, s_h1st, 16 * n)
                for s in range(NSEG):
                    last = nc.vector.tensor_scalar(h1[:, s, :], psXf[:, s * D:(s + 1) * D],
                                                   rinv[:, s:s + 1], None, ALU.mult)
                last.then_inc(s_h1, 1)
                dve.wait_ge(s_h1, n + 1)
                stats(n, 0, h1)

            def add_block(m):
                dve.wait_ge(s_op, m + 1)
                dve.wait_ge(s_hb, 16 * (m + 1))
                h = h2[:, :, :].rearrange("p s d -> p (s d)")
                nc.vector.tensor_tensor(h, psXf[:, 0:NSEG * D], h, ALU.add).then_inc(s_h2, 1)
                dve.wait_ge(s_h2, m + 1)
                stats(m, 1, h2)

            def conv(n, k):
                if k == 1:
                    dve.wait_ge(s_xc[0], n + 1)
                    dve.wait_ge(s_xc[1], n + 1)
                else:
                    dve.wait_ge(s_cv, (TAPS - 1) * n + k - 1)
                t = TAPS - 1 - k
                for c in range(CH):
                    last = nc.vector.scalar_tensor_tensor(out=u[:, c, :], in0=xin[:, c, t:t + L],
                                                          scalar=w_cv[:, c, t:t + 1], in1=u[:, c, :],
                                                          op0=ALU.mult, op1=ALU.add)
                last.then_inc(s_cv, 1)

            def finish_dt(n, q, half):
                a, z = 2 * half, 2 * half + 2
                dve.wait_ge(s_dl[half], n + 1)
                nc.vector.scalar_tensor_tensor(out=dt[q][:, a:z, :], in0=xin[:, a:z, TAPS - 1:], scalar=0.0,
                                               in1=soft[:, a:z, :], op0=ALU.max, op1=ALU.add).then_inc(s_dt[half], 1)

            def flat(t):
                return t[:, :, :].rearrange("p s e -> p (s e)")

            def counted(m):
                done = [0]

                def step(ins, carried=False):
                    done[0] += 1
                    ins.then_inc(s_rt, 1)
                    dve.wait_ge(s_rt, ROUTE_STEPS * m + done[0])
                    if carried:
                        dve.sem_inc(s_turn, 1)
                return step, done

            def route_groups(m):
                step, done = counted(m)
                dve.wait_ge(s_lge, m + 1)
                step(nc.vector.tensor_scalar(flat(denom), flat(denom), 1.0, None, ALU.add))
                step(nc.vector.reciprocal(flat(score), flat(denom)))
                step(nc.vector.tensor_tensor(biased[:, :, :], score[:, :, :],
                                             bias[:, :].unsqueeze(1).to_broadcast([P, NSEG, NE]), ALU.add))
                grp = biased[:, :, :].rearrange("p t (g h k) -> p (t g) h k", g=G, h=2)
                hi, lo = halves[:, 0, :, :], halves[:, 1, :, :]
                nc.vector.tensor_tensor(hi, grp[:, :, 0, :], grp[:, :, 1, :], ALU.max)
                step(nc.vector.tensor_tensor(lo, grp[:, :, 0, :], grp[:, :, 1, :], ALU.min))
                hi2, mn, mx, lo2 = (quarters[:, j, :, :] for j in range(4))
                nc.vector.tensor_tensor(hi2, hi[:, :, 0:2], hi[:, :, 2:4], ALU.max)
                nc.vector.tensor_tensor(mn, hi[:, :, 0:2], hi[:, :, 2:4], ALU.min)
                step(nc.vector.tensor_tensor(mx, lo[:, :, 0:2], lo[:, :, 2:4], ALU.max))
                step(nc.vector.tensor_tensor(lo2, mn, mx, ALU.max))
                v = [best[:, j, :] for j in range(4)]
                nc.vector.tensor_tensor(v[0], hi2[:, :, 0], hi2[:, :, 1], ALU.max)
                nc.vector.tensor_tensor(v[1], hi2[:, :, 0], hi2[:, :, 1], ALU.min)
                step(nc.vector.tensor_tensor(v[2], lo2[:, :, 0], lo2[:, :, 1], ALU.max))
                step(nc.vector.tensor_tensor(v[3], v[1], v[2], ALU.max))
                step(nc.vector.tensor_tensor(flat(gsum), v[0], v[3], ALU.add), carried=True)
                return step, done

            def route_experts(m, step, done):
                for s in range(NSEG):
                    last = nc.vector.max(gtop[:, s, :], gsum[:, s, :])
                step(last)
                step(nc.vector.memset(gtop[:, :, TOPG:G], ABSENT), carried=True)
                for s in range(NSEG):
                    last = nc.vector.match_replace(gleft[:, s, :], gtop[:, s, :], gsum[:, s, :], TAKEN)
                step(last)
                step(nc.vector.tensor_tensor(flat(gleft), flat(gleft), flat(gsum), ALU.is_equal))
                by_group = lambda t: t[:, :, :].rearrange("p s (g k) -> p (s g) k", g=G)
                step(nc.vector.scalar_tensor_tensor(
                    out=by_group(masked), in0=flat(gleft).unsqueeze(2).to_broadcast([P, NSEG * G, GE]), scalar=FAR,
                    in1=by_group(biased), op0=ALU.mult, op1=ALU.add), carried=True)
                for s in range(NSEG):
                    last = nc.vector.max(top8[:, s, :], masked[:, s, :])
                step(last, carried=True)
                assert done[0] == ROUTE_STEPS

            def weigh(m):
                for s in range(NSEG):
                    last = nc.vector.match_replace(left[:, s, :], top8[:, s, :], masked[:, s, :], TAKEN)
                last.then_inc(s_wg, 1)
                dve.wait_ge(s_wg, 5 * m + 1)
                dve.wait_ge(s_cst, 16 * (m + 1))
                nc.vector.tensor_tensor(flat(chosen), flat(left), flat(masked), ALU.not_equal).then_inc(s_ch, 1)
                dve.wait_ge(s_ch, m + 1)
                nc.vector.tensor_tensor(flat(score), flat(score), flat(chosen), ALU.mult).then_inc(s_wg, 1)
                dve.wait_ge(s_wg, 5 * m + 2)
                nc.vector.tensor_reduce(wsum[:, :], score[:, :, :], AX.X, ALU.add).then_inc(s_wg, 1)
                dve.wait_ge(s_wg, 5 * m + 3)
                nc.vector.tensor_scalar(wsum[:, :], wsum[:, :], 1e-20, None, ALU.add).then_inc(s_wg, 1)
                dve.wait_ge(s_wg, 5 * m + 4)
                nc.vector.reciprocal(winv[:, :], wsum[:, :]).then_inc(s_wg, 1)
                dve.wait_ge(s_wg, 5 * m + 5)
                dve.wait_ge(s_wst, 16 * (m + 1))
                nc.vector.scalar_tensor_tensor(
                    out=weight[:, :, :], in0=score[:, :, :], scalar=SCALE,
                    in1=winv[:, :].unsqueeze(2).to_broadcast([P, NSEG, NE]), op0=ALU.mult, op1=ALU.mult
                ).then_inc(s_wgt, 1)

            row_max(0)
            attended(0)
            norm(0, 0, h1)
            dve.wait_ge(s_w, 176)
            for k in range(1, TAPS):
                conv(0, k)
            finish_dt(0, 0, 0)
            finish_dt(0, 0, 1)
            row_max(1)

            def body(b, q, before, routed, next, after_next):
                n, m, a, r = b + 1, b - 1, b + 2, 1 - q
                for k in range(UNITS):
                    scan(b, k // NG, k % NG)
                    times_c(b, k // NG, k % NG)
                    if k in (5, 9, 13):
                        gate(b, q, k // NG - 1)
                    if before and k == 1:
                        gate(m, r, 3)
                    if next:
                        if k == 1:
                            attended(n)
                        if k == 3:
                            norm(n, 0, h1)
                    if before:
                        if k == 4:
                            add_block(m)
                        if k == 7:
                            norm(m, 1, h2)
                    if next:
                        for tap in range(1, TAPS):
                            if k == K_CONV[tap - 1]:
                                conv(n, tap)
                    if routed:
                        if k == K_ROUTE[0]:
                            steps = route_groups(b - 2)
                        if k == K_ROUTE[1]:
                            route_experts(b - 2, *steps)
                        if k == K_ROUTE[2]:
                            weigh(b - 2)
                    if next:
                        if k == K_DT[0]:
                            finish_dt(n, r, 0)
                        if k == K_DT[1]:
                            finish_dt(n, r, 1)
                    if after_next and k == K_MAX:
                        row_max(a)

            each(dve, body)
            gate(NB - 1, (NB - 1) % 2, 3)
            add_block(NB - 1)
            norm(NB - 1, 1, h2)
            for m in (NB - 2, NB - 1):
                steps = route_groups(m)
                route_experts(m, *steps)
                weigh(m)

        @block.tensor
        def _(pe):
            def turn_q(n):
                pe.wait_ge(s_x, 32 * (n + 1))
                for kd in range(KD):
                    for s in range(NSEG):
                        last = nc.tensor.transpose(psT[:, kd, s * P:(s + 1) * P],
                                                   xs[:, s, kd * P:(kd + 1) * P], ident[:, :])
                last.then_inc(s_qT, 1)

            def scores(n):
                pe.wait_ge(s_qTc, n + 1)
                for s in range(NSEG):
                    for kd in range(KD):
                        t = turned[:, kd, s * P:(s + 1) * P]
                        last = nc.tensor.matmul(psW[:, 0, s * P:(s + 1) * P], t, t, start=(kd == 0),
                                                stop=(kd == KD - 1))
                last.then_inc(s_S, 1)

            def turn_prob(n):
                pe.wait_ge(s_E, n + 1)
                for s in range(NSEG):
                    last = nc.tensor.transpose(psT[:, 0, s * P:(s + 1) * P], prob[:, s, :], ident[:, :])
                last.then_inc(s_ET, 1)

            def attend(n):
                pe.wait_ge(s_ETc, n + 1)
                after(pe, s_bcc, n)
                for s in range(NSEG):
                    last = nc.tensor.matmul(psXf[:, s * D:(s + 1) * D], prob_t[:, s, :], xs[:, s, :],
                                            start=True, stop=True)
                last.then_inc(s_at, 1)

            def turn_normed(n, j, done):
                pe.wait_ge(s_xn[j], n + 1)
                for kd in range(KD):
                    for s in range(NSEG):
                        last = nc.tensor.transpose(psT[:, kd, s * P:(s + 1) * P],
                                                   normed[:, s, kd * P:(kd + 1) * P], ident[:, :])
                last.then_inc(done, 1)

            def project(dst, lhs, cols, rhs, kk, done):
                for j, c in enumerate(cols):
                    for k in range(kk):
                        last = nc.tensor.matmul(dst[:, j, 0:L], lhs[:, k, c * P:(c + 1) * P], rhs[:, k, :],
                                                start=(k == 0), stop=(k == kk - 1))
                last.then_inc(done, 1)

            def project_xin(n):
                pe.wait_ge(s_xTc, n + 1)
                project(psW, w_in, (0, 1), turned, KD, s_xp[0])
                pe.wait_ge(s_h1, n + 1)
                after(pe, s_h2, n - 1)
                project(psX, w_in, (2, 3), turned, KD, s_xp[1])

            def project_z(n, half):
                if half == 0:
                    project(psT, w_in, (4, 5), turned, KD, s_zp[0])
                else:
                    pe.wait_ge(s_xc[0], n + 1)
                    project(psW, w_in, (6, 7), turned, KD, s_zp[1])

            def project_bc(n):
                pe.wait_ge(s_u, n + 1)
                pe.wait_ge(s_xc[1], n + 1)
                for k in range(CH):
                    last = nc.tensor.matmul(psX[0:2 * NS, 0, 0:L], w_bc[:, k, :], u[:, k, :],
                                            start=(k == 0), stop=(k == CH - 1))
                last.then_inc(s_bcp, 1)

            def project_dt(n, half):
                pe.wait_ge(s_zs[half], n + 1)
                project((psT, psW)[half], w_dt, (2 * half, 2 * half + 1), u, CH, s_dp[half])

            def project_out(m):
                pe.wait_ge(s_yz, CH * (m + 1))
                pe.wait_ge(s_h1, last_seq(m + 3))
                for s in range(NSEG):
                    for c in range(CH):
                        last = nc.tensor.matmul(psXf[:, s * D:(s + 1) * D], yz[:, c, s * P:(s + 1) * P],
                                                w_out[:, c, :], start=(c == 0), stop=(c == CH - 1))
                last.then_inc(s_op, 1)

            def route(m):
                pe.wait_ge(s_x2Tc, m + 1)
                pe.wait_ge(s_dx[1], last_seq(m + 3))
                for s in range(NSEG):
                    for kd in range(KD):
                        last = nc.tensor.matmul(psW[:, 0, s * NE:(s + 1) * NE], turned[:, kd, s * P:(s + 1) * P],
                                                w_gt[:, kd, :], start=(kd == 0), stop=(kd == KD - 1))
                last.then_inc(s_lg, 1)

            def sum_y(b, c, g):
                pe.wait_ge(s_hc[g], 4 * b + c + 1)
                if g == 0:
                    after(pe, s_yz, 4 * b + c - 1)
                for j in range(GN):
                    last = nc.tensor.matmul(psY[c % 2][:, 0:L], ident[:, :], hid[c % 2][g][:, j, :],
                                            start=(g == 0 and j == 0), stop=(g == NG - 1 and j == GN - 1))
                last.then_inc(s_ys[g], 1)

            pe.wait_ge(s_idn, 1)
            turn_q(0)
            scores(0)
            turn_prob(0)
            attend(0)
            turn_normed(0, 0, s_xT)
            pe.wait_ge(s_w, 176)
            project_xin(0)
            project_z(0, 0)
            project_z(0, 1)
            project_bc(0)
            project_dt(0, 0)
            project_dt(0, 1)
            pe.wait_ge(s_dx[0], 1)
            turn_q(1)
            pe.wait_ge(s_dx[1], 1)
            scores(1)
            turn_prob(1)
            attend(1)

            def body(b, q, before, routed, next, after_next):
                n, m, a = b + 1, b - 1, b + 2
                for k in range(UNITS):
                    sum_y(b, k // NG, k % NG)
                    if before and k == 1:
                        project_out(m)
                    if next:
                        if k == 2:
                            turn_normed(n, 0, s_xT)
                        if k == 3:
                            project_xin(n)
                        if k == 4:
                            project_z(n, 0)
                        if k == 5:
                            project_z(n, 1)
                        if k == 8:
                            project_bc(n)
                            project_dt(n, 0)
                        if k == 9:
                            project_dt(n, 1)
                    if before:
                        if k == 10:
                            pe.wait_ge(s_dx[0], last_seq(m + 3))
                            turn_normed(m, 1, s_x2T)
                        if k == 11:
                            route(m)
                    if after_next:
                        if k == 11:
                            if before:
                                pe.wait_ge(s_x2Tc, m + 1)
                            else:
                                pe.wait_ge(s_dx[0], n + 1)
                            turn_q(a)
                        if k == 12:
                            if before:
                                pe.wait_ge(s_lge, m + 1)
                            else:
                                pe.wait_ge(s_dx[1], n + 1)
                            scores(a)
                        if k == 14:
                            turn_prob(a)
                        if k == 15:
                            attend(a)

            each(pe, body)
            project_out(NB - 1)
            turn_normed(NB - 1, 1, s_x2T)
            route(NB - 1)


def count_phase(nc, ch_tab, diff, total, NT):
    R = NT + 1
    UB = 4
    NJ = NE // UB
    assert R <= P
    with ExitStack() as ctx:
        def sb(name, shape, dt=F32):
            return ctx.enter_context(nc.sbuf_tensor(name, shape, dt))

        def sem(name):
            return ctx.enter_context(nc.semaphore(name))

        chosen = sb("n_chosen", [P, NT + 2, NE], BF16)
        tri = sb("n_tri", [P, 2, P + 1], BF16)
        psU = [ctx.enter_context(nc.psum_tensor(f"n_psU{j}", [P, 2, 512], F32)) for j in range(2)]
        psT = ctx.enter_context(nc.psum_tensor("n_psT", [P, 512], F32))

        s_ld, s_pad = sem("n_chosen_loaded"), sem("n_padded")
        s_t0, s_t1, s_t2 = sem("n_tri_ones"), sem("n_tri_cut"), sem("n_tri_ready")
        s_one = sem("n_ones_set")
        s_u = sem("n_diff_product")
        s_uc = [sem(f"n_diff_copied{q}") for q in range(2)]
        s_tp, s_tot = sem("n_total_product"), sem("n_total_ready")
        block = ctx.enter_context(nc.Block())

        def diff_of(j):
            return diff[0:R, bass.ds(j * UB, UB), 0:P + 1].rearrange("p (a b) c -> p a b c", b=2)

        def product(q):
            return psU[q][0:R, :, 0:2 * (P + 1)].rearrange("p a (b c) -> p a b c", b=2)

        @block.sync
        def _(sp):
            sp.dma_start(chosen[:, 1:NT + 1, :].rearrange("p (b s) e -> p b (s e)", s=NSEG),
                         ch_tab.rearrange("b p s e -> p b (s e)")).then_inc(s_ld, 16)

        @block.gpsimd
        def _(pool):
            nc.gpsimd.memset(tri[:, 0, 0:P], 1.0).then_inc(s_t0, 1)
            pool.wait_ge(s_t0, 1)
            nc.gpsimd.affine_select(out=tri[:, 0, 0:P], in_=tri[:, 0, 0:P], compare_op=ALU.is_ge, fill=0.0,
                                    base=0, pattern=[[1, P]], channel_multiplier=-1).then_inc(s_t1, 1)

        @block.tensor
        def _(pe):
            pe.wait_ge(s_t2, 2)
            pe.wait_ge(s_pad, 1)
            pe.wait_ge(s_ld, 16)

            def differences(i, j, q):
                after(pe, s_uc[q], i)
                for k in range(UB):
                    for d in range(2):
                        last = nc.tensor.matmul(
                            psU[q][0:R, k // 2, (k % 2) * (P + 1):(k % 2 + 1) * (P + 1)],
                            chosen[:, 1 - d:1 - d + R, bass.ds(j * UB + k, 1)].rearrange("p t o -> p (t o)"),
                            tri[:, d, :], start=(d == 0), stop=(d == 1))
                last.then_inc(s_u, 1)

            for q in range(2):
                differences(0, q, q)
            with pe.Fori(1, NJ // 2) as i:
                for q in range(2):
                    differences(i, 2 * i + q, q)
            for q in range(2):
                pe.wait_ge(s_uc[q], NJ // 2)
            nc.tensor.matmul(psT[0:R, 0:NE], tri[0:R, 0, 0:R], diff[0:R, :, P], start=True,
                             stop=True).then_inc(s_tp, 1)

        @block.scalar
        def _(act):
            with act.Fori(0, NJ // 2) as i:
                act.wait_ge(s_u, 2 * i + 1)
                nc.scalar.activation(diff_of(2 * i), product(0), ACT.Copy).then_inc(s_uc[0], 1)

        @block.vector
        def _(dve):
            nc.vector.memset(chosen[:, 0, :], 0.0)
            nc.vector.memset(chosen[:, NT + 1, :], 0.0).then_inc(s_pad, 1)
            nc.vector.memset(tri[:, 0, P:P + 1], 0.0)
            nc.vector.memset(tri[:, 1, P:P + 1], 1.0).then_inc(s_t2, 1)
            dve.wait_ge(s_t1, 1)
            nc.vector.tensor_scalar(tri[:, 1, 0:P], tri[:, 0, 0:P], -1.0, None, ALU.mult).then_inc(s_t2, 1)
            nc.vector.memset(diff[0:R, :, P + 1:P + 2], 1.0).then_inc(s_one, 1)
            dve.wait_ge(s_one, 1)
            nc.vector.memset(diff[0:1, :, P + 1:P + 2], 0.0).then_inc(s_one, 1)
            with dve.Fori(0, NJ // 2) as i:
                dve.wait_ge(s_u, 2 * i + 2)
                nc.vector.tensor_copy(diff_of(2 * i + 1), product(1)).then_inc(s_uc[1], 1)
            dve.wait_ge(s_tp, 1)
            nc.vector.tensor_copy(total[0:R, :], psT[0:R, 0:NE]).then_inc(s_tot, 1)
            dve.wait_ge(s_one, 2)
            dve.wait_ge(s_tot, 1)


def expert_phase(nc, w, x_tab, diff, total, h_out, NT):
    NTOK = NT * P
    CAP = SLOTS
    NH = CAP // P
    XW = D + NE
    EB = 8
    AHEAD = 4
    STAGED = 6
    NR = NE // EB
    LOCATED = 2
    FIN = 5
    R = NT + 1
    UW = P + 2
    W = EB * NH
    I = w["gate"].shape[2]
    assert I == P
    with ExitStack() as ctx:
        def sb(name, shape, dt=F32):
            return ctx.enter_context(nc.sbuf_tensor(name, shape, dt))

        def sem(name):
            return ctx.enter_context(nc.semaphore(name))

        ident = sb("e_ident", [P, P])
        zero = sb("e_zero", [P, NH, D])
        src_st = [sb(f"e_src_st{q}", [P, NH], U32) for q in range(EB)]
        dst_st = [sb(f"e_dst_st{q}", [P, NH], U32) for q in range(EB)]
        xg = [sb(f"e_xg{q}", [P, NH, XW]) for q in range(EB)]
        xt = [sb(f"e_xt{q}", [P, KD, CAP]) for q in range(2)]
        wg = [sb(f"e_wg{q}", [P, KD, I]) for q in range(EB)]
        wu = [sb(f"e_wu{q}", [P, KD, I]) for q in range(EB)]
        wd = [sb(f"e_wd{q}", [P, D]) for q in range(EB)]
        sg = [sb(f"e_sg{q}", [P, CAP]) for q in range(2)]
        at = [sb(f"e_at{q}", [P, CAP]) for q in range(2)]
        wcol = [sb(f"e_wcol{q}", [P, NH]) for q in range(2)]
        ys = [sb(f"e_ys{q}", [P, NH, D]) for q in range(4)]
        src = sb("e_src", [P, NE * NH], U32)
        dst = sb("e_dst", [P, NE * NH], U32)
        slot_row = sb("e_slot_row", [P, CAP])
        slot_row_i = sb("e_slot_row_i", [P, CAP], I32)
        slot_i = sb("e_slot_i", [P, NH], I32)
        slot = sb("e_slot", [P, NH])
        slot_half = sb("e_slot_half", [P, NH])
        passed = [sb(f"e_passed{p}", [P, CAP], BF16) for p in range(2)]
        in_tile = [sb(f"e_in_tile{p}", [P, NH]) for p in range(2)]
        side = [[sb(f"e_side{p}{h}", [P, P]) for h in range(NH)] for p in range(2)]
        tile_of = sb("e_tile_of", [P, NE * NH])
        place = sb("e_place", [P, NE * NH])
        half = sb("e_half", [P, W])
        tok = sb("e_tok", [P, W])
        far = sb("e_far", [P, W])
        over = sb("e_over", [P, W])
        psL = [ctx.enter_context(nc.psum_tensor(f"e_psL{p}", [P, 512], F32)) for p in range(2)]
        psG = [ctx.enter_context(nc.psum_tensor(f"e_psG{j}", [P, KD, CAP], F32)) for j in range(2)]
        psU = [ctx.enter_context(nc.psum_tensor(f"e_psU{j}", [P, 2, CAP], F32)) for j in range(2)]
        psO = [ctx.enter_context(nc.psum_tensor(f"e_psO{j}", [P, NH, D], F32)) for j in range(2)]

        s_c0, s_c = sem("e_ident_cleared"), sem("e_ident_set")
        s_z, s_zst = sem("e_zeros_set"), sem("e_spare_rows_zeroed")
        s_wt = [sem(f"e_weights_loaded{q}") for q in range(EB)]
        s_st = sem("e_indices_staged")
        s_xg = [sem(f"e_x_gathered{q}") for q in range(EB)]
        s_xT, s_xTc = sem("e_x_turned"), sem("e_x_turned_copied")
        s_gu, s_sg, s_at = sem("e_gate_up"), sem("e_silu"), sem("e_act_ready")
        s_yo, s_wc, s_ys = sem("e_down"), sem("e_wcol_ready"), sem("e_scaled")
        s_sc = sem("e_scattered")
        s_turn = sem("e_wait_carrier")
        s_io, s_slot = sem("e_iotas"), sem("e_slots_ready")
        s_ps, s_g, s_in = sem("e_passed_ready"), sem("e_counts_gathered"), sem("e_in_tile_ready")
        s_pl, s_fin = sem("e_place_ready"), sem("e_rows_step")
        block = ctx.enter_context(nc.Block())

        def each(eng, body):
            for q in range(EB):
                body(0, q, q)
            with eng.Fori(1, NR - LOCATED) as i:
                for q in range(EB):
                    body(i, EB * i + q, q)
            for i in range(NR - LOCATED, NR):
                for q in range(EB):
                    body(i, EB * i + q, q)

        def exists(e):
            return not isinstance(e, int) or e < NE

        def to_locate(e, q):
            return e + LOCATED * EB, q % 2

        @block.sync
        def _(sp):
            sp.wait_ge(s_z, 1)
            sp.dma_start(h_out[NTOK:NTOK + CAP, :].rearrange("(h p) d -> p h d", p=P), zero[:, :, :]).then_inc(s_zst, 16)

            def load(e, q):
                sp.dma_start(wg[q][:, :, :], w["gate"][e].rearrange("(k p) i -> p k i", p=P)).then_inc(s_wt[q], 16)
                sp.dma_start(wu[q][:, :, :], w["up"][e].rearrange("(k p) i -> p k i", p=P)).then_inc(s_wt[q], 16)
                sp.dma_start(wd[q][:, :], w["down"][e]).then_inc(s_wt[q], 16)

            for q in range(EB):
                load(q, q)
            with sp.Fori(1, NE // EB) as i:
                for q in range(EB):
                    sp.wait_ge(s_yo, EB * i + q - EB + 1)
                    sp.sem_inc(s_turn, 1)
                    load(EB * i + q, q)
            sp.wait_ge(s_zst, 16)

        @block.gpsimd
        def _(pool):
            nc.gpsimd.memset(ident[:, :], 0.0).then_inc(s_c0, 1)
            pool.wait_ge(s_c0, 1)
            nc.gpsimd.affine_select(out=ident[:, :], in_=ident[:, :], compare_op=ALU.not_equal, fill=1.0,
                                    base=0, pattern=[[-1, P]], channel_multiplier=1).then_inc(s_c, 1)
            nc.gpsimd.iota(slot_row_i[:, :], pattern=[[1, CAP]], base=0, channel_multiplier=0).then_inc(s_io, 1)
            nc.gpsimd.iota(slot_i[:, :], pattern=[[P, NH]], base=0, channel_multiplier=1).then_inc(s_io, 1)

            def gather(e, q):
                pool.wait_ge(s_st, e + 1)
                pool.sem_inc(s_turn, 1)
                for h in range(NH):
                    nc.gpsimd.indirect_dma_start(
                        out=xg[q][:, h, :], out_offset=None, in_=x_tab,
                        in_offset=bass.IndirectOffsetOnAxis(ap=src_st[q][:, h:h + 1], axis=0)).then_inc(s_xg[q], 16)

            def scatter(e, q):
                pool.wait_ge(s_ys, e + 1)
                after(pool, s_sc, 16 * NH * e)
                pool.sem_inc(s_turn, 1)
                for h in range(NH):
                    nc.gpsimd.indirect_dma_start(
                        out=h_out, out_offset=bass.IndirectOffsetOnAxis(ap=dst_st[q][:, h:h + 1], axis=0),
                        in_=ys[q % 4][:, h, :], in_offset=None, compute_op=ALU.add).then_inc(s_sc, 16)

            for e in range(AHEAD):
                gather(e, e)
            pool.wait_ge(s_zst, 16)

            def expert(i, e, q):
                if exists(e + AHEAD):
                    gather(e + AHEAD, (q + AHEAD) % EB)
                scatter(e, q)

            each(pool, expert)
            pool.wait_ge(s_sc, 16 * NH * NE)

        @block.scalar
        def _(act):
            def silu(e, q):
                r = q % 2
                act.wait_ge(s_gu, e + 1)
                nc.scalar.activation(sg[r][:, :], psU[r][:, 0, :], ACT.Silu).then_inc(s_sg, 1)

            def count(e, p):
                act.wait_ge(s_in, e + 1)
                for h in range(NH):
                    last = nc.scalar.activation(side[p][h][:, :], psL[p][:, h * UW:h * UW + P], ACT.Sign, scale=-1.0,
                                                bias=in_tile[p][:, h:h + 1],
                                                accum_out=place[:, bass.ds(NH * e + h, 1)])
                last.then_inc(s_pl, 1)

            def expert(i, e, q):
                if exists(e + 1):
                    silu(e + 1, (q + 1) % EB)
                if exists(to_locate(e, q)[0]):
                    count(*to_locate(e, q))

            for e in range(LOCATED * EB):
                count(e, e % 2)
            silu(0, 0)
            each(act, expert)

        @block.tensor
        def _(pe):
            pe.wait_ge(s_c, 1)

            def turn(i, e, q):
                r = q % 2
                pe.wait_ge(s_xg[q], 16 * NH * (i + 1))
                after(pe, s_xTc, e - 1)
                for h in range(NH):
                    for k in range(KD):
                        last = nc.tensor.transpose(psG[r][:, k, h * P:(h + 1) * P], xg[q][:, h, k * P:(k + 1) * P],
                                                   ident[:, :])
                last.then_inc(s_xT, 1)

            def up(i, e, q):
                r = q % 2
                pe.wait_ge(s_wt[q], 48 * (i + 1))
                pe.wait_ge(s_xTc, e + 1)
                after(pe, s_at, e - 1)
                for j, m in enumerate((wg, wu)):
                    for k in range(KD):
                        last = nc.tensor.matmul(psU[r][:, j, :], m[q][:, k, :], xt[r][:, k, :],
                                                start=(k == 0), stop=(k == KD - 1))
                last.then_inc(s_gu, 1)

            def down(i, e, q):
                r = q % 2
                pe.wait_ge(s_at, e + 1)
                after(pe, s_ys, e - 1)
                for h in range(NH):
                    last = nc.tensor.matmul(psO[r][:, h, :], at[r][:, h * P:(h + 1) * P], wd[q][:, :],
                                            start=True, stop=True)
                last.then_inc(s_yo, 1)

            def expert(i, e, q):
                if exists(e + 1):
                    up(i + (q + 1) // EB, e + 1, (q + 1) % EB)
                if exists(e + 2):
                    turn(i + (q + 2) // EB, e + 2, (q + 2) % EB)
                if exists(to_locate(e, q)[0]):
                    gather_counts(*to_locate(e, q))
                down(i, e, q)

            def gather_counts(e, p):
                pe.wait_ge(s_ps, e + 1)
                after(pe, s_pl, e - 1)
                for h in range(NH):
                    last = nc.tensor.matmul(psL[p][:, h * UW:(h + 1) * UW], passed[p][0:R, h * P:(h + 1) * P],
                                            diff[0:R, bass.ds(e, 1), :].rearrange("p o c -> p (o c)"),
                                            start=True, stop=True)
                last.then_inc(s_g, 1)

            for e in range(LOCATED * EB):
                gather_counts(e, e % 2)
            turn(0, 0, 0)
            up(0, 0, 0)
            turn(0, 1, 1)
            each(pe, expert)

        @block.vector
        def _(dve):
            def stage(e, q):
                nc.vector.tensor_copy(src_st[q][:, :], src[:, bass.ds(e * NH, NH)])
                nc.vector.tensor_copy(dst_st[q][:, :], dst[:, bass.ds(e * NH, NH)]).then_inc(s_st, 1)

            def copy_turned(e, q):
                r = q % 2
                dve.wait_ge(s_xT, e + 1)
                after(dve, s_gu, e - 1)
                nc.vector.tensor_copy(xt[r][:, :, :], psG[r][:, :, :]).then_inc(s_xTc, 1)

            def expert(i, e, q):
                r = q % 2
                dve.wait_ge(s_sg, e + 1)
                nc.vector.tensor_tensor(at[r][:, :], sg[r][:, :], psU[r][:, 1, :], ALU.mult).then_inc(s_at, 1)
                nc.vector.tensor_copy(wcol[r][:, :], xg[q][:, :, bass.ds(D + e, 1)].rearrange("p h o -> p (h o)")
                                      ).then_inc(s_wc, 1)
                if exists(to_locate(e, q)[0]):
                    pass_tiles(*to_locate(e, q))
                if exists(e + 2):
                    copy_turned(e + 2, (q + 2) % EB)
                dve.wait_ge(s_yo, e + 1)
                dve.wait_ge(s_wc, e + 1)
                after(dve, s_sc, 16 * NH * (e - 3))
                for h in range(NH):
                    last = nc.vector.tensor_scalar(ys[q % 4][:, h, :], psO[r][:, h, :], wcol[r][:, h:h + 1], None,
                                                   ALU.mult)
                last.then_inc(s_ys, 1)
                if q == 1 and (not isinstance(i, int) or 0 < i < NR - 1):
                    find_rows(i + 1)
                if exists(e + STAGED):
                    after(dve, s_sc, 16 * NH * (e + STAGED - EB + 1))
                    stage(e + STAGED, (q + STAGED) % EB)
                if exists(to_locate(e, q)[0]):
                    enter_tiles(*to_locate(e, q))

            def pass_tiles(e, p):
                nc.vector.tensor_scalar(passed[p][0:R, :], slot_row[0:R, :], total[0:R, bass.ds(e, 1)], None,
                                        ALU.is_ge).then_inc(s_ps, 1)

            def enter_tiles(e, p):
                dve.wait_ge(s_g, e + 1)
                after(dve, s_pl, e - 1)
                got = psL[p][:, 0:NH * UW].rearrange("p (h c) -> p h c", h=NH)
                nc.vector.tensor_copy(tile_of[:, bass.ds(NH * e, NH)], got[:, :, P + 1])
                nc.vector.tensor_tensor(in_tile[p][:, :], slot_half[:, :], got[:, :, P],
                                        ALU.subtract).then_inc(s_in, 1)

            def find_rows(r):
                done = [0]

                def step(ins):
                    done[0] += 1
                    ins.then_inc(s_fin, 1)
                    dve.wait_ge(s_fin, FIN * r + done[0])

                dve.wait_ge(s_pl, EB * (r + 1))
                part = lambda t: t[:, bass.ds(r * W, W)]
                by_expert = lambda t: t.rearrange("p (e h) -> p e h", h=NH)
                step(nc.vector.tensor_scalar(half[:, :], part(place), 0.5, P / 2, ALU.mult, ALU.add))
                nc.vector.tensor_scalar(over[:, :], part(tile_of), float(NT), None, ALU.is_ge)
                step(nc.vector.scalar_tensor_tensor(out=tok[:, :], in0=part(tile_of), scalar=float(P),
                                                    in1=half[:, :], op0=ALU.mult, op1=ALU.add))
                nc.vector.tensor_scalar(part(src), tok[:, :], float(NTOK - 1), None, ALU.min)
                step(nc.vector.scalar_tensor_tensor(
                    out=by_expert(far[:, :]), in0=slot[:, :].unsqueeze(1).to_broadcast([P, EB, NH]),
                    scalar=float(NTOK), in1=by_expert(tok[:, :]), op0=ALU.add, op1=ALU.subtract))
                step(nc.vector.tensor_tensor(far[:, :], far[:, :], over[:, :], ALU.mult))
                step(nc.vector.tensor_tensor(part(dst), far[:, :], tok[:, :], ALU.add))
                assert done[0] == FIN

            nc.vector.memset(zero[:, :, :], 0.0).then_inc(s_z, 1)
            dve.wait_ge(s_io, 2)
            nc.vector.tensor_copy(slot[:, :], slot_i[:, :])
            nc.vector.tensor_scalar(slot_half[:, :], slot_i[:, :], 0.5, None, ALU.add)
            nc.vector.tensor_copy(slot_row[:, :], slot_row_i[:, :]).then_inc(s_slot, 1)
            dve.wait_ge(s_slot, 1)
            pass_tiles(0, 0)
            for e in range(LOCATED * EB):
                if e + 1 < LOCATED * EB:
                    pass_tiles(e + 1, (e + 1) % 2)
                enter_tiles(e, e % 2)
                if e % EB == EB - 1:
                    find_rows(e // EB)
                if e == EB - 1:
                    for j in range(STAGED):
                        stage(j, j)
            copy_turned(0, 0)
            copy_turned(1, 1)
            each(dve, expert)


def audio_tower_kernel(nc, x, w, out):
    NT = x.shape[0] * NSEG
    bc_dram = nc.dram_tensor("bc_rows_dram", (2, 2 * NS, L), F32, kind="Internal").ap()
    ch_tab = nc.dram_tensor("chosen_dram", (x.shape[0], P, NSEG, NE), BF16, kind="Internal").ap()
    x_tab = nc.dram_tensor("x2_weights_dram", (NT * P, D + NE), F32, kind="Internal").ap()
    sequence_phase(nc, x, w, bc_dram, out, x_tab, ch_tab)
    with ExitStack() as ctx:
        diff = ctx.enter_context(nc.sbuf_tensor("count_differences", [P, NE, P + 2], BF16))
        total = ctx.enter_context(nc.sbuf_tensor("tokens_before_tile", [P, NE], F32))
        count_phase(nc, ch_tab, diff, total, NT)
        expert_phase(nc, w, x_tab, diff, total, out, NT)


def kernel(**inputs):
    import numpy as np
    import concourse.bacc as bacc
    from concourse.bass_utils import run_bass_kernel_spmd

    def as_is(name):
        return np.ascontiguousarray(inputs[name])

    def turned(name):
        return np.ascontiguousarray(np.asarray(inputs[name]).T)

    def by_chunk(name):
        return np.ascontiguousarray(np.asarray(inputs[name]).reshape(CH, P).T)

    host = {
        "x": as_is("x"),
        "in_t": turned("L0_attn_W_in"),
        "conv": as_is("L0_attn_W_conv").reshape(DI, TAPS),
        "b_conv": by_chunk("L0_attn_b_conv"),
        "dt_t": turned("L0_attn_W_dt"),
        "b_dt": by_chunk("L0_attn_b_dt"),
        "b_t": turned("L0_attn_W_B"),
        "c_t": turned("L0_attn_W_C"),
        "a_log": as_is("L0_attn_A_log"),
        "out_t": turned("L0_attn_W_out"),
        "gate_t": turned("L0_ffn_gate_w"),
        "gate_bias": as_is("L0_ffn_gate_bias"),
        "gate": as_is("L0_ffn_w_gate"),
        "up": as_is("L0_ffn_w_up"),
        "down": as_is("L0_ffn_w_down"),
    }
    nc = bacc.Bacc("TRN2", target_bir_lowering=False, num_devices=1)
    w = {k: nc.dram_tensor(f"in_{k}_dram", v.shape, F32, kind="ExternalInput").ap() for k, v in host.items()}
    NB = host["x"].shape[0]
    out = nc.dram_tensor("out_dram", (NB * L + SLOTS, D), F32, kind="ExternalOutput").ap()
    audio_tower_kernel(nc, w["x"], w, out)
    r = run_bass_kernel_spmd(nc, [{f"in_{k}_dram": v for k, v in host.items()}], core_ids=[0])
    return r.results[0]["out_dram"][:NB * L].reshape(NB, L, D)
```
